# Optimizing a Trainium2 kernel written in Bass

```python
import numpy as np
import jax
import jax.numpy as jnp

def _softmax(x, axis=-1):
    return jax.nn.softmax(x, axis=axis)

def _gelu(x):
    return jax.nn.gelu(x, approximate=True)

def _silu(x):
    return jax.nn.silu(x)

def _sigmoid(x):
    return jax.nn.sigmoid(x)

def _layernorm(x, axis=-1, eps=1e-05):
    m = jnp.mean(x, axis=axis, keepdims=True)
    v = jnp.var(x, axis=axis, keepdims=True)
    return (x - m) / jnp.sqrt(v + eps)

def _scatter_add(tgt, idx, src, axis=0):
    return tgt.at[idx].add(src)

def _segment_sum(src, seg, n):
    return jax.ops.segment_sum(src, seg, n)
kernel_name = 'mk_adaln_d1_jaxref_r4_31f03b'

def setup_inputs(seed: int=0):
    np.random.seed(seed)
    _w = jnp.asarray

    def _L0_attn_setup():
        import jax, jax.numpy as jnp
        import numpy as np
        B, S, D = (8, 2048, 256)
        MIN_RAD, MAX_RAD = (0.9, 0.999)

        def _a_param_init(key, d):
            unif = jax.random.uniform(key, (d,))
            a = 0.5 * jnp.log(unif * (MAX_RAD ** 2 - MIN_RAD ** 2) + MIN_RAD ** 2)
            return jnp.log(jnp.exp(-a) - 1.0)
        key = jax.random.key(seed)
        ks = jax.random.split(key, 6)
        s = 1.0 / np.sqrt(D)
        return {'x': jax.random.normal(ks[0], (B, S, D), jnp.float32), 'W_in': jax.random.normal(ks[1], (D, D), jnp.float32) * s, 'b_in': jnp.zeros((D,), jnp.float32), 'W_gx': jax.random.normal(ks[2], (D, D), jnp.float32) * s, 'b_gx': jnp.zeros((D,), jnp.float32), 'W_ga': jax.random.normal(ks[3], (D, D), jnp.float32) * s, 'b_ga': jnp.zeros((D,), jnp.float32), 'a_param': _a_param_init(ks[4], D), 'W_out': jax.random.normal(ks[5], (D, D), jnp.float32) * s, 'b_out': jnp.zeros((D,), jnp.float32)}
    _L0_attn_in = _L0_attn_setup()

    def _L0_ffn_setup():
        import jax, jax.numpy as jnp
        import numpy as np
        N, T, D = (4, 1024, 256)
        NUM_EXPERTS = 8
        EXPERT_CAP = 2.0
        MLP_RATIO = 4
        HIDDEN = MLP_RATIO * D
        key = jax.random.key(seed)
        k1, k2, k3, k4 = jax.random.split(key, 4)
        x = jax.random.normal(k1, (N, T, D), dtype=jnp.float32)
        gate_w = jax.random.truncated_normal(k2, -2.0, 2.0, (D, NUM_EXPERTS), dtype=jnp.float32) * 0.02
        w1 = jax.random.normal(k3, (NUM_EXPERTS, D, HIDDEN), dtype=jnp.float32) * 0.02
        w2 = jax.random.normal(k4, (NUM_EXPERTS, HIDDEN, D), dtype=jnp.float32) * 0.02
        return {'x': x, 'gate_w': gate_w, 'w1': w1, 'w2': w2}
    _L0_ffn_in = _L0_ffn_setup()
    _L0_c = _w((lambda *s: np.random.randn(*s).astype(np.float32) * 0.05)(4, 256))
    _L0_wmod = _w((lambda *s: np.random.randn(*s).astype(np.float32) * 0.05)(256, 6 * 256) * 256 ** (-0.5))
    _d = {'L0_attn_x': _L0_attn_in['x'], 'L0_attn_W_in': _L0_attn_in['W_in'], 'L0_attn_b_in': _L0_attn_in['b_in'], 'L0_attn_W_gx': _L0_attn_in['W_gx'], 'L0_attn_b_gx': _L0_attn_in['b_gx'], 'L0_attn_W_ga': _L0_attn_in['W_ga'], 'L0_attn_b_ga': _L0_attn_in['b_ga'], 'L0_attn_a_param': _L0_attn_in['a_param'], 'L0_attn_W_out': _L0_attn_in['W_out'], 'L0_attn_b_out': _L0_attn_in['b_out'], 'L0_ffn_gate_w': _L0_ffn_in['gate_w'], 'L0_ffn_w1': _L0_ffn_in['w1'], 'L0_ffn_w2': _L0_ffn_in['w2'], 'L0_c': _L0_c, 'L0_wmod': _L0_wmod}
    _x0 = _d['L0_attn_x']
    _d['L0_attn_x'] = jax.random.normal(jax.random.fold_in(jax.random.key(seed), 1), (4, 2048, 256), dtype=_x0.dtype)
    del _x0
    return _d

def reference(L0_attn_x, L0_attn_W_in, L0_attn_b_in, L0_attn_W_gx, L0_attn_b_gx, L0_attn_W_ga, L0_attn_b_ga, L0_attn_a_param, L0_attn_W_out, L0_attn_b_out, L0_ffn_gate_w, L0_ffn_w1, L0_ffn_w2, L0_c, L0_wmod):

    def _L0_attn_ref(x, W_in, b_in, W_gx, b_gx, W_ga, b_ga, a_param, W_out, b_out):
        import jax, jax.numpy as jnp
        import numpy as np
        B, S, D = (8, 2048, 256)
        MIN_RAD, MAX_RAD = (0.9, 0.999)

        def _a_param_init(key, d):
            unif = jax.random.uniform(key, (d,))
            a = 0.5 * jnp.log(unif * (MAX_RAD ** 2 - MIN_RAD ** 2) + MIN_RAD ** 2)
            return jnp.log(jnp.exp(-a) - 1.0)
        x = x @ W_in + b_in
        gate_x = jax.nn.sigmoid(x @ W_gx + b_gx)
        gate_a = jax.nn.sigmoid(x @ W_ga + b_ga)
        log_a = -8.0 * gate_a * jax.nn.softplus(a_param)
        a = jnp.exp(log_a)
        scale = jnp.sqrt(1.0 - jnp.exp(2.0 * log_a))
        xg = gate_x * x

        def step(h, inp):
            xt, at, st = inp
            h = at * h + st * xt
            return (h, h)
        init = jnp.zeros((x.shape[0], x.shape[2]), x.dtype)
        xs = (jnp.swapaxes(xg, 0, 1), jnp.swapaxes(a, 0, 1), jnp.swapaxes(scale, 0, 1))
        _, h = jax.lax.scan(step, init, xs, reverse=False)
        h = jnp.swapaxes(h, 0, 1)
        return h @ W_out + b_out

    def _L0_ffn_ref(x, gate_w, w1, w2):
        import jax, jax.numpy as jnp
        import numpy as np
        N, T, D = (4, 1024, 256)
        NUM_EXPERTS = 8
        EXPERT_CAP = 2.0
        MLP_RATIO = 4
        HIDDEN = MLP_RATIO * D
        x = x.astype(jnp.float32)
        n, t, d = x.shape
        k = int(EXPERT_CAP * t / NUM_EXPERTS)
        scores = jnp.einsum('ntd,de->nte', x, gate_w)
        probs = jax.nn.softmax(scores, axis=-1)
        probs = jnp.transpose(probs, (0, 2, 1))
        g, m = jax.lax.top_k(probs, k)
        xin = jax.vmap(lambda xb, mb: xb[mb])(x, m)
        h = jax.nn.gelu(jnp.einsum('nekd,edf->nekf', xin, w1))
        h = jnp.einsum('nekf,efd->nekd', h, w2)
        weighted = g[..., None] * h
        flat_idx = (m + jnp.arange(n, dtype=m.dtype)[:, None, None] * t).reshape(-1)
        out = jnp.zeros((n * t, d), dtype=jnp.float32).at[flat_idx].add(weighted.reshape(-1, d))
        out = out.reshape(n, t, d)
        return out.astype(jnp.bfloat16)
    x = L0_attn_x
    mod = (_silu(L0_c) @ L0_wmod).reshape(L0_c.shape[0], 6, 1, -1)
    sa, ca, ga, sb, cb, gb = (mod[:, 0], mod[:, 1], mod[:, 2], mod[:, 3], mod[:, 4], mod[:, 5])
    ga = (2 * (ga >= 0) - 1) * jnp.maximum(jnp.abs(ga), 0.25)
    gb = (2 * (gb >= 0) - 1) * jnp.maximum(jnp.abs(gb), 0.25)
    h = _layernorm(x, axis=-1) * (1 + ca) + sa
    x = x + ga * _L0_attn_ref(h, L0_attn_W_in, L0_attn_b_in, L0_attn_W_gx, L0_attn_b_gx, L0_attn_W_ga, L0_attn_b_ga, L0_attn_a_param, L0_attn_W_out, L0_attn_b_out)
    h = _layernorm(x, axis=-1) * (1 + cb) + sb
    x = x + gb * _L0_ffn_ref(h, L0_ffn_gate_w, L0_ffn_w1, L0_ffn_w2)
    return x

_drawn_inputs = setup_inputs


def setup_inputs(seed=0):
    import zlib

    import numpy as np

    out = dict(_drawn_inputs(seed))
    spreads = {'L0_attn_b_in': (0.0, 0.1),
     'L0_attn_b_gx': (0.0, 0.8),
     'L0_attn_b_ga': (0.0, 0.8),
     'L0_attn_b_out': (0.0, 0.342)}
    factors = {'L0_ffn_gate_w': 8.0, 'L0_ffn_w1': 8.0, 'L0_ffn_w2': 8.0}
    for name, (base, spread) in spreads.items():
        noise = np.random.default_rng([zlib.crc32(name.encode()), seed]).standard_normal(out[name].shape)
        drawn = base * np.exp(spread * noise) if base else spread * noise
        out[name] = jnp.asarray(drawn.astype(out[name].dtype))
    for name, factor in factors.items():
        out[name] = (out[name] * factor).astype(out[name].dtype)
    return out
```

```python
from contextlib import ExitStack

import concourse.bass as bass
from concourse import mybir

F32 = mybir.dt.float32
F32R = mybir.dt.float32r
BF16 = mybir.dt.bfloat16
I32 = mybir.dt.int32
ALU = mybir.AluOpType
ACT = mybir.ActivationFunctionType
AX = mybir.AxisListType

P = 128
EPS = 1e-5
GATE_C = 8.0
MOD_MIN = 0.25
CAP = 2
PASSES = ((0, 0), (0, 1), (1, 0))


class Nth:

    def __init__(self, i, n, span):
        self.i, self.n, self.span = i, n, span

    def count(self, per, k=0):
        v = per * self.n + k
        return v if self.i is None else (per * self.span) * self.i + v

    def turn(self, slots, per=16):
        v = per * (self.n // slots + 1)
        return v if self.i is None else (per * self.span // slots) * self.i + v

    def block(self, size):
        v = self.n // size
        return v if self.i is None else (self.span // size) * self.i + v

    def has(self, back):
        return self.i is not None or self.n >= back


def adaln_kernel(nc, x, W_in, b_in, W_gx, b_gx, W_ga, b_ga, a_param, W_out, b_out, gate_w, w1, w2, c, wmod, out):
    B, S, D = x.shape
    E, _, H = w1.shape
    KD = D // P
    KH = H // P
    TOK = B * S
    GT = 512
    TT = GT // P
    NG = TOK // GT
    GB = S // GT
    ST = S // P
    CAPK = CAP * S // E
    CT = CAPK // P
    NMOD = 6
    assert D == 256 and CAPK == GT and ST * E == P and B == 4 and GB == 4

    z_dram = nc.dram_tensor("z_rows", (TOK, D), F32, kind="Internal").ap()
    x1_dram = nc.dram_tensor("x1_rows", (TOK, D), F32, kind="Internal").ap()
    acc_dram = nc.dram_tensor("ffn_rows", (TOK, D), F32, kind="Internal").ap()
    x_rows = x.rearrange("b s d -> (b s) d")
    out_rows = out.rearrange("b s d -> (b s) d")

    def rows(dram, first):
        return dram[bass.ds(first, GT), :].rearrange("(t p) d -> p t d", p=P)

    keep = ExitStack()
    with keep:
        def sbk(name, shape, dt=F32):
            return keep.enter_context(nc.sbuf_tensor(name, shape, dt))

        def sem(name):
            return keep.enter_context(nc.semaphore(name))

        held = [sem(f"waited_{n}") for n in ("pool", "act", "dve", "sp")]
        psum = [keep.enter_context(nc.psum_tensor(f"psum{n}", [P, 2, 512], F32)) for n in range(4)]

        ident = sbk("ident", [P, P])
        gb_bc = sbk("gb_bc", [P, B, D])
        cb1 = sbk("cb1", [P, B, KD])
        sbc = sbk("sbc", [P, B, KD])
        scores = sbk("scores", [P, B, ST, E])

        recur = ExitStack()

        def sbr(name, shape, dt=F32):
            return recur.enter_context(nc.sbuf_tensor(name, shape, dt))

        W_raw = {n: sbr(f"{n}_raw", [P, KD, D]) for n in ("in", "gx", "ga", "out")}
        G_raw = sbr("G_raw", [P, KD, E])
        Wgx = [sbr(f"Wgx{q}", [P, KD, D], F32R) for q in range(2)]
        Wga = [sbr(f"Wga{q}", [P, KD, D], F32R) for q in range(2)]
        ga_bc = sbr("ga_bc", [P, B, D])
        bias_bc = sbr("bias_bc", [P, B, D])
        ca1 = sbr("ca1", [P, B, KD])
        bias_u = sbr("bias_u", [P, B, KD])
        sG_bc = sbr("sG_bc", [P, B, E])
        half_bgx = sbr("half_bgx", [P, KD])
        half_bga = sbr("half_bga", [P, KD])
        decay = sbr("decay", [P, KD])
        decay2 = sbr("decay2", [P, KD])
        mhalf = sbr("mhalf", [P, TT])
        quarter = sbr("quarter", [P, 1])

        su = ExitStack()

        def sbs(name, shape, dt=F32):
            return su.enter_context(nc.sbuf_tensor(name, shape, dt))

        wmod_sb = sbs("wmod_sb", [P, KD, NMOD * D])
        cT = sbs("cT", [P, KD, B])
        silu_c = sbs("silu_c", [P, KD, B])
        silu_bc = sbs("silu_bc", [P, KD, B, P])
        sb_bc = sbs("sb_bc", [P, KD, B, P])
        sa = sbs("sa", [P, B, KD])
        bcol = {n: sbs(f"{n}_col", [P, KD]) for n in ("in", "gx", "ga", "a")}
        bout_bc = sbs("bout_bc", [P, D])
        ap = {n: sbs(f"sp_{n}", [P, KD]) for n in ("neg", "abs", "exp", "u", "ln", "um", "zero", "num", "den", "rec", "l1", "sp")}
        gtmp = {n: sbs(f"gm_{n}", [P, B, D]) for n in ("sign", "neg", "mag")}
        zero_row = sbs("zero_row", [P, 2048])

        s_in = sem("setup_loaded")
        s_silu = sem("silu_ready")
        s_chain = sem("setup_vector_steps")
        s_exp = sem("setup_exp_ready")
        s_mod = sem("mod_products")
        s_row = sem("mod_rows")
        s_one = sem("setup_pool")
        s_zero = sem("acc_zeroed")

        with nc.Block() as block:
            @block.sync
            def _(sp):
                for k in range(KD):
                    sp.dma_start(cT[:, k, :], c[:, k * P:(k + 1) * P].rearrange("b p -> p b"),
                                 allow_slow_non_contiguous=True).then_inc(s_in, 16)
                sp.dma_start(wmod_sb[:], wmod.rearrange("(k p) n -> p k n", p=P)).then_inc(s_in, 16)
                for n, w in (("in", W_in), ("gx", W_gx), ("ga", W_ga), ("out", W_out)):
                    sp.dma_start(W_raw[n][:], w.rearrange("(k p) n -> p k n", p=P)).then_inc(s_in, 16)
                sp.dma_start(G_raw[:], gate_w.rearrange("(k p) n -> p k n", p=P)).then_inc(s_in, 16)
                for n, v in (("in", b_in), ("gx", b_gx), ("ga", b_ga), ("a", a_param)):
                    sp.dma_start(bcol[n][:], v.rearrange("(k p) -> p k", p=P), allow_slow_non_contiguous=True).then_inc(s_in, 16)
                sp.dma_start(bout_bc[:], b_out.rearrange("(o n) -> o n", o=1).to_broadcast([P, D])).then_inc(s_in, 16)
                sp.wait_ge(s_one, 1)
                acc_flat = acc_dram.rearrange("(p r) d -> p (r d)", p=P)
                for n in range(TOK * D // P // 2048):
                    sp.dma_start(acc_flat[:, 2048 * n:2048 * (n + 1)], zero_row[:]).then_inc(s_zero, 16)
                sp.wait_ge(s_zero, 16 * (TOK * D // P // 2048))
            LOADS = 16 * (KD + 11)

            @block.gpsimd
            def _(pool):
                pool.memset(zero_row[:], 0.0).then_inc(s_one, 1)
                pool.memset(mhalf[:], -0.5).then_inc(s_one, 1)
                pool.memset(quarter[:], 0.25).then_inc(s_one, 1)
                pool.memset(ident[:], 0.0).then_inc(s_one, 1)
                pool.wait_ge(s_one, 4)
                pool.affine_select(out=ident[:], in_=ident[:], compare_op=ALU.not_equal, fill=1.0, base=0,
                                   pattern=[[-1, P]], channel_multiplier=1).then_inc(s_one, 1)

            @block.scalar
            def _(act):
                act.wait_ge(s_in, LOADS)
                act.activation(silu_c[:], cT[:], ACT.Silu).then_inc(s_silu, 1)
                act.wait_ge(s_chain, 3)
                act.activation(ap["exp"][:], ap["abs"][:], ACT.Exp, scale=-1.0).then_inc(s_exp, 1)
                act.wait_ge(s_chain, 4)
                act.activation(ap["ln"][:], ap["u"][:], ACT.Ln).then_inc(s_exp, 1)

            @block.tensor
            def _(pe):
                pe.wait_ge(s_in, LOADS)
                pe.wait_ge(s_silu, 1)
                cols = psum[0][:, 0, 0:8 * B].rearrange("p (j m b) -> p j m b", j=4, m=KD)
                for j, part in enumerate((0, 1, 3, 4)):
                    for m in range(KD):
                        for k in range(KD):
                            w = wmod_sb[:, k, part * D + m * P:part * D + (m + 1) * P]
                            last = pe.matmul(cols[:, j, m, :], w, silu_c[:, k, :], start=(k == 0), stop=(k == KD - 1))
                last.then_inc(s_mod, 1)
                pe.wait_ge(s_chain, 1)
                for n, part in ((1, 2), (2, 5)):
                    for b in range(B):
                        for k in range(KD):
                            last = pe.matmul(psum[n][:, b // 2, (b % 2) * D:(b % 2 + 1) * D], silu_bc[:, k, b, :],
                                             wmod_sb[:, k, part * D:(part + 1) * D], start=(k == 0), stop=(k == KD - 1))
                    last.then_inc(s_row, 1)
                pe.wait_ge(s_chain, 15)
                su_cols = psum[0][:, 1, 0:KD * B].rearrange("p (m b) -> p m b", m=KD)
                for m in range(KD):
                    for k in range(KD):
                        pe.matmul(su_cols[:, m, :], W_raw["in"][:, k, m * P:(m + 1) * P], sa[:, :, k],
                                  start=(k == 0), stop=(k == KD - 1))
                sg = psum[0][:, 1, 64:64 + B * E].rearrange("p (b e) -> p b e", b=B)
                for b in range(B):
                    for k in range(KD):
                        last = pe.matmul(sg[:, b, :], sb_bc[:, k, b, :], G_raw[:, k, :], start=(k == 0), stop=(k == KD - 1))
                last.then_inc(s_mod, 1)

            @block.vector
            def _(dve):
                done = [0]

                def step(ins):
                    ins.then_inc(s_chain, 1)
                    done[0] += 1
                    dve.wait_ge(s_chain, done[0])

                dve.wait_ge(s_in, LOADS)
                dve.wait_ge(s_silu, 1)
                step(dve.tensor_copy(silu_bc[:], silu_c[:].unsqueeze(3).to_broadcast([P, KD, B, P])))
                step(dve.tensor_scalar(ap["neg"][:], bcol["a"][:], -1.0, None, ALU.mult))
                step(dve.tensor_tensor(ap["abs"][:], bcol["a"][:], ap["neg"][:], ALU.max))
                dve.wait_ge(s_exp, 1)
                step(dve.tensor_scalar(ap["u"][:], ap["exp"][:], 1.0, None, ALU.add))
                step(dve.tensor_scalar(ap["um"][:], ap["u"][:], -1.0, None, ALU.add))
                step(dve.tensor_scalar(ap["zero"][:], ap["um"][:], 0.0, None, ALU.is_equal))
                step(dve.tensor_tensor(ap["den"][:], ap["um"][:], ap["zero"][:], ALU.add))
                dve.wait_ge(s_exp, 2)
                step(dve.tensor_tensor(ap["num"][:], ap["ln"][:], ap["zero"][:], ALU.add))
                step(dve.reciprocal(ap["rec"][:], ap["den"][:]))
                step(dve.tensor_tensor(ap["l1"][:], ap["num"][:], ap["rec"][:], ALU.mult))
                dve.wait_ge(s_mod, 1)
                cols = psum[0][:, 0, 0:8 * B].rearrange("p (j m b) -> p j b m", j=4, m=KD)
                step(dve.tensor_copy(sa[:], cols[:, 0]))
                step(dve.tensor_scalar(ca1[:], cols[:, 1], 1.0, None, ALU.add))
                step(dve.tensor_copy(sbc[:], cols[:, 2]))
                step(dve.tensor_scalar(cb1[:], cols[:, 3], 1.0, None, ALU.add))
                step(dve.tensor_copy(sb_bc[:], sbc[:].rearrange("p b k -> p k b").unsqueeze(3)
                                     .to_broadcast([P, KD, B, P])))
                step(dve.tensor_tensor(ap["l1"][:], ap["l1"][:], ap["exp"][:], ALU.mult))
                step(dve.scalar_tensor_tensor(out=ap["sp"][:], in0=bcol["a"][:], scalar=0.0, in1=ap["l1"][:],
                                              op0=ALU.max, op1=ALU.add))
                step(dve.tensor_scalar(decay[:], ap["sp"][:], -GATE_C / 2, None, ALU.mult))
                step(dve.tensor_scalar(decay2[:], ap["sp"][:], -GATE_C, None, ALU.mult))
                step(dve.tensor_scalar(half_bgx[:], bcol["gx"][:], 0.5, None, ALU.mult))
                step(dve.tensor_scalar(half_bga[:], bcol["ga"][:], 0.5, None, ALU.mult))
                for w, parts in ((W_raw["gx"], Wgx), (W_raw["ga"], Wga)):
                    step(dve.tensor_copy(parts[0][:], w[:]))
                    step(dve.tensor_tensor(parts[1][:], w[:], parts[0][:].bitcast(F32), ALU.subtract))
                for n, dst in ((1, ga_bc), (2, gb_bc)):
                    dve.wait_ge(s_row, n)
                    g = psum[n][:].rearrange("p h (q d) -> p (h q) d", d=D)
                    step(dve.tensor_scalar(gtmp["sign"][:], g, 0.0, 2.0, ALU.is_ge, ALU.mult))
                    step(dve.tensor_scalar(gtmp["neg"][:], g, -1.0, MOD_MIN, ALU.mult, ALU.max))
                    step(dve.tensor_tensor(gtmp["mag"][:], g, gtmp["neg"][:], ALU.max))
                    step(dve.scalar_tensor_tensor(out=dst[:], in0=gtmp["sign"][:], scalar=-1.0, in1=gtmp["mag"][:],
                                                  op0=ALU.add, op1=ALU.mult))
                step(dve.tensor_tensor(bias_bc[:], ga_bc[:], bout_bc[:].unsqueeze(1).to_broadcast([P, B, D]), ALU.mult))
                dve.wait_ge(s_mod, 2)
                step(dve.tensor_tensor(bias_u[:], psum[0][:, 1, 0:KD * B].rearrange("p (m b) -> p b m", m=KD),
                                       bcol["in"][:].unsqueeze(1).to_broadcast([P, B, KD]), ALU.add))
                step(dve.tensor_copy(sG_bc[:], psum[0][:, 1, 64:64 + B * E].rearrange("p (b e) -> p b e", b=B)))
        su.close()

        x_buf = [sbr(f"x_buf{n}", [P, TT, D]) for n in range(4)]
        xb_buf = [sbr(f"xb_buf{n}", [P, TT, D]) for n in range(4)]
        st1 = sbr("st1", [P, TT, 6])
        mv1 = [sbr(f"mv1_{n}", [P, TT, 2]) for n in range(2)]
        ve1 = sbr("ve1", [P, TT])
        rs1 = sbr("rs1", [P, TT])
        z1 = [sbr(f"z1_{n}", [P, TT, D]) for n in range(2)]
        zT = [sbr(f"zT{q}", [P, KD, GT], F32R) for q in range(2)]
        u_f = [sbr(f"u_f{n}", [P, KD, GT]) for n in range(2)]
        uT = [sbr(f"uT{q}", [P, KD, GT], F32R) for q in range(2)]
        tx = sbr("tx", [P, KD, GT])
        ta = sbr("ta", [P, KD, GT])
        a_t = sbr("a_t", [P, KD, GT])
        a2_t = sbr("a2_t", [P, KD, GT])
        sc_t = sbr("sc_t", [P, KD, GT])
        xg = sbr("xg", [P, KD, GT])
        b_t = sbr("b_t", [P, KD, GT])
        hs = [sbr(f"hs{n}", [P, KD, GT]) for n in range(2)]
        hT = [sbr(f"hT{q}", [P, KD, GT], F32R) for q in range(2)]
        x1 = sbr("x1", [P, TT, D])
        st2 = sbr("st2", [P, TT, 6])
        mv2 = sbr("mv2", [P, TT, 2])
        ve2 = sbr("ve2", [P, TT])
        rs2 = sbr("rs2", [P, TT])
        z2 = [sbr(f"z2_{n}", [P, TT, D]) for n in range(2)]
        z2T = [sbr(f"z2T{q}", [P, KD, GT], F32R) for q in range(2)]
        Win_f = sbr("Win_f", [P, KD, D])
        Win = [sbr(f"Win{q}", [P, KD, D], F32R) for q in range(2)]
        Wout_f = sbr("Wout_f", [P, KD, D])
        Wout = [sbr(f"Wout{q}", [P, KD, D], F32R) for q in range(2)]
        G_f = sbr("G_f", [P, KD, E])
        G = [sbr(f"G{q}", [P, KD, E], F32R) for q in range(2)]

        psT, psU, psG, psO = psum
        O_tok = psO[:].rearrange("p h (q d) -> p (h q) d", d=D)

        r_x = [sem(f"x_loaded{n}") for n in range(4)]
        r_st = sem("stats1_written")
        r_rs = sem("rstd1_steps")
        r_z1 = sem("z1_ready")
        r_xb = sem("xb_ready")
        r_zps = sem("z1T_in_psum")
        r_zh = sem("zT_hi_ready")
        r_zl = sem("zT_lo_ready")
        r_U = sem("u_in_psum")
        r_uf = sem("u_ready")
        r_uh = sem("uT_split")
        r_X = sem("gate_x_in_psum")
        r_A = sem("gate_a_in_psum")
        r_tx = sem("tx_ready")
        r_ta = sem("ta_ready")
        r_a = sem("a_ready")
        r_m = sem("min_a2_ready")
        r_sc = sem("scale_ready")
        r_xg = sem("xg_ready")
        r_b = sem("b_ready")
        r_hs = sem("h_ready")
        r_hh = sem("hT_hi_ready")
        r_hl = sem("hT_lo_ready")
        r_O = sem("out_in_psum")
        r_x1 = sem("x1_ready")
        r_st2 = sem("stats2_written")
        r_rs2 = sem("rstd2_steps")
        r_z2 = sem("z2_ready")
        r_x1s = sem("x1_stored")
        r_z2s = sem("z2_stored")
        r_z2ps = sem("z2T_in_psum")
        r_z2h = sem("z2T_hi_ready")
        r_z2l = sem("z2T_lo_ready")
        r_S = sem("scores_in_psum")
        r_se = sem("scores_kept")
        r_win = sem("W_in_steps")
        r_wout = sem("W_out_steps")
        r_g = sem("gate_w_steps")

        LAG = dict(a=0, b=1, c=2, d=3, e=4)
        PEELED = LAG["e"]
        LOOPS = (NG - PEELED) // GB
        LAST = NG - 1 + LAG["e"]

        def run_steps(eng, step, loops=LOOPS):
            for s in range(PEELED):
                step(None, s)
            with eng.Fori(0, loops) as i:
                for s in range(PEELED, PEELED + GB):
                    step(i, s)
            for s in range(PEELED + loops * GB, LAST + 1):
                step(None, s)

        def stage(i, s, name):
            n = s - LAG[name]
            return Nth(i, n, GB) if i is not None or 0 <= n < NG else None

        def through(i, s, name):
            n = s - LAG[name]
            return GB * i + n if i is not None else max(0, min(n, NG))

        with nc.Block() as block:
            @block.sync
            def _(sp):
                def load_x(g):
                    if g.has(4):
                        sp.wait_ge(r_z1, g.count(1, -3))
                        sp.wait_ge(r_xb, g.count(1, -3))
                    sp.sem_inc(held[3], 1)
                    sp.dma_start(x_buf[g.n % 4][:], rows(x_rows, g.count(GT))).then_inc(r_x[g.n % 4], 16)

                def step(i, s):
                    if i is None and s == 0:
                        for n in range(3):
                            load_x(Nth(None, n, GB))
                    if i is not None or s + 3 < NG:
                        load_x(Nth(i, s + 3, GB))
                    d = stage(i, s, "d")
                    if d:
                        sp.wait_ge(r_x1, d.count(1, 1))
                        sp.sem_inc(held[3], 1)
                        sp.dma_start(rows(x1_dram, d.count(GT)), x1[:]).then_inc(r_x1s, 16)
                        sp.wait_ge(r_z2, d.count(1, 1))
                        sp.sem_inc(held[3], 1)
                        if d.has(1):
                            sp.wait_ge(r_z2s, d.count(16))
                        sp.sem_inc(held[3], 1)
                        sp.dma_start(rows(z_dram, d.count(GT)), z2[d.n % 2][:]).then_inc(r_z2s, 16)

                run_steps(sp, step, LOOPS - 1)
                sp.wait_ge(r_x1s, 16 * NG)
                sp.wait_ge(r_z2s, 16 * NG)

            @block.gpsimd
            def _(pool):
                def step(i, s):
                    a, c_, d = (stage(i, s, k) for k in "acd")
                    if a:
                        mv, z, xs = mv1[a.n % 2], z1[a.n % 2], x_buf[a.n % 4]
                        pool.wait_ge(r_st, a.count(2, 2))
                        pool.wait_ge(r_x[a.n % 4], a.turn(4))
                        if a.has(1):
                            pool.wait_ge(r_z1, a.count(1))
                        pool.sem_inc(held[0], 1)
                        pool.tensor_scalar(ve1[:], mv[:, :, 1], EPS, None, ALU.add).then_inc(r_rs, 1)
                        pool.wait_ge(r_rs, a.count(2, 1))
                        pool.tensor_tensor(rs1[:], ve1[:], mhalf[:], ALU.pow).then_inc(r_rs, 1)
                        pool.wait_ge(r_rs, a.count(2, 2))
                        if a.has(2):
                            pool.wait_ge(r_zps, a.count(1, -1))
                        pool.sem_inc(held[0], 1)
                        for t in range(TT):
                            ins = pool.tensor_scalar(z[:, t, :], xs[:, t, :], mv[:, t, 0:1], rs1[:, t:t + 1],
                                                     ALU.subtract, ALU.mult)
                        ins.then_inc(r_z1, 1)
                    if c_:
                        pool.wait_ge(r_xg, c_.count(1, 1))
                        pool.wait_ge(r_sc, c_.count(1, 1))
                        if c_.has(1):
                            pool.wait_ge(r_hs, c_.count(1))
                        pool.tensor_tensor(b_t[:], xg[:], sc_t[:], ALU.mult).then_inc(r_b, 1)
                    if a:
                        if a.has(4):
                            pool.wait_ge(r_x1, a.count(1, -3))
                        pool.sem_inc(held[0], 1)
                        pool.tensor_tensor(xb_buf[a.n % 4][:], xs[:],
                                           bias_bc[:, bass.ds(a.block(GB), 1), :].to_broadcast([P, TT, D]),
                                           ALU.add).then_inc(r_xb, 1)
                    if d:
                        z = z2[d.n % 2]
                        pool.wait_ge(r_st2, d.count(2, 2))
                        if d.has(1):
                            pool.wait_ge(r_z2, d.count(1))
                        pool.sem_inc(held[0], 1)
                        pool.tensor_scalar(ve2[:], mv2[:, :, 1], EPS, None, ALU.add).then_inc(r_rs2, 1)
                        pool.wait_ge(r_rs2, d.count(2, 1))
                        pool.tensor_tensor(rs2[:], ve2[:], mhalf[:], ALU.pow).then_inc(r_rs2, 1)
                        pool.wait_ge(r_rs2, d.count(2, 2))
                        if d.has(2):
                            pool.wait_ge(r_z2ps, d.count(1, -1))
                            pool.wait_ge(r_z2s, d.count(16, -16))
                        pool.sem_inc(held[0], 1)
                        for t in range(TT):
                            ins = pool.tensor_scalar(z[:, t, :], x1[:, t, :], mv2[:, t, 0:1], rs2[:, t:t + 1],
                                                     ALU.subtract, ALU.mult)
                        ins.then_inc(r_z2, 1)

                run_steps(pool, step)

            @block.scalar
            def _(act):
                def step(i, s):
                    b_, c_, e_ = (stage(i, s, k) for k in "bce")
                    if e_:
                        act.wait_ge(r_z2ps, e_.count(1, 1))
                        act.activation(z2T[0][:], psT[:], ACT.Copy).then_inc(r_z2h, 1)
                    if c_:
                        act.wait_ge(r_X, c_.count(1, 1))
                        if c_.has(1):
                            act.wait_ge(r_xg, c_.count(1))
                        for m in range(KD):
                            ins = act.activation(tx[:, m, :], psG[:, m, :], ACT.Tanh, bias=half_bgx[:, m:m + 1], scale=0.5)
                        ins.then_inc(r_tx, 1)
                        act.wait_ge(r_A, c_.count(1, 1))
                        if c_.has(1):
                            act.wait_ge(r_a, c_.count(2))
                        for m in range(KD):
                            ins = act.activation(ta[:, m, :], psU[:, m, :], ACT.Tanh, bias=half_bga[:, m:m + 1], scale=0.5)
                        ins.then_inc(r_ta, 1)
                        act.wait_ge(r_ta, c_.count(1, 1))
                        if c_.has(1):
                            act.wait_ge(r_sc, c_.count(1))
                        for m in range(KD):
                            ins = act.activation(a2_t[:, m, :], ta[:, m, :], ACT.Exp, bias=decay2[:, m:m + 1],
                                                 scale=decay2[:, m:m + 1])
                        ins.then_inc(r_a, 1)
                        if c_.has(1):
                            act.wait_ge(r_hs, c_.count(1))
                        for m in range(KD):
                            ins = act.activation(a_t[:, m, :], ta[:, m, :], ACT.Exp, bias=decay[:, m:m + 1],
                                                 scale=decay[:, m:m + 1])
                        ins.then_inc(r_a, 1)
                    if b_:
                        act.wait_ge(r_zps, b_.count(1, 1))
                        if b_.has(1):
                            act.wait_ge(r_U, b_.count(1))
                        act.activation(zT[0][:], psT[:], ACT.Copy).then_inc(r_zh, 1)
                    if c_:
                        act.wait_ge(r_m, c_.count(1, 1))
                        if c_.has(1):
                            act.wait_ge(r_b, c_.count(1))
                        act.activation(sc_t[:], a2_t[:], ACT.Sqrt, bias=quarter[:, 0:1], scale=0.25).then_inc(r_sc, 1)
                    if b_:
                        act.wait_ge(r_U, b_.count(1, 1))
                        if b_.has(2):
                            act.wait_ge(r_xg, b_.count(1, -1))
                        act.sem_inc(held[1], 1)
                        for m in range(KD):
                            ins = act.activation(u_f[b_.n % 2][:, m, :], psU[:, m, :], ACT.Identity,
                                                 bias=bias_u[:, bass.ds(b_.block(GB), 1), m])
                        ins.then_inc(r_uf, 1)
                    if c_:
                        act.wait_ge(r_hs, c_.count(1, 1))
                        if c_.has(1):
                            act.wait_ge(r_O, c_.count(1))
                        act.activation(hT[0][:], hs[c_.n % 2][:], ACT.Copy).then_inc(r_hh, 1)

                run_steps(act, step)

            @block.vector
            def _(dve):
                def split(parts, full, done, count):
                    dve.tensor_copy(parts[0][:], full[:]).then_inc(done, 1)
                    dve.wait_ge(done, count + 1)
                    dve.tensor_tensor(parts[1][:], full[:], parts[0][:].bitcast(F32), ALU.subtract).then_inc(done, 1)

                def step(i, s):
                    a, b_, c_, d, e_ = (stage(i, s, k) for k in "abcde")
                    if b_ and b_.n % GB == 0:
                        if b_.has(1):
                            dve.wait_ge(r_U, b_.count(1))
                        for k in range(KD):
                            ins = dve.tensor_scalar(Win_f[:, k, :], W_raw["in"][:, k, :],
                                                    ca1[:, bass.ds(b_.block(GB), 1), k], None, ALU.mult)
                        ins.then_inc(r_win, 1)
                        dve.wait_ge(r_win, 3 * b_.block(GB) + 1)
                        split(Win, Win_f, r_win, 3 * b_.block(GB) + 1)
                    if d and d.n % GB == 0:
                        if d.has(1):
                            dve.wait_ge(r_O, d.count(1))
                        dve.tensor_tensor(Wout_f[:], W_raw["out"][:],
                                          ga_bc[:, bass.ds(d.block(GB), 1), :].to_broadcast([P, KD, D]),
                                          ALU.mult).then_inc(r_wout, 1)
                        dve.wait_ge(r_wout, 3 * d.block(GB) + 1)
                        split(Wout, Wout_f, r_wout, 3 * d.block(GB) + 1)
                    if e_ and e_.n % GB == 0:
                        if e_.has(1):
                            dve.wait_ge(r_S, e_.count(1))
                        for k in range(KD):
                            ins = dve.tensor_scalar(G_f[:, k, :], G_raw[:, k, :], cb1[:, bass.ds(e_.block(GB), 1), k],
                                                    None, ALU.mult)
                        ins.then_inc(r_g, 1)
                        dve.wait_ge(r_g, 3 * e_.block(GB) + 1)
                        split(G, G_f, r_g, 3 * e_.block(GB) + 1)
                    if a:
                        dve.wait_ge(r_x[a.n % 4], a.turn(4))
                        if a.has(1):
                            dve.wait_ge(r_st, a.count(2))
                        for t in range(TT):
                            ins = dve.bn_stats(st1[:, t, :], x_buf[a.n % 4][:, t, :])
                        ins.then_inc(r_st, 1)
                        dve.wait_ge(r_st, a.count(2, 1))
                        if a.has(2):
                            dve.wait_ge(r_z1, a.count(1, -1))
                        dve.sem_inc(held[2], 1)
                        for t in range(TT):
                            ins = dve.bn_aggr(mv1[a.n % 2][:, t, :], st1[:, t, :])
                        ins.then_inc(r_st, 1)
                    if e_:
                        dve.wait_ge(r_z2h, e_.count(1, 1))
                        if e_.has(1):
                            dve.wait_ge(r_S, e_.count(1))
                        dve.tensor_tensor(z2T[1][:], psT[:], z2T[0][:].bitcast(F32), ALU.subtract).then_inc(r_z2l, 1)
                    if c_:
                        dve.wait_ge(r_tx, c_.count(1, 1))
                        dve.wait_ge(r_uf, c_.count(1, 1))
                        if c_.has(1):
                            dve.wait_ge(r_b, c_.count(1))
                        dve.scalar_tensor_tensor(out=xg[:], in0=tx[:], scalar=1.0, in1=u_f[c_.n % 2][:], op0=ALU.add,
                                                 op1=ALU.mult).then_inc(r_xg, 1)
                        dve.wait_ge(r_a, c_.count(2, 1))
                        dve.tensor_scalar(a2_t[:], a2_t[:], 1.0, -1.0, ALU.min, ALU.mult).then_inc(r_m, 1)
                    if e_:
                        dve.wait_ge(r_S, e_.count(1, 1))
                        q = e_.n % GB
                        dve.tensor_tensor(scores[:, bass.ds(e_.block(GB), 1), TT * q:TT * (q + 1), :],
                                          psT[:, 0, 0:TT * E].rearrange("p (o t e) -> p o t e", o=1, e=E),
                                          sG_bc[:, bass.ds(e_.block(GB), 1), :].unsqueeze(2).to_broadcast([P, 1, TT, E]),
                                          ALU.add).then_inc(r_se, 1)
                    if d:
                        dve.wait_ge(r_O, d.count(1, 1))
                        dve.wait_ge(r_xb, d.count(1, 1))
                        if d.has(1):
                            dve.wait_ge(r_x1s, d.count(16))
                            dve.wait_ge(r_z2, d.count(1))
                        dve.tensor_tensor(x1[:], O_tok, xb_buf[d.n % 4][:], ALU.add).then_inc(r_x1, 1)
                        dve.wait_ge(r_x1, d.count(1, 1))
                        for t in range(TT):
                            ins = dve.bn_stats(st2[:, t, :], x1[:, t, :])
                        ins.then_inc(r_st2, 1)
                        dve.wait_ge(r_st2, d.count(2, 1))
                        dve.sem_inc(held[2], 1)
                        for t in range(TT):
                            ins = dve.bn_aggr(mv2[:, t, :], st2[:, t, :])
                        ins.then_inc(r_st2, 1)
                    if b_:
                        dve.wait_ge(r_zh, b_.count(1, 1))
                        dve.tensor_tensor(zT[1][:], psT[:], zT[0][:].bitcast(F32), ALU.subtract).then_inc(r_zl, 1)
                    if c_:
                        dve.wait_ge(r_b, c_.count(1, 1))
                        dve.wait_ge(r_a, c_.count(2, 2))
                        if c_.has(1):
                            dve.wait_ge(r_hs, c_.count(1))
                            dve.wait_ge(r_hl, c_.count(1))
                        if c_.has(2):
                            dve.wait_ge(r_hh, c_.count(1, -1))
                        for m in range(KD):
                            before = 0.0 if c_.n % GB == 0 else hs[(c_.n - 1) % 2][:, m, GT - 1:GT]
                            ins = dve.tensor_tensor_scan(hs[c_.n % 2][:, m, :], a_t[:, m, :], b_t[:, m, :], before,
                                                         ALU.mult, ALU.add)
                        ins.then_inc(r_hs, 1)
                    if b_:
                        dve.wait_ge(r_uf, b_.count(1, 1))
                        if b_.has(1):
                            dve.wait_ge(r_A, b_.count(1))
                        split(uT, u_f[b_.n % 2], r_uh, b_.count(2))
                    if c_:
                        dve.wait_ge(r_hh, c_.count(1, 1))
                        dve.tensor_tensor(hT[1][:], hs[c_.n % 2][:], hT[0][:].bitcast(F32), ALU.subtract).then_inc(r_hl, 1)

                run_steps(dve, step)

            @block.tensor
            def _(pe):
                def product(out_, stationary, moving):
                    terms = [(k, q) for k in range(KD) for q in PASSES]
                    for j, (k, (qs, qm)) in enumerate(terms):
                        ins = pe.matmul(out_, stationary(qs, k), moving(qm, k), start=(j == 0), stop=(j == len(terms) - 1))
                    return ins

                def cols(w, m):
                    return lambda q, k: w[q][:, k, m * P:(m + 1) * P]

                def whole(t):
                    return lambda q, k: t[q][:, k, :]

                def to_channels(z):
                    for t in range(TT):
                        for k in range(KD):
                            ins = pe.transpose(psT[:, k, t * P:(t + 1) * P], z[:, t, k * P:(k + 1) * P], ident[:])
                    return ins

                def step(i, s):
                    b_, c_, d, e_ = (stage(i, s, k) for k in "bcde")
                    if e_:
                        pe.wait_ge(r_z2, e_.count(1, 1))
                        pe.wait_ge(r_zl, through(i, s, "b"))
                        to_channels(z2[e_.n % 2]).then_inc(r_z2ps, 1)
                    if c_:
                        pe.wait_ge(r_uh, c_.count(2, 2))
                        if c_.has(1):
                            pe.wait_ge(r_tx, c_.count(1))
                        for m in range(KD):
                            ins = product(psG[:, m, :], cols(Wgx, m), whole(uT))
                        ins.then_inc(r_X, 1)
                    if e_:
                        pe.wait_ge(r_z2l, e_.count(1, 1))
                        pe.wait_ge(r_g, 3 * e_.block(GB) + 3)
                        for t in range(TT):
                            ins = product(psT[:, 0, t * E:(t + 1) * E], cols(z2T, t), whole(G))
                        ins.then_inc(r_S, 1)
                    if c_:
                        for m in range(KD):
                            ins = product(psU[:, m, :], cols(Wga, m), whole(uT))
                        ins.then_inc(r_A, 1)
                    if d:
                        pe.wait_ge(r_hl, d.count(1, 1))
                        pe.wait_ge(r_wout, 3 * d.block(GB) + 3)
                        if d.has(1):
                            pe.wait_ge(r_x1, d.count(1))
                        for t in range(TT):
                            ins = product(O_tok[:, t, :], cols(hT, t), whole(Wout))
                        ins.then_inc(r_O, 1)
                    if b_:
                        pe.wait_ge(r_z1, b_.count(1, 1))
                        if e_:
                            pe.wait_ge(r_se, e_.count(1, 1))
                        elif b_.has(1):
                            pe.wait_ge(r_zl, b_.count(1))
                        to_channels(z1[b_.n % 2]).then_inc(r_zps, 1)
                        pe.wait_ge(r_zl, b_.count(1, 1))
                        pe.wait_ge(r_win, 3 * b_.block(GB) + 3)
                        if c_:
                            pe.wait_ge(r_ta, c_.count(1, 1))
                        for m in range(KD):
                            ins = product(psU[:, m, :], cols(Win, m), whole(zT))
                        ins.then_inc(r_U, 1)

                run_steps(pe, step)
        recur.close()

        NC = B * ST * E
        BITS = 30
        VALS = 5
        route = ExitStack()

        def sbt(name, shape, dt=F32):
            return route.enter_context(nc.sbuf_tensor(name, shape, dt))

        idx_all = sbk("idx_all", [P, E, B, CT], I32)
        g_all = sbk("g_all", [P, E, B, CT])
        top = sbt("top", [P, B * ST])
        shifted = sbt("shifted", [P, NC])
        expd = sbt("expd", [P, NC])
        total = sbt("total", [P, B * ST])
        inv = sbt("inv", [P, B * ST])
        probs = sbt("probs", [P, NC])
        probsT = sbt("probsT", [P, B, P])
        rel = sbt("rel", [P, P], I32)
        rel7 = sbt("rel7", [P, P], I32)
        same_e = sbt("same_e", [P, P], BF16)
        before_e = sbt("before_e", [P, P], BF16)
        row_id = sbt("row_id", [P, P], BF16)
        ct_id = sbt("ct_id", [P, CT])
        tok_id = sbt("tok_id", [P, 1])
        tile_id = sbt("tile_id", [P, NC])
        ones = sbt("ones", [P, P])
        cand = sbt("cand", [P, B], I32)
        bit = sbt("bit", [P, 2])
        over = sbt("over", [P, B])
        flip = sbt("flip", [P, B], I32)
        hit = sbt("hit", [P, B, P], BF16)
        n_hit = sbt("n_hit", [P, B], BF16)
        gt = sbt("gt", [P, B, P])
        eq = sbt("eq", [P, B, P])
        ceq = sbt("ceq", [P, B, P])
        n_eq = sbt("n_eq", [P, B], BF16)
        need = sbt("need", [P, B])
        room = sbt("room", [P, B])
        sel = sbt("sel", [P, B, P])
        csel = sbt("csel", [P, B, P])
        n_sel = sbt("n_sel", [P, B], BF16)
        first_slot = sbt("first_slot", [P, B])
        slot1 = sbt("slot1", [P, B, P])
        slot_i = sbt("slot_i", [P, NC], I32)
        slot_lo = sbt("slot_lo", [P, NC], I32)
        slot_hi = sbt("slot_hi", [P, NC], I32)
        slot_lo_f = sbt("slot_lo_f", [P, B, ST, E])
        slot_hi_f = sbt("slot_hi_f", [P, NC])
        in_ct = sbt("in_ct", [P, NC, CT], BF16)
        gpart = [sbt(f"gpart{n}", [P, NC], BF16) for n in range(3)]
        grest = [sbt(f"grest{n}", [P, NC]) for n in range(2)]
        vals = sbt("vals", [P, NC, VALS, CT], BF16)
        place = [sbt(f"place{n}", [P, ST, P], BF16) for n in range(B)]
        lists = [sbt(f"lists{n}", [P, B, VALS, CT]) for n in range(2)]
        slot_e = sbt("slot_e", [P, B, ST, 1])
        g12 = sbt("g12", [P, B, CT])

        t_pool = sem("route_pool")
        t_step = sem("route_vector_steps")
        t_exp = sem("route_exp")
        t_pT = sem("probsT_in_psum")
        t_cnt = sem("hits_counted")
        t_num = sem("hits_summed")
        t_bit = sem("candidate_steps")
        t_off = sem("offsets_in_psum")
        t_slot = sem("slots_turned")
        t_place = [sem(f"place_ready{n}") for n in range(B)]
        t_read = [sem(f"place_used{n}") for n in range(B)]
        t_se = sem("slot_e_ready")
        t_kept = sem("lists_kept")
        t_idx = sem("lists_steps")
        COUNTS_DONE, SELECTED, SLOT_KNOWN, VALS_DONE = 15, 21, 23, 39
        with nc.Block() as block:
            @block.gpsimd
            def _(pool):
                pool.iota(rel[:], [[1, P]], base=P, channel_multiplier=-1).then_inc(t_pool, 1)
                pool.iota(row_id[:], [[1, P]], base=0, channel_multiplier=0,
                          allow_small_or_imprecise_dtypes=True).then_inc(t_pool, 1)
                pool.iota(ct_id[:], [[1, CT]], base=0, channel_multiplier=0,
                          allow_small_or_imprecise_dtypes=True).then_inc(t_pool, 1)
                pool.iota(tok_id[:], [[1, 1]], base=0, channel_multiplier=1,
                          allow_small_or_imprecise_dtypes=True).then_inc(t_pool, 1)
                pool.iota(tile_id[:], [[1, B * ST], [0, E]], base=0, channel_multiplier=0,
                          allow_small_or_imprecise_dtypes=True).then_inc(t_pool, 1)
                pool.memset(ones[:], 1.0).then_inc(t_pool, 1)

            @block.scalar
            def _(act):
                act.wait_ge(t_step, 2)
                act.activation(expd[:], shifted[:], ACT.Exp).then_inc(t_exp, 1)

            @block.tensor
            def _(pe):
                pe.wait_ge(t_step, 5)
                for b in range(B):
                    ins = pe.transpose(psum[0][:, 0, b * P:(b + 1) * P], probs[:, b * P:(b + 1) * P], ident[:])
                ins.then_inc(t_pT, 1)
                with pe.Fori(0, BITS) as j:
                    pe.wait_ge(t_cnt, j + 1)
                    pe.matmul(psum[1][:, 0, 0:B], same_e[:], n_hit[:], start=True, stop=True).then_inc(t_num, 1)
                pe.wait_ge(t_step, COUNTS_DONE)
                pe.matmul(psum[1][:, 1, 0:B], same_e[:], n_hit[:], start=True, stop=True)
                pe.matmul(psum[1][:, 1, B:2 * B], before_e[:], n_eq[:], start=True, stop=True).then_inc(t_off, 1)
                pe.wait_ge(t_step, SELECTED)
                pe.matmul(psum[1][:, 1, 2 * B:3 * B], before_e[:], n_sel[:], start=True, stop=True).then_inc(t_off, 1)
                pe.wait_ge(t_step, SLOT_KNOWN)
                for b in range(B):
                    ins = pe.transpose(psum[0][:, 1, b * P:(b + 1) * P], slot1[:, b, :], ident[:])
                ins.then_inc(t_slot, 1)
                pe.wait_ge(t_step, VALS_DONE)

                def one(j, q):
                    e = Nth(j, q, 2)
                    ps = psum[2 + q][:, 0, 0:B * VALS * CT].rearrange("p (b v) -> p b v", b=B)
                    if e.has(2):
                        pe.wait_ge(t_kept, e.count(1, -1))
                    for b in range(B):
                        pe.wait_ge(t_place[b], e.count(1, 1))
                        for t in range(ST):
                            row = bass.ds((b * ST + t) * E + e.count(1), 1)
                            ins = pe.matmul(ps[:, b, :], place[b][:, t, :],
                                            vals[:, row, :, :].rearrange("p o v c -> p (o v c)"),
                                            start=(t == 0), stop=(t == ST - 1))
                        ins.then_inc(t_read[b], 1)
                for q in range(2):
                    one(None, q)
                with pe.Fori(1, E // 2) as j:
                    for q in range(2):
                        one(j, q)

            @block.vector
            def _(dve):
                n_step = [0]

                def step(ins):
                    ins.then_inc(t_step, 1)
                    n_step[0] += 1
                    dve.wait_ge(t_step, n_step[0])

                sc = scores[:].rearrange("p b t e -> p (b t) e")
                sh = shifted[:].rearrange("p (t e) -> p t e", e=E)
                ex = expd[:].rearrange("p (t e) -> p t e", e=E)
                step(dve.tensor_reduce(top[:], sc, AX.X, ALU.max))
                step(dve.tensor_tensor(sh, sc, top[:].unsqueeze(2).to_broadcast([P, B * ST, E]), ALU.subtract))
                dve.wait_ge(t_exp, 1)
                step(dve.tensor_reduce(total[:], ex, AX.X, ALU.add))
                step(dve.reciprocal(inv[:], total[:]))
                step(dve.tensor_tensor(probs[:].rearrange("p (t e) -> p t e", e=E), ex,
                                       inv[:].unsqueeze(2).to_broadcast([P, B * ST, E]), ALU.mult))
                dve.wait_ge(t_pool, 6)
                step(dve.tensor_scalar(rel7[:], rel[:], E - 1, None, ALU.bitwise_and))
                step(dve.tensor_scalar(same_e[:], rel7[:], 0, None, ALU.is_equal))
                step(dve.scalar_tensor_tensor(out=before_e[:], in0=rel[:], scalar=float(P), in1=same_e[:],
                                              op0=ALU.is_gt, op1=ALU.mult))
                step(dve.memset(cand[:], 1 << (BITS - 1)))
                step(dve.memset(bit[:, 0:1], float(1 << (BITS - 1))))
                step(dve.memset(bit[:, 1:2], float(1 << (BITS - 2))))
                dve.wait_ge(t_pT, 1)
                step(dve.tensor_copy(probsT[:], psum[0][:, 0, :].rearrange("p (b t) -> p b t", b=B)))
                cand_f = cand[:].bitcast(F32)

                def search(j, last):
                    for b in range(B):
                        ins = dve.tensor_scalar(hit[:, b, :], probsT[:, b, :], cand_f[:, b:b + 1], None, ALU.is_ge,
                                                ALU.add, accum_out=n_hit[:, b:b + 1])
                    ins.then_inc(t_cnt, 1)
                    dve.wait_ge(t_num, j + 1)
                    if last:
                        dve.tensor_scalar(flip[:], psum[1][:, 0, 0:B], float(CAPK), bit[:, 0:1], ALU.is_lt,
                                          ALU.mult).then_inc(t_bit, 1)
                        dve.wait_ge(t_bit, 4 * (BITS - 1) + 1)
                        dve.tensor_tensor(cand[:], cand[:], flip[:], ALU.bitwise_xor).then_inc(t_bit, 1)
                        dve.wait_ge(t_bit, 4 * (BITS - 1) + 2)
                        return
                    dve.tensor_scalar(over[:], psum[1][:, 0, 0:B], float(CAPK), bit[:, 0:1], ALU.is_lt,
                                      ALU.mult).then_inc(t_bit, 1)
                    dve.wait_ge(t_bit, 4 * j + 1)
                    dve.tensor_scalar(flip[:], over[:], bit[:, 1:2], None, ALU.add).then_inc(t_bit, 1)
                    dve.wait_ge(t_bit, 4 * j + 2)
                    dve.tensor_tensor(cand[:], cand[:], flip[:], ALU.bitwise_xor).then_inc(t_bit, 1)
                    dve.tensor_scalar(bit[:], bit[:], 0.5, None, ALU.mult).then_inc(t_bit, 1)
                    dve.wait_ge(t_bit, 4 * j + 4)

                with dve.Fori(0, BITS - 1) as j:
                    search(j, False)
                search(BITS - 1, True)
                for b in range(B):
                    dve.tensor_scalar(gt[:, b, :], probsT[:, b, :], cand_f[:, b:b + 1], None, ALU.is_gt, ALU.add,
                                            accum_out=n_hit[:, b:b + 1])
                    eq_last = dve.tensor_scalar(eq[:, b, :], probsT[:, b, :], cand_f[:, b:b + 1], None, ALU.is_equal)
                step(eq_last)
                for b in range(B):
                    ins = dve.tensor_tensor_scan(ceq[:, b, :], ones[:], eq[:, b, :], 0.0, ALU.mult, ALU.add)
                step(ins)
                step(dve.tensor_copy(n_eq[:], ceq[:, :, P - 1]))
                assert n_step[0] == COUNTS_DONE
                dve.wait_ge(t_off, 1)
                step(dve.tensor_scalar(need[:], psum[1][:, 1, 0:B], -1.0, float(CAPK), ALU.mult, ALU.add))
                step(dve.tensor_tensor(room[:], need[:], psum[1][:, 1, B:2 * B], ALU.subtract))
                for b in range(B):
                    ins = dve.scalar_tensor_tensor(out=sel[:, b, :], in0=ceq[:, b, :], scalar=room[:, b:b + 1],
                                                   in1=eq[:, b, :], op0=ALU.is_le, op1=ALU.mult)
                step(ins)
                step(dve.tensor_tensor(sel[:], sel[:], gt[:], ALU.add))
                for b in range(B):
                    ins = dve.tensor_tensor_scan(csel[:, b, :], ones[:], sel[:, b, :], 0.0, ALU.mult, ALU.add)
                step(ins)
                step(dve.tensor_copy(n_sel[:], csel[:, :, P - 1]))
                assert n_step[0] == SELECTED
                dve.wait_ge(t_off, 2)
                step(dve.tensor_copy(first_slot[:], psum[1][:, 1, 2 * B:3 * B]))
                for b in range(B):
                    ins = dve.scalar_tensor_tensor(out=slot1[:, b, :], in0=csel[:, b, :], scalar=first_slot[:, b:b + 1],
                                                   in1=sel[:, b, :], op0=ALU.add, op1=ALU.mult)
                step(ins)
                assert n_step[0] == SLOT_KNOWN
                dve.wait_ge(t_slot, 1)
                step(dve.tensor_scalar(slot_i[:], psum[0][:, 1, :], -1.0, None, ALU.add))
                step(dve.tensor_scalar(slot_lo[:], slot_i[:], P - 1, None, ALU.bitwise_and))
                step(dve.tensor_copy(slot_lo_f[:].rearrange("p b t e -> p (b t e)"), slot_lo[:]))
                step(dve.tensor_scalar(slot_hi[:], slot_i[:], P.bit_length() - 1, None, ALU.arith_shift_right))
                step(dve.tensor_copy(slot_hi_f[:], slot_hi[:]))
                step(dve.tensor_tensor(in_ct[:], slot_hi_f[:].unsqueeze(2).to_broadcast([P, NC, CT]),
                                       ct_id[:].unsqueeze(1).to_broadcast([P, NC, CT]), ALU.is_equal))
                step(dve.tensor_copy(gpart[0][:], probs[:]))
                step(dve.tensor_tensor(grest[0][:], probs[:], gpart[0][:], ALU.subtract))
                step(dve.tensor_copy(gpart[1][:], grest[0][:]))
                step(dve.tensor_tensor(grest[1][:], grest[0][:], gpart[1][:], ALU.subtract))
                step(dve.tensor_copy(gpart[2][:], grest[1][:]))
                step(dve.tensor_scalar(vals[:, :, 0, :], in_ct[:], tok_id[:, 0:1], None, ALU.mult))
                for v, src in enumerate((tile_id, *gpart)):
                    step(dve.tensor_tensor(vals[:, :, 1 + v, :], in_ct[:], src[:].unsqueeze(2).to_broadcast([P, NC, CT]),
                                           ALU.mult))
                assert n_step[0] == VALS_DONE

                def one(j, q):
                    e = Nth(j, q, 2)
                    if e.has(1):
                        dve.wait_ge(t_read[B - 1], e.count(1))
                    dve.tensor_copy(slot_e[:], slot_lo_f[:, :, :, bass.ds(e.count(1), 1)]).then_inc(t_se, 1)
                    dve.wait_ge(t_se, e.count(1, 1))
                    for b in range(B):
                        if e.has(1):
                            dve.wait_ge(t_read[b], e.count(1))
                        for t in range(ST):
                            ins = dve.tensor_scalar(place[b][:, t, :], row_id[:], slot_e[:, b, t, 0:1], None, ALU.is_equal)
                        ins.then_inc(t_place[b], 1)
                    dve.wait_ge(t_read[B - 1], e.count(1, 1))
                    ls = lists[q]
                    if e.has(1):
                        dve.wait_ge(t_idx, e.count(3))
                    dve.tensor_copy(ls[:], psum[2 + q][:, 0, 0:B * VALS * CT]
                                    .rearrange("p (b v c) -> p b v c", b=B, v=VALS)).then_inc(t_kept, 1)
                    dve.wait_ge(t_kept, e.count(1, 1))
                    at = bass.ds(e.count(1), 1)
                    dve.scalar_tensor_tensor(out=idx_all[:, at, :, :].rearrange("p o b c -> p (o b) c"),
                                             in0=ls[:, :, 1, :], scalar=float(P), in1=ls[:, :, 0, :],
                                             op0=ALU.mult, op1=ALU.add).then_inc(t_idx, 1)
                    dve.tensor_tensor(g12[:], ls[:, :, 2, :], ls[:, :, 3, :], ALU.add).then_inc(t_idx, 1)
                    dve.wait_ge(t_idx, e.count(3, 2))
                    dve.tensor_tensor(g_all[:, at, :, :].rearrange("p o b c -> p (o b) c"), g12[:], ls[:, :, 4, :],
                                      ALU.add).then_inc(t_idx, 1)

                for q in range(2):
                    one(None, q)
                with dve.Fori(1, E // 2) as j:
                    for q in range(2):
                        one(j, q)
        route.close()
        BODY = 2 * B
        PASSES_F = E // 2
        HC = H // KD
        moe = ExitStack()

        def sbf(name, shape, dt=F32):
            return moe.enter_context(nc.sbuf_tensor(name, shape, dt))

        w1_raw = sbf("w1_raw", [P, KD, H])
        w2_raw = sbf("w2_raw", [P, KH, D])
        w1_s = [[sbf(f"w1_{n}{q}", [P, KD, H], F32R) for q in range(2)] for n in range(2)]
        w2_s = [[sbf(f"w2_{n}{q}", [P, KH, D], F32R) for q in range(2)] for n in range(2)]
        idx_cur = [sbf(f"idx_cur{n}", [P, B, CT], I32) for n in range(2)]
        g_cur = [sbf(f"g_cur{n}", [P, B, CT]) for n in range(2)]
        rows_in = [sbf(f"rows_in{n}", [P, CT, D]) for n in range(2)]
        xf = sbf("xf", [P, KD, CAPK])
        xT = [sbf(f"xT{q}", [P, KD, CAPK], F32R) for q in range(2)]
        HF = 4
        hf = [sbf(f"hf{n}", [P, CAPK]) for n in range(HF)]
        hidT = [sbf(f"hidT{q}", [P, KH, CAPK], F32R) for q in range(2)]
        rows_y = [sbf(f"rows_y{n}", [P, CT, D]) for n in range(2)]

        f_w1 = sem("w1_loaded")
        f_w2 = sem("w2_loaded")
        f_ws = sem("weights_split")
        f_idx = sem("idx_cur_ready")
        f_in = [sem(f"rows_gathered{n}") for n in range(2)]
        f_T = sem("rows_turned")
        f_xf = sem("xf_ready")
        f_x = sem("xT_split")
        f_H = sem("hidden_in_psum")
        f_hf = sem("hidden_ready")
        f_hh = sem("hidT_hi_ready")
        f_hl = sem("hidT_lo_ready")
        f_Y = sem("y_in_psum")
        f_y = sem("rows_y_ready")
        f_add = [sem(f"rows_added{b}") for b in range(B)]

        psT, psH0, psH1, psY = psum
        H_bank = [psH0[:, 0, :], psH0[:, 1, :], psH1[:, 0, :], psH1[:, 1, :]]
        Y_tok = psY[:].rearrange("p h (q d) -> p (h q) d", d=D)
        w1_v = w1.rearrange("e (k p) h -> e p k h", p=P)
        w2_v = w2.rearrange("e (k p) d -> e p k d", p=P)

        def run_units(eng, step):
            for j in range(BODY):
                step(None, j)
            with eng.Fori(1, PASSES_F - 1) as i:
                for j in range(BODY):
                    step(i, j)
            for j in range((PASSES_F - 1) * BODY, PASSES_F * BODY):
                step(None, j)

        with nc.Block() as block:
            @block.sync
            def _(sp):
                def load(e):
                    if e.has(1):
                        sp.wait_ge(f_ws, e.count(8, -4))
                    sp.dma_start(w1_raw[:], w1_v[bass.ds(e.count(1), 1)].rearrange("o p k h -> p (o k) h")).then_inc(f_w1, 16)
                    if e.has(1):
                        sp.wait_ge(f_ws, e.count(8))
                    sp.dma_start(w2_raw[:], w2_v[bass.ds(e.count(1), 1)].rearrange("o p k d -> p (o k) d")).then_inc(f_w2, 16)
                load(Nth(None, 0, 1))
                with sp.Fori(1, E) as i:
                    load(Nth(i, 0, 1))

            @block.gpsimd
            def _(pool):
                def fetch(u):
                    n = (u.n // B) % 2
                    if u.n % B == 0:
                        if u.has(2 * B):
                            for b in range(B):
                                pool.wait_ge(f_add[b], 16 * CT * (u.block(B) - 1))
                            pool.wait_ge(f_y, 2 * B * (u.block(B) - 1))
                        e = bass.ds(u.block(B), 1)
                        pool.tensor_copy(idx_cur[n][:], idx_all[:, e, :, :].rearrange("p o b c -> p (o b) c")).then_inc(f_idx, 1)
                        pool.tensor_copy(g_cur[n][:], g_all[:, e, :, :].rearrange("p o b c -> p (o b) c")).then_inc(f_idx, 1)
                        pool.wait_ge(f_idx, 2 * u.block(B) + 2)
                    if u.has(2):
                        pool.wait_ge(f_T, u.count(1, -1))
                    pool.sem_inc(held[0], 1)
                    for t in range(CT):
                        pool.indirect_dma_start(rows_in[u.n % 2][:, t, :], None, z_dram,
                                                bass.IndirectOffsetOnAxis(ap=idx_cur[n][:, u.n % B, t:t + 1], axis=0))\
                            .then_inc(f_in[u.n % 2], 16)

                def add(u):
                    n, b = (u.n // B) % 2, u.n % B
                    pool.wait_ge(f_y, u.count(2, 2))
                    if u.has(B):
                        pool.wait_ge(f_add[b], 16 * CT * u.block(B))
                    pool.sem_inc(held[0], 1)
                    for t in range(CT):
                        pool.indirect_dma_start(acc_dram, bass.IndirectOffsetOnAxis(ap=idx_cur[n][:, b, t:t + 1], axis=0),
                                                rows_y[u.n % 2][:, t, :], None, compute_op=ALU.add).then_inc(f_add[b], 16)

                def step(i, j):
                    if i is not None or j + 1 < E * B:
                        fetch(Nth(i, j + 1, BODY))
                    if i is not None or j >= 1:
                        add(Nth(i, j - 1, BODY))
                fetch(Nth(None, 0, BODY))
                run_units(pool, step)
                add(Nth(None, E * B - 1, BODY))
                for b in range(B):
                    pool.wait_ge(f_add[b], 16 * CT * E)

            @block.scalar
            def _(act):
                def weigh(u):
                    n, b = (u.n // B) % 2, u.n % B
                    act.wait_ge(f_idx, 2 * u.block(B) + 2)
                    for h in range(2):
                        act.wait_ge(f_Y, u.count(2, h + 1))
                        if h == 0 and u.has(2):
                            v = Nth(u.i, u.n - 2, BODY)
                            act.wait_ge(f_add[v.n % B], 16 * CT * (v.block(B) + 1))
                        for t in range(2 * h, 2 * h + 2):
                            ins = act.activation(rows_y[u.n % 2][:, t, :], Y_tok[:, t, :], ACT.Copy,
                                                 scale=g_cur[n][:, b, t:t + 1])
                        ins.then_inc(f_y, 1)

                def step(i, j):
                    u = Nth(i, j, BODY)
                    act.wait_ge(f_T, u.count(1, 1))
                    if u.has(1):
                        act.wait_ge(f_x, u.count(2))
                    for k in range(KD):
                        ins = act.activation(xf[:, k, :], psT[:, k, :], ACT.Identity, bias=sbc[:, j % B, k:k + 1],
                                             scale=cb1[:, j % B, k:k + 1])
                    ins.then_inc(f_xf, 1)
                    if u.has(1):
                        weigh(Nth(i, j - 1, BODY))
                    for m in range(KH):
                        act.wait_ge(f_H, u.count(KH, m + 1))
                        if u.has(1) or m >= HF:
                            act.wait_ge(f_hl, u.count(KH, m + 1 - HF))
                        act.activation(hf[m % HF][:], H_bank[m % 4], ACT.Gelu_apprx_tanh).then_inc(f_hf, 1)
                run_units(act, step)
                weigh(Nth(None, E * B - 1, BODY))

            @block.vector
            def _(dve):
                def split_chunk(e, n, q):
                    raw, parts, half = (w1_raw, w1_s[n], q) if q < 2 else (w2_raw, w2_s[n], q - 2)
                    at = slice(half, half + 1) if q < 2 else slice(half * KH // 2, (half + 1) * KH // 2)
                    dve.wait_ge(f_w1 if q < 2 else f_w2, 16 * e + 16)
                    dve.tensor_copy(parts[0][:, at, :], raw[:, at, :]).then_inc(f_ws, 1)
                    dve.wait_ge(f_ws, 8 * e + (2 * q + 1))
                    dve.tensor_tensor(parts[1][:, at, :], raw[:, at, :], parts[0][:, at, :].bitcast(F32),
                                      ALU.subtract).then_inc(f_ws, 1)

                def step(i, j):
                    u = Nth(i, j, BODY)
                    dve.wait_ge(f_xf, u.count(1, 1))
                    if u.has(1):
                        dve.wait_ge(f_H, u.count(KH))
                    dve.tensor_copy(xT[0][:], xf[:]).then_inc(f_x, 1)
                    dve.wait_ge(f_x, u.count(2, 1))
                    dve.tensor_tensor(xT[1][:], xf[:], xT[0][:].bitcast(F32), ALU.subtract).then_inc(f_x, 1)
                    for m in range(KH):
                        dve.wait_ge(f_hf, u.count(KH, m + 1))
                        if m == 0 and u.has(1):
                            dve.wait_ge(f_Y, u.count(2))
                        dve.tensor_copy(hidT[0][:, m, :], hf[m % HF][:]).then_inc(f_hh, 1)
                        dve.wait_ge(f_hh, u.count(KH, m + 1))
                        dve.tensor_tensor(hidT[1][:, m, :], hf[m % HF][:], hidT[0][:, m, :].bitcast(F32),
                                          ALU.subtract).then_inc(f_hl, 1)
                        if m == 3 and (i is not None or j // B + 1 < E):
                            split_chunk(u.block(B) + 1, (j // B + 1) % 2, j % B)
                for q in range(4):
                    split_chunk(0, 0, q)
                run_units(dve, step)

            @block.tensor
            def _(pe):
                def turn(u):
                    pe.wait_ge(f_in[u.n % 2], u.turn(2, 16 * CT))
                    if u.has(1):
                        pe.wait_ge(f_xf, u.count(1))
                    for t in range(CT):
                        for k in range(KD):
                            ins = pe.transpose(psT[:, k, t * P:(t + 1) * P], rows_in[u.n % 2][:, t, k * P:(k + 1) * P],
                                               ident[:])
                    ins.then_inc(f_T, 1)

                def layer2(u):
                    n = (u.n // B) % 2
                    pe.wait_ge(f_ws, 8 * u.block(B) + 8)
                    for t in range(CT):
                        if t % 2 == 0 and u.has(1):
                            pe.wait_ge(f_y, u.count(2, t // 2 - 1))
                        terms = [(k, q) for k in range(KH) for q in PASSES]
                        for x_, (k, (qs, qm)) in enumerate(terms):
                            if t == 0 and x_ % len(PASSES) == 0:
                                pe.wait_ge(f_hl, u.count(KH, k + 1))
                            ins = pe.matmul(Y_tok[:, t, :], hidT[qs][:, k, t * P:(t + 1) * P], w2_s[n][qm][:, k, :],
                                            start=(x_ == 0), stop=(x_ == len(terms) - 1))
                        if t % 2 == 1:
                            ins.then_inc(f_Y, 1)

                def layer1(u):
                    n = (u.n // B) % 2
                    pe.wait_ge(f_x, u.count(2, 2))
                    pe.wait_ge(f_ws, 8 * u.block(B) + 4)
                    for m in range(KH):
                        if u.has(1) or m >= 4:
                            pe.wait_ge(f_hf, u.count(KH, m + 1 - 4))
                        terms = [(k, q) for k in range(KD) for q in PASSES]
                        for x_, (k, (qs, qm)) in enumerate(terms):
                            ins = pe.matmul(H_bank[m % 4], w1_s[n][qs][:, k, m * P:(m + 1) * P], xT[qm][:, k, :],
                                            start=(x_ == 0), stop=(x_ == len(terms) - 1))
                        ins.then_inc(f_H, 1)

                def step(i, j):
                    u = Nth(i, j, BODY)
                    turn(u)
                    if u.has(1):
                        layer2(Nth(i, j - 1, BODY))
                    layer1(u)
                run_units(pe, step)
                layer2(Nth(None, E * B - 1, BODY))
        moe.close()

        fin = ExitStack()

        def sbz(name, shape, dt=F32):
            return fin.enter_context(nc.sbuf_tensor(name, shape, dt))

        acc_t = [sbz(f"acc_t{n}", [P, TT, D]) for n in range(4)]
        res_t = [sbz(f"res_t{n}", [P, TT, D]) for n in range(4)]
        acc16 = [sbz(f"acc16_{n}", [P, TT, D], BF16) for n in range(4)]
        prod = [sbz(f"prod{n}", [P, TT, D]) for n in range(4)]
        o_acc = [sem(f"acc_loaded{n}") for n in range(4)]
        o_x1 = [sem(f"x1_loaded{n}") for n in range(4)]
        o_16 = sem("acc16_ready")
        o_p = sem("gated_ready")
        o_r = sem("result_ready")
        o_out = [sem(f"out_stored{n}") for n in range(4)]

        def run_groups(eng, step):
            for s in range(GB):
                step(Nth(None, s, GB))
            with eng.Fori(1, B) as i:
                for s in range(GB):
                    step(Nth(i, s, GB))

        with nc.Block() as block:
            @block.sync
            def _(sp):
                def step(g):
                    n = g.n % 4
                    if g.has(4):
                        sp.wait_ge(o_16, g.count(1, -3))
                        sp.sem_inc(held[3], 1)
                        sp.wait_ge(o_out[n], g.turn(4, 16) - 16)
                    sp.dma_start(acc_t[n][:], rows(acc_dram, g.count(GT))).then_inc(o_acc[n], 16)
                    sp.dma_start(res_t[n][:], rows(x1_dram, g.count(GT))).then_inc(o_x1[n], 16)
                run_groups(sp, step)

            @block.vector
            def _(dve):
                def step(g):
                    n = g.n % 4
                    dve.wait_ge(o_acc[n], g.turn(4))
                    if g.has(4):
                        dve.wait_ge(o_p, g.count(1, -3))
                    dve.tensor_copy(acc16[n][:], acc_t[n][:]).then_inc(o_16, 1)
                    if g.has(1):
                        finish(Nth(g.i, g.n - 1, GB))

                def finish(g):
                    n = g.n % 4
                    dve.wait_ge(o_p, g.count(1, 1))
                    dve.wait_ge(o_x1[n], g.turn(4))
                    dve.tensor_tensor(res_t[n][:], prod[n][:], res_t[n][:], ALU.add).then_inc(o_r, 1)
                run_groups(dve, step)
                finish(Nth(None, NG - 1, GB))

            @block.gpsimd
            def _(pool):
                def step(g):
                    n = g.n % 4
                    pool.wait_ge(o_16, g.count(1, 1))
                    if g.has(4):
                        pool.wait_ge(o_r, g.count(1, -3))
                    pool.sem_inc(held[0], 1)
                    pool.tensor_tensor(prod[n][:], acc16[n][:], gb_bc[:, bass.ds(g.block(GB), 1), :]
                                       .to_broadcast([P, TT, D]), ALU.mult).then_inc(o_p, 1)
                run_groups(pool, step)

            @block.scalar
            def _(act):
                def step(g):
                    act.wait_ge(o_r, g.count(1, 1))
                    act.dma_start(rows(out_rows, g.count(GT)), res_t[g.n % 4][:]).then_inc(o_out[g.n % 4], 16)
                run_groups(act, step)
                for n in range(4):
                    act.wait_ge(o_out[n], 16 * B)
        fin.close()


_INS = ["L0_attn_x", "L0_attn_W_in", "L0_attn_b_in", "L0_attn_W_gx", "L0_attn_b_gx", "L0_attn_W_ga", "L0_attn_b_ga",
        "L0_attn_a_param", "L0_attn_W_out", "L0_attn_b_out", "L0_ffn_gate_w", "L0_ffn_w1", "L0_ffn_w2", "L0_c", "L0_wmod"]


def kernel(**inputs):
    import numpy as _np
    import concourse.bacc as _bacc
    from concourse import mybir as _mybir
    from concourse.bass_utils import run_bass_kernel_spmd as _run

    nc = _bacc.Bacc("TRN2", target_bir_lowering=False, num_devices=1)
    arrays, args = {}, []
    for name in _INS:
        a = _np.ascontiguousarray(inputs[name])
        arrays[f"in_{name}"] = a
        args.append(nc.dram_tensor(f"in_{name}", a.shape, _mybir.dt.from_np(a.dtype), kind="ExternalInput").ap())
    shape = arrays["in_L0_attn_x"].shape
    args.append(nc.dram_tensor("out_x", shape, _mybir.dt.float32, kind="ExternalOutput").ap())
    adaln_kernel(nc, *args)
    r = _run(nc, [arrays], core_ids=[0])
    return r.results[0]["out_x"]
```

```python
from contextlib import ExitStack

import concourse.bass as bass
from concourse import mybir

F32 = mybir.dt.float32
F32R = mybir.dt.float32r
BF16 = mybir.dt.bfloat16
I32 = mybir.dt.int32
ALU = mybir.AluOpType
ACT = mybir.ActivationFunctionType
AX = mybir.AxisListType

P = 128
EPS = 1e-5
GATE_C = 8.0
MOD_MIN = 0.25
CAP = 2
PASSES = ((0, 0), (0, 1), (1, 0))


class Nth:

    def __init__(self, i, n, span):
        self.i, self.n, self.span = i, n, span

    def count(self, per, k=0):
        v = per * self.n + k
        return v if self.i is None else (per * self.span) * self.i + v

    def turn(self, slots, per=16):
        v = per * (self.n // slots + 1)
        return v if self.i is None else (per * self.span // slots) * self.i + v

    def block(self, size):
        v = self.n // size
        return v if self.i is None else (self.span // size) * self.i + v

    def has(self, back):
        return self.i is not None or self.n >= back


def adaln_kernel(nc, x, W_in, b_in, W_gx, b_gx, W_ga, b_ga, a_param, W_out, b_out, gate_w, w1, w2, c, wmod, out):
    B, S, D = x.shape
    E, _, H = w1.shape
    KD = D // P
    KH = H // P
    TOK = B * S
    GT = 512
    TT = GT // P
    NG = TOK // GT
    GB = S // GT
    ST = S // P
    CAPK = CAP * S // E
    CT = CAPK // P
    NMOD = 6
    assert D == 256 and CAPK == GT and ST * E == P and B == 4 and GB == 4

    z_dram = nc.dram_tensor("z_rows", (TOK, D + E), F32, kind="Internal").ap()
    x1_dram = nc.dram_tensor("x1_rows", (TOK, D), F32, kind="Internal").ap()
    acc_dram = nc.dram_tensor("ffn_rows", (TOK, D), F32, kind="Internal").ap()
    x_rows = x.rearrange("b s d -> (b s) d")
    out_rows = out.rearrange("b s d -> (b s) d")

    def rows(dram, first):
        return dram[bass.ds(first, GT), :].rearrange("(t p) d -> p t d", p=P)

    keep = ExitStack()
    with keep:
        def sbk(name, shape, dt=F32):
            return keep.enter_context(nc.sbuf_tensor(name, shape, dt))

        def sem(name):
            return keep.enter_context(nc.semaphore(name))

        held = [sem(f"waited_{n}") for n in ("pool", "act", "dve", "sp", "pe")]
        psum = [keep.enter_context(nc.psum_tensor(f"psum{n}", [P, 2, 512], F32)) for n in range(4)]

        ident = sbk("ident", [P, P])
        gb_bc = sbk("gb_bc", [P, B, D])
        cb1 = sbk("cb1", [P, B, KD])
        sbc = sbk("sbc", [P, B, KD])
        scores = sbk("scores", [P, B, ST, E])

        recur = ExitStack()

        def sbr(name, shape, dt=F32):
            return recur.enter_context(nc.sbuf_tensor(name, shape, dt))

        W_raw = {n: sbr(f"{n}_raw", [P, KD, D]) for n in ("in", "gx", "ga", "out")}
        G_raw = sbr("G_raw", [P, KD, E])
        Wgx = [sbr(f"Wgx{q}", [P, KD, D], F32R) for q in range(2)]
        Wga = [sbr(f"Wga{q}", [P, KD, D], F32R) for q in range(2)]
        ga_bc = sbr("ga_bc", [P, B, D])
        bias_bc = sbr("bias_bc", [P, B, D])
        ca1 = sbr("ca1", [P, B, KD])
        bias_u = sbr("bias_u", [P, B, KD])
        bias_s = sbr("bias_s", [E, B])
        half_bgx = sbr("half_bgx", [P, KD])
        half_bga = sbr("half_bga", [P, KD])
        decay = sbr("decay", [P, KD])
        decay2 = sbr("decay2", [P, KD])
        mhalf = sbr("mhalf", [P, TT])
        quarter = sbr("quarter", [P, 1])

        su = ExitStack()

        def sbs(name, shape, dt=F32):
            return su.enter_context(nc.sbuf_tensor(name, shape, dt))

        wmod_sb = sbs("wmod_sb", [P, KD, NMOD * D])
        cT = sbs("cT", [P, KD, B])
        silu_c = sbs("silu_c", [P, KD, B])
        silu_bc = sbs("silu_bc", [P, KD, B, P])
        sa = sbs("sa", [P, B, KD])
        bcol = {n: sbs(f"{n}_col", [P, KD]) for n in ("in", "gx", "ga", "a")}
        bout_bc = sbs("bout_bc", [P, D])
        ap = {n: sbs(f"sp_{n}", [P, KD]) for n in ("neg", "abs", "exp", "u", "ln", "um", "zero", "num", "den", "rec", "l1", "sp")}
        gtmp = {n: sbs(f"gm_{n}", [P, B, D]) for n in ("sign", "neg", "mag")}
        zero_row = sbs("zero_row", [P, 2048])

        s_in = sem("setup_loaded")
        s_silu = sem("silu_ready")
        s_chain = sem("setup_vector_steps")
        s_exp = sem("setup_exp_ready")
        s_mod = sem("mod_products")
        s_row = sem("mod_rows")
        s_one = sem("setup_pool")
        s_zero = sem("acc_zeroed")

        with nc.Block() as block:
            @block.sync
            def _(sp):
                for k in range(KD):
                    sp.dma_start(cT[:, k, :], c[:, k * P:(k + 1) * P].rearrange("b p -> p b"),
                                 allow_slow_non_contiguous=True).then_inc(s_in, 16)
                sp.dma_start(wmod_sb[:], wmod.rearrange("(k p) n -> p k n", p=P)).then_inc(s_in, 16)
                for n, w in (("in", W_in), ("gx", W_gx), ("ga", W_ga), ("out", W_out)):
                    sp.dma_start(W_raw[n][:], w.rearrange("(k p) n -> p k n", p=P)).then_inc(s_in, 16)
                sp.dma_start(G_raw[:], gate_w.rearrange("(k p) n -> p k n", p=P)).then_inc(s_in, 16)
                for n, v in (("in", b_in), ("gx", b_gx), ("ga", b_ga), ("a", a_param)):
                    sp.dma_start(bcol[n][:], v.rearrange("(k p) -> p k", p=P), allow_slow_non_contiguous=True).then_inc(s_in, 16)
                sp.dma_start(bout_bc[:], b_out.rearrange("(o n) -> o n", o=1).to_broadcast([P, D])).then_inc(s_in, 16)
                sp.wait_ge(s_one, 1)
                acc_flat = acc_dram.rearrange("(p r) d -> p (r d)", p=P)
                for n in range(TOK * D // P // 2048):
                    sp.dma_start(acc_flat[:, 2048 * n:2048 * (n + 1)], zero_row[:]).then_inc(s_zero, 16)
                sp.wait_ge(s_zero, 16 * (TOK * D // P // 2048))
            LOADS = 16 * (KD + 11)

            @block.gpsimd
            def _(pool):
                pool.memset(zero_row[:], 0.0).then_inc(s_one, 1)
                pool.memset(mhalf[:], -0.5).then_inc(s_one, 1)
                pool.memset(quarter[:], 0.25).then_inc(s_one, 1)
                pool.memset(ident[:], 0.0).then_inc(s_one, 1)
                pool.wait_ge(s_one, 4)
                pool.affine_select(out=ident[:], in_=ident[:], compare_op=ALU.not_equal, fill=1.0, base=0,
                                   pattern=[[-1, P]], channel_multiplier=1).then_inc(s_one, 1)

            @block.scalar
            def _(act):
                act.wait_ge(s_in, LOADS)
                act.activation(silu_c[:], cT[:], ACT.Silu).then_inc(s_silu, 1)
                act.wait_ge(s_chain, 3)
                act.activation(ap["exp"][:], ap["abs"][:], ACT.Exp, scale=-1.0).then_inc(s_exp, 1)
                act.wait_ge(s_chain, 4)
                act.activation(ap["ln"][:], ap["u"][:], ACT.Ln).then_inc(s_exp, 1)

            @block.tensor
            def _(pe):
                pe.wait_ge(s_in, LOADS)
                pe.wait_ge(s_silu, 1)
                cols = psum[0][:, 0, 0:8 * B].rearrange("p (j m b) -> p j m b", j=4, m=KD)
                for j, part in enumerate((0, 1, 3, 4)):
                    for m in range(KD):
                        for k in range(KD):
                            w = wmod_sb[:, k, part * D + m * P:part * D + (m + 1) * P]
                            last = pe.matmul(cols[:, j, m, :], w, silu_c[:, k, :], start=(k == 0), stop=(k == KD - 1))
                last.then_inc(s_mod, 1)
                pe.wait_ge(s_chain, 1)
                for n, part in ((1, 2), (2, 5)):
                    for b in range(B):
                        for k in range(KD):
                            last = pe.matmul(psum[n][:, b // 2, (b % 2) * D:(b % 2 + 1) * D], silu_bc[:, k, b, :],
                                             wmod_sb[:, k, part * D:(part + 1) * D], start=(k == 0), stop=(k == KD - 1))
                    last.then_inc(s_row, 1)
                pe.wait_ge(s_chain, 14)
                su_cols = psum[0][:, 1, 0:KD * B].rearrange("p (m b) -> p m b", m=KD)
                for m in range(KD):
                    for k in range(KD):
                        pe.matmul(su_cols[:, m, :], W_raw["in"][:, k, m * P:(m + 1) * P], sa[:, :, k],
                                  start=(k == 0), stop=(k == KD - 1))
                for k in range(KD):
                    last = pe.matmul(psum[0][0:E, 1, 64:64 + B], G_raw[:, k, :], sbc[:, :, k], start=(k == 0), stop=(k == KD - 1))
                last.then_inc(s_mod, 1)

            @block.vector
            def _(dve):
                done = [0]

                def step(ins):
                    ins.then_inc(s_chain, 1)
                    done[0] += 1
                    dve.wait_ge(s_chain, done[0])

                dve.wait_ge(s_in, LOADS)
                dve.wait_ge(s_silu, 1)
                step(dve.tensor_copy(silu_bc[:], silu_c[:].unsqueeze(3).to_broadcast([P, KD, B, P])))
                step(dve.tensor_scalar(ap["neg"][:], bcol["a"][:], -1.0, None, ALU.mult))
                step(dve.tensor_tensor(ap["abs"][:], bcol["a"][:], ap["neg"][:], ALU.max))
                dve.wait_ge(s_exp, 1)
                step(dve.tensor_scalar(ap["u"][:], ap["exp"][:], 1.0, None, ALU.add))
                step(dve.tensor_scalar(ap["um"][:], ap["u"][:], -1.0, None, ALU.add))
                step(dve.tensor_scalar(ap["zero"][:], ap["um"][:], 0.0, None, ALU.is_equal))
                step(dve.tensor_tensor(ap["den"][:], ap["um"][:], ap["zero"][:], ALU.add))
                dve.wait_ge(s_exp, 2)
                step(dve.tensor_tensor(ap["num"][:], ap["ln"][:], ap["zero"][:], ALU.add))
                step(dve.reciprocal(ap["rec"][:], ap["den"][:]))
                step(dve.tensor_tensor(ap["l1"][:], ap["num"][:], ap["rec"][:], ALU.mult))
                dve.wait_ge(s_mod, 1)
                cols = psum[0][:, 0, 0:8 * B].rearrange("p (j m b) -> p j b m", j=4, m=KD)
                step(dve.tensor_copy(sa[:], cols[:, 0]))
                step(dve.tensor_scalar(ca1[:], cols[:, 1], 1.0, None, ALU.add))
                step(dve.tensor_copy(sbc[:], cols[:, 2]))
                step(dve.tensor_scalar(cb1[:], cols[:, 3], 1.0, None, ALU.add))
                step(dve.tensor_tensor(ap["l1"][:], ap["l1"][:], ap["exp"][:], ALU.mult))
                step(dve.scalar_tensor_tensor(out=ap["sp"][:], in0=bcol["a"][:], scalar=0.0, in1=ap["l1"][:],
                                              op0=ALU.max, op1=ALU.add))
                step(dve.tensor_scalar(decay[:], ap["sp"][:], -GATE_C / 2, None, ALU.mult))
                step(dve.tensor_scalar(decay2[:], ap["sp"][:], -GATE_C, None, ALU.mult))
                step(dve.tensor_scalar(half_bgx[:], bcol["gx"][:], 0.5, None, ALU.mult))
                step(dve.tensor_scalar(half_bga[:], bcol["ga"][:], 0.5, None, ALU.mult))
                for w, parts in ((W_raw["gx"], Wgx), (W_raw["ga"], Wga)):
                    step(dve.tensor_copy(parts[0][:], w[:]))
                    step(dve.tensor_tensor(parts[1][:], w[:], parts[0][:].bitcast(F32), ALU.subtract))
                for n, dst in ((1, ga_bc), (2, gb_bc)):
                    dve.wait_ge(s_row, n)
                    g = psum[n][:].rearrange("p h (q d) -> p (h q) d", d=D)
                    step(dve.tensor_scalar(gtmp["sign"][:], g, 0.0, 2.0, ALU.is_ge, ALU.mult))
                    step(dve.tensor_scalar(gtmp["neg"][:], g, -1.0, MOD_MIN, ALU.mult, ALU.max))
                    step(dve.tensor_tensor(gtmp["mag"][:], g, gtmp["neg"][:], ALU.max))
                    step(dve.scalar_tensor_tensor(out=dst[:], in0=gtmp["sign"][:], scalar=-1.0, in1=gtmp["mag"][:],
                                                  op0=ALU.add, op1=ALU.mult))
                step(dve.tensor_tensor(bias_bc[:], ga_bc[:], bout_bc[:].unsqueeze(1).to_broadcast([P, B, D]), ALU.mult))
                dve.wait_ge(s_mod, 2)
                step(dve.tensor_tensor(bias_u[:], psum[0][:, 1, 0:KD * B].rearrange("p (m b) -> p b m", m=KD),
                                       bcol["in"][:].unsqueeze(1).to_broadcast([P, B, KD]), ALU.add))
                step(dve.tensor_copy(bias_s[:], psum[0][0:E, 1, 64:64 + B]))
        su.close()

        x_buf = [sbr(f"x_buf{n}", [P, TT, D]) for n in range(4)]
        xb_buf = [sbr(f"xb_buf{n}", [P, TT, D]) for n in range(4)]
        st1 = sbr("st1", [P, TT, 6])
        mv1 = [sbr(f"mv1_{n}", [P, TT, 2]) for n in range(2)]
        ve1 = sbr("ve1", [P, TT])
        rs1 = sbr("rs1", [P, TT])
        z1 = [sbr(f"z1_{n}", [P, TT, D]) for n in range(2)]
        zT = [sbr(f"zT{q}", [P, KD, GT], F32R) for q in range(2)]
        u_f = [sbr(f"u_f{n}", [P, KD, GT]) for n in range(2)]
        uT = [sbr(f"uT{q}", [P, KD, GT], F32R) for q in range(2)]
        tx = sbr("tx", [P, KD, GT])
        ta = sbr("ta", [P, KD, GT])
        a_t = [sbr(f"a_t{n}", [P, KD, GT]) for n in range(2)]
        a2_t = [sbr(f"a2_t{n}", [P, KD, GT]) for n in range(2)]
        sc_t = sbr("sc_t", [P, KD, GT])
        xg = [sbr(f"xg{n}", [P, KD, GT]) for n in range(2)]
        b_t = sbr("b_t", [P, KD, GT])
        hs = [sbr(f"hs{n}", [P, KD, GT]) for n in range(2)]
        hT = [sbr(f"hT{q}", [P, KD, GT], F32R) for q in range(2)]
        x1 = sbr("x1", [P, TT, D])
        st2 = sbr("st2", [P, TT, 6])
        mv2 = sbr("mv2", [P, TT, 2])
        ve2 = sbr("ve2", [P, TT])
        rs2 = sbr("rs2", [P, TT])
        z2 = [sbr(f"z2_{n}", [P, TT, D]) for n in range(2)]
        z2T = [sbr(f"z2T{q}", [P, KD, GT], F32R) for q in range(2)]
        Win_f = sbr("Win_f", [P, KD, D])
        Win = [sbr(f"Win{q}", [P, KD, D], F32R) for q in range(2)]
        Wout_f = sbr("Wout_f", [P, KD, D])
        Wout = [sbr(f"Wout{q}", [P, KD, D], F32R) for q in range(2)]
        G_f = sbr("G_f", [P, KD, E])
        G = [sbr(f"G{q}", [P, KD, E], F32R) for q in range(2)]
        scoresT = sbr("scoresT", [E, GT])

        psT, psU, psG, psO = psum
        O_tok = psO[:].rearrange("p h (q d) -> p (h q) d", d=D)

        r_x = [sem(f"x_loaded{n}") for n in range(4)]
        r_st = sem("stats1_written")
        r_rs = sem("rstd1_steps")
        r_z1 = sem("z1_ready")
        r_xb = sem("xb_ready")
        r_zps = sem("z1T_in_psum")
        r_zh = sem("zT_hi_ready")
        r_zl = sem("zT_lo_ready")
        r_U = sem("u_in_psum")
        r_uf = sem("u_ready")
        r_uh = sem("uT_split")
        r_X = sem("gate_x_in_psum")
        r_A = sem("gate_a_in_psum")
        r_tx = sem("tx_ready")
        r_ta = sem("ta_ready")
        r_a = sem("a_ready")
        r_m = sem("min_a2_ready")
        r_sc = sem("scale_ready")
        r_xg = sem("xg_ready")
        r_b = sem("b_ready")
        r_hs = sem("h_ready")
        r_hh = sem("hT_hi_ready")
        r_hl = sem("hT_lo_ready")
        r_O = sem("out_in_psum")
        r_x1 = sem("x1_ready")
        r_st2 = sem("stats2_written")
        r_rs2 = sem("rstd2_steps")
        r_z2 = sem("z2_ready")
        r_x1s = sem("x1_stored")
        r_z2s = sem("z2_stored")
        r_z2ps = sem("z2T_in_psum")
        r_z2h = sem("z2T_hi_ready")
        r_z2l = sem("z2T_lo_ready")
        r_S = sem("scores_in_psum")
        r_sT = sem("scoresT_ready")
        r_sps = sem("scores_turned")
        r_se = sem("scores_kept")
        r_win = sem("W_in_steps")
        r_wout = sem("W_out_steps")
        r_g = sem("gate_w_steps")

        LAG = dict(a=0, b=1, c=2, r=3, d=4, e=5, f=6)
        PEELED = LAG["f"]
        LOOPS = (NG - PEELED) // GB
        AHEAD = 2
        LAST = NG - 1 + LAG["f"]

        def run_steps(eng, step):
            for s in range(PEELED):
                step(None, s)
            with eng.Fori(0, LOOPS) as i:
                for s in range(PEELED, PEELED + GB):
                    step(i, s)
            for s in range(PEELED + LOOPS * GB, LAST + 1):
                step(None, s)

        def stage(i, s, name):
            n = s - LAG[name]
            return Nth(i, n, GB) if i is not None or 0 <= n < NG else None

        def through(i, s, name):
            n = s - LAG[name]
            return GB * i + n if i is not None else max(0, min(n, NG))

        with nc.Block() as block:
            @block.sync
            def _(sp):
                def load_x(g):
                    if g.has(4):
                        sp.wait_ge(r_z1, g.count(1, -3))
                        sp.wait_ge(r_xb, g.count(1, -3))
                    sp.sem_inc(held[3], 1)
                    sp.dma_start(x_buf[g.n % 4][:], rows(x_rows, g.count(GT))).then_inc(r_x[g.n % 4], 16)

                def step(i, s):
                    if i is None and s == 0:
                        for n in range(AHEAD):
                            load_x(Nth(None, n, GB))
                    if i is not None or s + AHEAD < NG:
                        load_x(Nth(i, s + AHEAD, GB))
                    d = stage(i, s, "d")
                    if d:
                        sp.wait_ge(r_x1, d.count(1, 1))
                        sp.sem_inc(held[3], 1)
                        sp.dma_start(rows(x1_dram, d.count(GT)), x1[:]).then_inc(r_x1s, 16)
                        sp.wait_ge(r_z2, d.count(1, 1))
                        sp.sem_inc(held[3], 1)
                        if d.has(1):
                            sp.wait_ge(r_z2s, d.count(16))
                        sp.sem_inc(held[3], 1)
                        sp.dma_start(rows(z_dram, d.count(GT))[:, :, 0:D], z2[d.n % 2][:]).then_inc(r_z2s, 16)

                run_steps(sp, step)
                sp.wait_ge(r_x1s, 16 * NG)
                sp.wait_ge(r_z2s, 16 * NG)

            @block.gpsimd
            def _(pool):
                def step(i, s):
                    a, r_, d = (stage(i, s, k) for k in "ard")
                    if r_:
                        pool.wait_ge(r_xg, r_.count(1, 1))
                        pool.wait_ge(r_sc, r_.count(1, 1))
                        if r_.has(1):
                            pool.wait_ge(r_hs, r_.count(1))
                        pool.tensor_tensor(b_t[:], xg[r_.n % 2][:], sc_t[:], ALU.mult).then_inc(r_b, 1)
                    if a:
                        pool.wait_ge(r_st, a.count(2, 2))
                        if a.has(1):
                            pool.wait_ge(r_z1, a.count(1))
                        pool.sem_inc(held[0], 1)
                        pool.tensor_scalar(ve1[:], mv1[a.n % 2][:, :, 1], EPS, None, ALU.add).then_inc(r_rs, 1)
                        pool.wait_ge(r_rs, a.count(2, 1))
                        pool.tensor_tensor(rs1[:], ve1[:], mhalf[:], ALU.pow).then_inc(r_rs, 1)
                    if d:
                        pool.wait_ge(r_st2, d.count(2, 2))
                        if d.has(1):
                            pool.wait_ge(r_z2, d.count(1))
                        pool.sem_inc(held[0], 1)
                        pool.tensor_scalar(ve2[:], mv2[:, :, 1], EPS, None, ALU.add).then_inc(r_rs2, 1)
                        pool.wait_ge(r_rs2, d.count(2, 1))
                        pool.tensor_tensor(rs2[:], ve2[:], mhalf[:], ALU.pow).then_inc(r_rs2, 1)
                    if r_:
                        pool.wait_ge(r_hh, r_.count(1, 1))
                        pool.tensor_tensor(hT[1][:], hs[r_.n % 2][:], hT[0][:].bitcast(F32),
                                           ALU.subtract).then_inc(r_hl, 1)
                    if a:
                        pool.wait_ge(r_x[a.n % 4], a.turn(4))
                        if a.has(4):
                            pool.wait_ge(r_x1, a.count(1, -3))
                        pool.sem_inc(held[0], 1)
                        pool.tensor_tensor(xb_buf[a.n % 4][:], x_buf[a.n % 4][:],
                                           bias_bc[:, bass.ds(a.block(GB), 1), :].to_broadcast([P, TT, D]),
                                           ALU.add).then_inc(r_xb, 1)

                run_steps(pool, step)

            @block.scalar
            def _(act):
                def step(i, s):
                    b_, c_, r_, e_, f_ = (stage(i, s, k) for k in "bcref")
                    if r_:
                        act.wait_ge(r_m, r_.count(1, 1))
                        if r_.has(1):
                            act.wait_ge(r_b, r_.count(1))
                        act.activation(sc_t[:], a2_t[r_.n % 2][:], ACT.Sqrt, bias=quarter[:, 0:1],
                                       scale=0.25).then_inc(r_sc, 1)
                    if b_:
                        act.wait_ge(r_zps, b_.count(1, 1))
                        if b_.has(1):
                            act.wait_ge(r_U, b_.count(1))
                        act.activation(zT[0][:], psT[:], ACT.Copy).then_inc(r_zh, 1)
                    if f_:
                        act.wait_ge(r_S, f_.count(1, 1))
                        if f_.has(1):
                            act.wait_ge(r_sps, f_.count(1))
                        act.sem_inc(held[1], 1)
                        act.activation(scoresT[:], psG[0:E, 0, :], ACT.Identity,
                                       bias=bias_s[:, bass.ds(f_.block(GB), 1)]).then_inc(r_sT, 1)
                    if c_:
                        act.wait_ge(r_X, c_.count(1, 1))
                        if c_.has(1):
                            act.wait_ge(r_xg, c_.count(1))
                        for m in range(KD):
                            ins = act.activation(tx[:, m, :], psG[:, m, :], ACT.Tanh, bias=half_bgx[:, m:m + 1], scale=0.5)
                        ins.then_inc(r_tx, 1)
                    if c_:
                        act.wait_ge(r_A, c_.count(1, 1))
                        if c_.has(1):
                            act.wait_ge(r_a, c_.count(2))
                        for m in range(KD):
                            ins = act.activation(ta[:, m, :], psU[:, m, :], ACT.Tanh, bias=half_bga[:, m:m + 1], scale=0.5)
                        ins.then_inc(r_ta, 1)
                        act.wait_ge(r_ta, c_.count(1, 1))
                        if c_.has(2):
                            act.wait_ge(r_sc, c_.count(1, -1))
                        for m in range(KD):
                            ins = act.activation(a2_t[c_.n % 2][:, m, :], ta[:, m, :], ACT.Exp, bias=decay2[:, m:m + 1],
                                                 scale=decay2[:, m:m + 1])
                        ins.then_inc(r_a, 1)
                        if c_.has(2):
                            act.wait_ge(r_hs, c_.count(1, -1))
                        for m in range(KD):
                            ins = act.activation(a_t[c_.n % 2][:, m, :], ta[:, m, :], ACT.Exp, bias=decay[:, m:m + 1],
                                                 scale=decay[:, m:m + 1])
                        ins.then_inc(r_a, 1)
                    if r_:
                        act.wait_ge(r_hs, r_.count(1, 1))
                        if r_.has(1):
                            act.wait_ge(r_O, r_.count(1))
                        act.activation(hT[0][:], hs[r_.n % 2][:], ACT.Copy).then_inc(r_hh, 1)
                    if e_:
                        act.wait_ge(r_z2ps, e_.count(1, 1))
                        act.activation(z2T[0][:], psT[:], ACT.Copy).then_inc(r_z2h, 1)
                    if b_:
                        act.wait_ge(r_U, b_.count(1, 1))
                        if b_.has(2):
                            act.wait_ge(r_xg, b_.count(1, -1))
                        act.sem_inc(held[1], 1)
                        for m in range(KD):
                            ins = act.activation(u_f[b_.n % 2][:, m, :], psU[:, m, :], ACT.Identity,
                                                 bias=bias_u[:, bass.ds(b_.block(GB), 1), m])
                        ins.then_inc(r_uf, 1)

                run_steps(act, step)

            @block.vector
            def _(dve):
                def split(parts, full, done, count):
                    dve.tensor_copy(parts[0][:], full[:]).then_inc(done, 1)
                    dve.wait_ge(done, count + 1)
                    dve.tensor_tensor(parts[1][:], full[:], parts[0][:].bitcast(F32), ALU.subtract).then_inc(done, 1)

                def scale_weights(i, s):
                    b_, d, f_ = (stage(i, s, k) for k in "bdf")
                    if b_ and b_.n % GB == 0:
                        if b_.has(1):
                            dve.wait_ge(r_U, b_.count(1))
                        for k in range(KD):
                            ins = dve.tensor_scalar(Win_f[:, k, :], W_raw["in"][:, k, :],
                                                    ca1[:, bass.ds(b_.block(GB), 1), k], None, ALU.mult)
                        ins.then_inc(r_win, 1)
                        dve.wait_ge(r_win, 3 * b_.block(GB) + 1)
                        split(Win, Win_f, r_win, 3 * b_.block(GB) + 1)
                    if d and d.n % GB == 0:
                        if d.has(1):
                            dve.wait_ge(r_O, d.count(1))
                        dve.tensor_tensor(Wout_f[:], W_raw["out"][:],
                                          ga_bc[:, bass.ds(d.block(GB), 1), :].to_broadcast([P, KD, D]),
                                          ALU.mult).then_inc(r_wout, 1)
                        dve.wait_ge(r_wout, 3 * d.block(GB) + 1)
                        split(Wout, Wout_f, r_wout, 3 * d.block(GB) + 1)
                    if f_ and f_.n % GB == 0:
                        if f_.has(1):
                            dve.wait_ge(r_S, f_.count(1))
                        for k in range(KD):
                            ins = dve.tensor_scalar(G_f[:, k, :], G_raw[:, k, :], cb1[:, bass.ds(f_.block(GB), 1), k],
                                                    None, ALU.mult)
                        ins.then_inc(r_g, 1)
                        dve.wait_ge(r_g, 3 * f_.block(GB) + 1)
                        split(G, G_f, r_g, 3 * f_.block(GB) + 1)

                def step(i, s):
                    a, b_, c_, r_, d, e_, f_ = (stage(i, s, k) for k in "abcrdef")
                    if a:
                        dve.wait_ge(r_x[a.n % 4], a.turn(4))
                        if a.has(1):
                            dve.wait_ge(r_st, a.count(2))
                        for t in range(TT):
                            ins = dve.bn_stats(st1[:, t, :], x_buf[a.n % 4][:, t, :])
                        ins.then_inc(r_st, 1)
                        dve.wait_ge(r_st, a.count(2, 1))
                        if a.has(2):
                            dve.wait_ge(r_z1, a.count(1, -1))
                        dve.sem_inc(held[2], 1)
                        for t in range(TT):
                            ins = dve.bn_aggr(mv1[a.n % 2][:, t, :], st1[:, t, :])
                        ins.then_inc(r_st, 1)
                    if b_:
                        dve.wait_ge(r_zh, b_.count(1, 1))
                        dve.tensor_tensor(zT[1][:], psT[:], zT[0][:].bitcast(F32), ALU.subtract).then_inc(r_zl, 1)
                    if r_:
                        dve.wait_ge(r_b, r_.count(1, 1))
                        dve.wait_ge(r_a, r_.count(2, 2))
                        if r_.has(1):
                            dve.wait_ge(r_hs, r_.count(1))
                        if r_.has(2):
                            dve.wait_ge(r_hl, r_.count(1, -1))
                        for m in range(KD):
                            before = 0.0 if r_.n % GB == 0 else hs[(r_.n - 1) % 2][:, m, GT - 1:GT]
                            ins = dve.tensor_tensor_scan(hs[r_.n % 2][:, m, :], a_t[r_.n % 2][:, m, :], b_t[:, m, :],
                                                         before, ALU.mult, ALU.add)
                        ins.then_inc(r_hs, 1)
                    if a:
                        dve.wait_ge(r_rs, a.count(2, 2))
                        if a.has(2):
                            dve.wait_ge(r_zps, a.count(1, -1))
                        dve.sem_inc(held[2], 1)
                        for t in range(TT):
                            ins = dve.tensor_scalar(z1[a.n % 2][:, t, :], x_buf[a.n % 4][:, t, :],
                                                    mv1[a.n % 2][:, t, 0:1], rs1[:, t:t + 1], ALU.subtract, ALU.mult)
                        ins.then_inc(r_z1, 1)
                    if c_:
                        dve.wait_ge(r_tx, c_.count(1, 1))
                        dve.wait_ge(r_uf, c_.count(1, 1))
                        if c_.has(2):
                            dve.wait_ge(r_b, c_.count(1, -1))
                        dve.scalar_tensor_tensor(out=xg[c_.n % 2][:], in0=tx[:], scalar=1.0, in1=u_f[c_.n % 2][:],
                                                 op0=ALU.add, op1=ALU.mult).then_inc(r_xg, 1)
                    if d:
                        dve.wait_ge(r_O, d.count(1, 1))
                        dve.wait_ge(r_xb, d.count(1, 1))
                        if d.has(1):
                            dve.wait_ge(r_x1s, d.count(16))
                            dve.wait_ge(r_z2, d.count(1))
                        dve.tensor_tensor(x1[:], O_tok, xb_buf[d.n % 4][:], ALU.add).then_inc(r_x1, 1)
                        dve.wait_ge(r_x1, d.count(1, 1))
                        for t in range(TT):
                            ins = dve.bn_stats(st2[:, t, :], x1[:, t, :])
                        ins.then_inc(r_st2, 1)
                        dve.wait_ge(r_st2, d.count(2, 1))
                        dve.sem_inc(held[2], 1)
                        for t in range(TT):
                            ins = dve.bn_aggr(mv2[:, t, :], st2[:, t, :])
                        ins.then_inc(r_st2, 1)
                    if c_:
                        dve.wait_ge(r_a, c_.count(2, 1))
                        dve.tensor_scalar(a2_t[c_.n % 2][:], a2_t[c_.n % 2][:], 1.0, -1.0, ALU.min,
                                          ALU.mult).then_inc(r_m, 1)
                    if f_:
                        dve.wait_ge(r_sps, f_.count(1, 1))
                        q = f_.n % GB
                        dve.tensor_copy(scores[:, bass.ds(f_.block(GB), 1), TT * q:TT * (q + 1), :],
                                        psG[:, 0, 0:TT * E].rearrange("p (o t e) -> p o t e", o=1, e=E)).then_inc(r_se, 1)
                    if e_:
                        dve.wait_ge(r_z2h, e_.count(1, 1))
                        if e_.has(1):
                            dve.wait_ge(r_S, e_.count(1))
                        dve.tensor_tensor(z2T[1][:], psT[:], z2T[0][:].bitcast(F32), ALU.subtract).then_inc(r_z2l, 1)
                    if d:
                        dve.wait_ge(r_rs2, d.count(2, 2))
                        if d.has(2):
                            dve.wait_ge(r_z2ps, d.count(1, -1))
                            dve.wait_ge(r_z2s, d.count(16, -16))
                        dve.sem_inc(held[2], 1)
                        for t in range(TT):
                            ins = dve.tensor_scalar(z2[d.n % 2][:, t, :], x1[:, t, :], mv2[:, t, 0:1], rs2[:, t:t + 1],
                                                    ALU.subtract, ALU.mult)
                        ins.then_inc(r_z2, 1)
                    if b_:
                        dve.wait_ge(r_uf, b_.count(1, 1))
                        if b_.has(1):
                            dve.wait_ge(r_A, b_.count(1))
                        split(uT, u_f[b_.n % 2], r_uh, b_.count(2))
                    scale_weights(i, s + 1)

                run_steps(dve, step)

            @block.tensor
            def _(pe):
                def product(out_, stationary, moving):
                    terms = [(k, q) for k in range(KD) for q in PASSES]
                    for j, (k, (qs, qm)) in enumerate(terms):
                        ins = pe.matmul(out_, stationary(qs, k), moving(qm, k), start=(j == 0), stop=(j == len(terms) - 1))
                    return ins

                def cols(w, m):
                    return lambda q, k: w[q][:, k, m * P:(m + 1) * P]

                def whole(t):
                    return lambda q, k: t[q][:, k, :]

                def to_channels(z):
                    for t in range(TT):
                        for k in range(KD):
                            ins = pe.transpose(psT[:, k, t * P:(t + 1) * P], z[:, t, k * P:(k + 1) * P], ident[:])
                    return ins

                def step(i, s):
                    b_, c_, d, e_, f_ = (stage(i, s, k) for k in "bcdef")
                    if b_:
                        pe.wait_ge(r_z1, b_.count(1, 1))
                        if i is not None or s > LAG["e"]:
                            pe.wait_ge(r_z2l, through(i, s, "e"))
                        elif b_.has(1):
                            pe.wait_ge(r_zl, b_.count(1))
                        to_channels(z1[b_.n % 2]).then_inc(r_zps, 1)
                    if f_:
                        pe.wait_ge(r_z2l, f_.count(1, 1))
                        pe.wait_ge(r_g, 3 * f_.block(GB) + 3)
                        pe.wait_ge(r_tx, through(i, s, "c"))
                        if f_.has(1):
                            pe.wait_ge(r_se, f_.count(1))
                        product(psG[0:E, 0, :], whole(G), whole(z2T)).then_inc(r_S, 1)
                    if c_:
                        pe.wait_ge(r_uh, c_.count(2, 2))
                        if c_.has(1):
                            pe.wait_ge(r_tx, c_.count(1))
                        if f_:
                            pe.wait_ge(r_sT, f_.count(1, 1))
                        for m in range(KD):
                            ins = product(psG[:, m, :], cols(Wgx, m), whole(uT))
                        ins.then_inc(r_X, 1)
                        for m in range(KD):
                            ins = product(psU[:, m, :], cols(Wga, m), whole(uT))
                        ins.then_inc(r_A, 1)
                    if d:
                        pe.wait_ge(r_hl, d.count(1, 1))
                        pe.wait_ge(r_wout, 3 * d.block(GB) + 3)
                        if d.has(1):
                            pe.wait_ge(r_x1, d.count(1))
                        for t in range(TT):
                            ins = product(O_tok[:, t, :], cols(hT, t), whole(Wout))
                        ins.then_inc(r_O, 1)
                    if f_:
                        pe.wait_ge(r_sT, f_.count(1, 1))
                        pe.wait_ge(r_tx, through(i, s + 1, "c"))
                        pe.sem_inc(held[4], 1)
                        for t in range(TT):
                            ins = pe.transpose(psG[:, 0, t * E:(t + 1) * E], scoresT[:, t * P:(t + 1) * P], ident[0:E, 0:E])
                        ins.then_inc(r_sps, 1)
                    if e_:
                        pe.wait_ge(r_z2, e_.count(1, 1))
                        pe.wait_ge(r_zl, through(i, s + 1, "b"))
                        if not b_:
                            pe.wait_ge(r_z2l, e_.count(1))
                        to_channels(z2[e_.n % 2]).then_inc(r_z2ps, 1)
                    if b_:
                        pe.wait_ge(r_zl, b_.count(1, 1))
                        pe.wait_ge(r_win, 3 * b_.block(GB) + 3)
                        if c_:
                            pe.wait_ge(r_ta, c_.count(1, 1))
                        for m in range(KD):
                            ins = product(psU[:, m, :], cols(Win, m), whole(zT))
                        ins.then_inc(r_U, 1)

                run_steps(pe, step)
        recur.close()

        NC = B * ST * E
        BITS = 30
        ROUNDS = 5
        VALS = 2
        moe = ExitStack()

        def sbf(name, shape, dt=F32):
            return moe.enter_context(nc.sbuf_tensor(name, shape, dt))

        w1_raw = sbf("w1_raw", [P, KD, H])
        w2_raw = sbf("w2_raw", [P, KH, D])
        w1_s = [[sbf(f"w1_{n}{q}", [P, KD, H], F32R) for q in range(2)] for n in range(2)]
        w2_s = [[sbf(f"w2_{n}{q}", [P, KH, D], F32R) for q in range(2)] for n in range(2)]
        w1_v = w1.rearrange("e (k p) h -> e p k h", p=P)
        w2_v = w2.rearrange("e (k p) d -> e p k d", p=P)
        row_id = sbf("row_id", [P, P], BF16)
        slot_lo_f = sbf("slot_lo_f", [P, B, ST, E])
        vals = sbf("vals", [P, B * ST, E, VALS, CT], BF16)

        def quarter_of(w_s, q):
            raw, parts, half = (w1_raw, w1_s[w_s], q) if q < 2 else (w2_raw, w2_s[w_s], q - 2)
            return raw, parts, slice(half, half + 1) if q < 2 else slice(half * KH // 2, (half + 1) * KH // 2)

        route = ExitStack()

        def sbt(name, shape, dt=F32):
            return route.enter_context(nc.sbuf_tensor(name, shape, dt))

        top = sbt("top", [P, B * ST])
        shifted = sbt("shifted", [P, NC])
        expd = sbt("expd", [P, NC])
        total = sbt("total", [P, B * ST])
        inv = sbt("inv", [P, B * ST])
        probs = sbt("probs", [P, NC])
        probsT = sbt("probsT", [P, B, P])
        rel = sbt("rel", [P, P], I32)
        rel7 = sbt("rel7", [P, P], I32)
        same_e = sbt("same_e", [P, P], BF16)
        before_e = sbt("before_e", [P, P], BF16)
        ct_id = sbt("ct_id", [P, CT])
        tok_id = sbt("tok_id", [P, 1])
        tile_id = sbt("tile_id", [P, NC])
        ones = sbt("ones", [P, P])
        cand = sbt("cand", [P, B], I32)
        bit = sbt("bit", [P, 2])
        over = sbt("over", [P, B])
        flip = sbt("flip", [P, B], I32)
        hit = sbt("hit", [P, B, P], BF16)
        n_hit = sbt("n_hit", [P, B], BF16)
        gt = sbt("gt", [P, B, P])
        eq = sbt("eq", [P, B, P])
        ceq = sbt("ceq", [P, B, P])
        n_eq = sbt("n_eq", [P, B], BF16)
        need = sbt("need", [P, B])
        room = sbt("room", [P, B])
        sel = sbt("sel", [P, B, P])
        csel = sbt("csel", [P, B, P])
        n_sel = sbt("n_sel", [P, B], BF16)
        first_slot = sbt("first_slot", [P, B])
        slot1 = sbt("slot1", [P, B, P])
        slot_i = sbt("slot_i", [P, NC], I32)
        slot_lo = sbt("slot_lo", [P, NC], I32)
        slot_hi = sbt("slot_hi", [P, NC], I32)
        slot_hi_f = sbt("slot_hi_f", [P, NC])
        in_ct = sbt("in_ct", [P, NC, CT], BF16)
        t_pool = sem("route_pool")
        t_step = sem("route_vector_steps")
        t_exp = sem("route_exp")
        t_pT = sem("probsT_in_psum")
        t_cnt = sem("hits_counted")
        t_num = sem("hits_summed")
        t_bit = sem("candidate_steps")
        t_off = sem("offsets_in_psum")
        t_slot = sem("slots_turned")
        t_w = sem("first_weights_loaded")
        t_wh = sem("first_weights_hi")
        t_wl = sem("first_weights_lo")
        t_pz = sem("probs_stored")
        PROBS_KNOWN, COUNTS_DONE, SELECTED, SLOT_KNOWN = 5, 15, 21, 23
        with nc.Block() as block:
            @block.sync
            def _(sp):
                sp.dma_start(w1_raw[:], w1_v[0]).then_inc(t_w, 16)
                sp.dma_start(w2_raw[:], w2_v[0]).then_inc(t_w, 16)
                sp.wait_ge(t_step, PROBS_KNOWN)
                sp.dma_start(z_dram[:, D:].rearrange("(t p) e -> p t e", p=P), probs[:].rearrange("p (t e) -> p t e", e=E),
                             allow_slow_non_contiguous=True).then_inc(t_pz, 16)
                sp.wait_ge(t_pz, 16)

            @block.gpsimd
            def _(pool):
                pool.iota(rel[:], [[1, P]], base=P, channel_multiplier=-1).then_inc(t_pool, 1)
                pool.iota(row_id[:], [[1, P]], base=0, channel_multiplier=0,
                          allow_small_or_imprecise_dtypes=True).then_inc(t_pool, 1)
                pool.iota(ct_id[:], [[1, CT]], base=0, channel_multiplier=0,
                          allow_small_or_imprecise_dtypes=True).then_inc(t_pool, 1)
                pool.iota(tok_id[:], [[1, 1]], base=0, channel_multiplier=1,
                          allow_small_or_imprecise_dtypes=True).then_inc(t_pool, 1)
                pool.iota(tile_id[:], [[P, B * ST], [0, E]], base=0, channel_multiplier=0,
                          allow_small_or_imprecise_dtypes=True).then_inc(t_pool, 1)
                pool.memset(ones[:], 1.0).then_inc(t_pool, 1)
                for q in range(4):
                    raw, parts, at = quarter_of(0, q)
                    pool.wait_ge(t_wh, q + 1)
                    pool.tensor_tensor(parts[1][:, at, :], raw[:, at, :], parts[0][:, at, :].bitcast(F32),
                                       ALU.subtract).then_inc(t_wl, 1)

            @block.scalar
            def _(act):
                act.wait_ge(t_step, 2)
                act.activation(expd[:], shifted[:], ACT.Exp).then_inc(t_exp, 1)
                act.wait_ge(t_w, 32)
                for q in range(4):
                    raw, parts, at = quarter_of(0, q)
                    act.activation(parts[0][:, at, :], raw[:, at, :], ACT.Copy).then_inc(t_wh, 1)

            @block.tensor
            def _(pe):
                pe.wait_ge(t_step, PROBS_KNOWN)
                for b in range(B):
                    ins = pe.transpose(psum[0][:, 0, b * P:(b + 1) * P], probs[:, b * P:(b + 1) * P], ident[:])
                ins.then_inc(t_pT, 1)
                def count_hits(j, n):
                    r = Nth(j, n, ROUNDS)
                    pe.wait_ge(t_cnt, r.count(1, 1))
                    pe.matmul(psum[1][:, 0, 0:B], same_e[:], n_hit[:], start=True, stop=True).then_inc(t_num, 1)

                with pe.Fori(0, BITS // ROUNDS) as j:
                    for n in range(ROUNDS):
                        count_hits(j, n)
                pe.wait_ge(t_step, COUNTS_DONE)
                pe.matmul(psum[1][:, 1, 0:B], same_e[:], n_hit[:], start=True, stop=True)
                pe.matmul(psum[1][:, 1, B:2 * B], before_e[:], n_eq[:], start=True, stop=True).then_inc(t_off, 1)
                pe.wait_ge(t_step, SELECTED)
                pe.matmul(psum[1][:, 1, 2 * B:3 * B], before_e[:], n_sel[:], start=True, stop=True).then_inc(t_off, 1)
                pe.wait_ge(t_step, SLOT_KNOWN)
                for b in range(B):
                    ins = pe.transpose(psum[0][:, 1, b * P:(b + 1) * P], slot1[:, b, :], ident[:])
                ins.then_inc(t_slot, 1)

            @block.vector
            def _(dve):
                n_step = [0]

                def step(ins):
                    ins.then_inc(t_step, 1)
                    n_step[0] += 1
                    dve.wait_ge(t_step, n_step[0])

                sc = scores[:].rearrange("p b t e -> p (b t) e")
                sh = shifted[:].rearrange("p (t e) -> p t e", e=E)
                ex = expd[:].rearrange("p (t e) -> p t e", e=E)
                step(dve.tensor_reduce(top[:], sc, AX.X, ALU.max))
                step(dve.tensor_tensor(sh, sc, top[:].unsqueeze(2).to_broadcast([P, B * ST, E]), ALU.subtract))
                dve.wait_ge(t_exp, 1)
                step(dve.tensor_reduce(total[:], ex, AX.X, ALU.add))
                step(dve.reciprocal(inv[:], total[:]))
                step(dve.tensor_tensor(probs[:].rearrange("p (t e) -> p t e", e=E), ex,
                                       inv[:].unsqueeze(2).to_broadcast([P, B * ST, E]), ALU.mult))
                dve.wait_ge(t_pool, 6)
                step(dve.tensor_scalar(rel7[:], rel[:], E - 1, None, ALU.bitwise_and))
                step(dve.tensor_scalar(same_e[:], rel7[:], 0, None, ALU.is_equal))
                step(dve.scalar_tensor_tensor(out=before_e[:], in0=rel[:], scalar=float(P), in1=same_e[:],
                                              op0=ALU.is_gt, op1=ALU.mult))
                step(dve.memset(cand[:], 1 << (BITS - 1)))
                step(dve.memset(bit[:, 0:1], float(1 << (BITS - 1))))
                step(dve.memset(bit[:, 1:2], float(1 << (BITS - 2))))
                dve.wait_ge(t_pT, 1)
                step(dve.tensor_copy(probsT[:], psum[0][:, 0, :].rearrange("p (b t) -> p b t", b=B)))
                cand_f = cand[:].bitcast(F32)

                def search(j, n):
                    r = Nth(j, n, ROUNDS)
                    for b in range(B):
                        ins = dve.tensor_scalar(hit[:, b, :], probsT[:, b, :], cand_f[:, b:b + 1], None, ALU.is_ge,
                                                ALU.add, accum_out=n_hit[:, b:b + 1])
                    ins.then_inc(t_cnt, 1)
                    dve.wait_ge(t_num, r.count(1, 1))
                    dve.tensor_scalar(over[:], psum[1][:, 0, 0:B], float(CAPK), bit[:, 0:1], ALU.is_lt,
                                      ALU.mult).then_inc(t_bit, 1)
                    dve.wait_ge(t_bit, r.count(4, 1))
                    if j is None and n == BITS - 1:
                        dve.tensor_copy(flip[:], over[:]).then_inc(t_bit, 1)
                    else:
                        dve.tensor_scalar(flip[:], over[:], bit[:, 1:2], None, ALU.add).then_inc(t_bit, 1)
                    dve.wait_ge(t_bit, r.count(4, 2))
                    dve.tensor_tensor(cand[:], cand[:], flip[:], ALU.bitwise_xor).then_inc(t_bit, 1)
                    dve.tensor_scalar(bit[:], bit[:], 0.5, None, ALU.mult).then_inc(t_bit, 1)
                    dve.wait_ge(t_bit, r.count(4, 4))

                with dve.Fori(0, BITS // ROUNDS - 1) as j:
                    for n in range(ROUNDS):
                        search(j, n)
                for n in range(BITS - ROUNDS, BITS):
                    search(None, n)
                for b in range(B):
                    dve.tensor_scalar(gt[:, b, :], probsT[:, b, :], cand_f[:, b:b + 1], None, ALU.is_gt, ALU.add,
                                            accum_out=n_hit[:, b:b + 1])
                    eq_last = dve.tensor_scalar(eq[:, b, :], probsT[:, b, :], cand_f[:, b:b + 1], None, ALU.is_equal)
                step(eq_last)
                for b in range(B):
                    ins = dve.tensor_tensor_scan(ceq[:, b, :], ones[:], eq[:, b, :], 0.0, ALU.mult, ALU.add)
                step(ins)
                step(dve.tensor_copy(n_eq[:], ceq[:, :, P - 1]))
                assert n_step[0] == COUNTS_DONE
                dve.wait_ge(t_off, 1)
                step(dve.tensor_scalar(need[:], psum[1][:, 1, 0:B], -1.0, float(CAPK), ALU.mult, ALU.add))
                step(dve.tensor_tensor(room[:], need[:], psum[1][:, 1, B:2 * B], ALU.subtract))
                for b in range(B):
                    ins = dve.scalar_tensor_tensor(out=sel[:, b, :], in0=ceq[:, b, :], scalar=room[:, b:b + 1],
                                                   in1=eq[:, b, :], op0=ALU.is_le, op1=ALU.mult)
                step(ins)
                step(dve.tensor_tensor(sel[:], sel[:], gt[:], ALU.add))
                for b in range(B):
                    ins = dve.tensor_tensor_scan(csel[:, b, :], ones[:], sel[:, b, :], 0.0, ALU.mult, ALU.add)
                step(ins)
                step(dve.tensor_copy(n_sel[:], csel[:, :, P - 1]))
                assert n_step[0] == SELECTED
                dve.wait_ge(t_off, 2)
                step(dve.tensor_copy(first_slot[:], psum[1][:, 1, 2 * B:3 * B]))
                for b in range(B):
                    ins = dve.scalar_tensor_tensor(out=slot1[:, b, :], in0=csel[:, b, :], scalar=first_slot[:, b:b + 1],
                                                   in1=sel[:, b, :], op0=ALU.add, op1=ALU.mult)
                step(ins)
                assert n_step[0] == SLOT_KNOWN
                dve.wait_ge(t_slot, 1)
                step(dve.tensor_scalar(slot_i[:], psum[0][:, 1, :], -1.0, None, ALU.add))
                step(dve.tensor_scalar(slot_lo[:], slot_i[:], P - 1, None, ALU.bitwise_and))
                step(dve.tensor_copy(slot_lo_f[:].rearrange("p b t e -> p (b t e)"), slot_lo[:]))
                step(dve.tensor_scalar(slot_hi[:], slot_i[:], P.bit_length() - 1, None, ALU.arith_shift_right))
                step(dve.tensor_copy(slot_hi_f[:], slot_hi[:]))
                step(dve.tensor_tensor(in_ct[:], slot_hi_f[:].unsqueeze(2).to_broadcast([P, NC, CT]),
                                       ct_id[:].unsqueeze(1).to_broadcast([P, NC, CT]), ALU.is_equal))
                ids = vals[:].rearrange("p t e v c -> p (t e) v c")
                step(dve.tensor_scalar(ids[:, :, 0, :], in_ct[:], tok_id[:, 0:1], None, ALU.mult))
                step(dve.tensor_tensor(ids[:, :, 1, :], in_ct[:], tile_id[:].unsqueeze(2).to_broadcast([P, NC, CT]),
                                       ALU.mult))
        route.close()
        BODY = 2 * B
        PASSES_F = E // 2
        HC = H // KD
        idx_cur = [sbf(f"idx_cur{n}", [P, B, CT], I32) for n in range(2)]
        g_cur = [sbf(f"g_cur{n}", [P, CT, 1]) for n in range(2)]
        slot_u = [sbf(f"slot_u{n}", [P, ST, 1]) for n in range(2)]
        vals_u = [sbf(f"vals_u{n}", [P, ST, 1, VALS * CT], BF16) for n in range(2)]
        place = [sbf(f"place{n}", [P, ST, P], BF16) for n in range(2)]
        lists = [sbf(f"lists{n}", [P, VALS, CT]) for n in range(2)]
        rows_in = [sbf(f"rows_in{n}", [P, CT, D + E]) for n in range(2)]
        xf = sbf("xf", [P, KD, CAPK])
        xT = [sbf(f"xT{q}", [P, KD, CAPK], F32R) for q in range(2)]
        HF = 4
        hf = [sbf(f"hf{n}", [P, CAPK]) for n in range(HF)]
        hidT = [sbf(f"hidT{q}", [P, KH, CAPK], F32R) for q in range(2)]
        rows_y = [sbf(f"rows_y{n}", [P, CT, D]) for n in range(2)]

        f_w1 = sem("w1_loaded")
        f_w2 = sem("w2_loaded")
        f_ws = sem("weights_split")
        f_se = sem("unit_slots_ready")
        f_pl = sem("place_ready")
        f_lm = sem("list_in_psum")
        f_lc = sem("list_copied")
        f_idx = sem("idx_cur_ready")
        f_g = sem("g_cur_ready")
        f_in = [sem(f"rows_gathered{n}") for n in range(2)]
        f_T = sem("rows_turned")
        f_xf = sem("xf_ready")
        f_x = sem("xT_split")
        f_H = sem("hidden_in_psum")
        f_hf = sem("hidden_ready")
        f_hh = sem("hidT_hi_ready")
        f_hl = sem("hidT_lo_ready")
        f_Y = sem("y_in_psum")
        f_y = sem("rows_y_ready")
        f_add = [sem(f"rows_added{b}") for b in range(B)]

        psT, psH0, psH1, psY = psum
        H_bank = [psH0[:, 0, :], psH0[:, 1, :], psH1[:, 0, :], psH1[:, 1, :]]
        Y_tok = psY[:].rearrange("p h (q d) -> p (h q) d", d=D)

        LISTED = 2

        def list_psum(v):
            in_prologue = v.i is None and v.n < LISTED
            return psY[:, 0, 8 * v.n:8 * v.n + VALS * CT] if in_prologue else psT[:, 0, 0:VALS * CT]

        def listed(i, j):
            return Nth(i, j + LISTED, BODY) if i is not None or j + LISTED < E * B else None

        def run_units(eng, step):
            for j in range(BODY):
                step(None, j)
            with eng.Fori(1, PASSES_F - 1) as i:
                for j in range(BODY):
                    step(i, j)
            for j in range((PASSES_F - 1) * BODY, PASSES_F * BODY):
                step(None, j)

        with nc.Block() as block:
            @block.sync
            def _(sp):
                def load(e):
                    if e.has(2):
                        sp.wait_ge(f_ws, e.count(8, -12))
                    sp.dma_start(w1_raw[:], w1_v[bass.ds(e.count(1), 1)].rearrange("o p k h -> p (o k) h")).then_inc(f_w1, 16)
                    if e.has(2):
                        sp.wait_ge(f_ws, e.count(8, -8))
                    sp.dma_start(w2_raw[:], w2_v[bass.ds(e.count(1), 1)].rearrange("o p k d -> p (o k) d")).then_inc(f_w2, 16)
                load(Nth(None, 1, 1))
                with sp.Fori(2, E) as i:
                    load(Nth(i, 0, 1))

            @block.gpsimd
            def _(pool):
                def fetch(u):
                    n = (u.n // B) % 2
                    pool.wait_ge(f_idx, u.count(1, 1))
                    if u.has(2):
                        pool.wait_ge(f_T, u.count(1, -1))
                        pool.wait_ge(f_g, u.count(1, -1))
                    pool.sem_inc(held[0], 1)
                    for t in range(CT):
                        pool.indirect_dma_start(rows_in[u.n % 2][:, t, :], None, z_dram,
                                                bass.IndirectOffsetOnAxis(ap=idx_cur[n][:, u.n % B, t:t + 1], axis=0))\
                            .then_inc(f_in[u.n % 2], 16)

                def add(u):
                    n, b = (u.n // B) % 2, u.n % B
                    pool.wait_ge(f_y, u.count(2, 2))
                    if u.has(B):
                        pool.wait_ge(f_add[b], 16 * CT * u.block(B))
                    pool.sem_inc(held[0], 1)
                    for t in range(CT):
                        pool.indirect_dma_start(acc_dram, bass.IndirectOffsetOnAxis(ap=idx_cur[n][:, b, t:t + 1], axis=0),
                                                rows_y[u.n % 2][:, t, :], None, compute_op=ALU.add).then_inc(f_add[b], 16)

                def step(i, j):
                    if i is not None or j + 1 < E * B:
                        fetch(Nth(i, j + 1, BODY))
                    if i is not None or j >= 1:
                        add(Nth(i, j - 1, BODY))
                fetch(Nth(None, 0, BODY))
                run_units(pool, step)
                add(Nth(None, E * B - 1, BODY))
                for b in range(B):
                    pool.wait_ge(f_add[b], 16 * CT * E)

            @block.scalar
            def _(act):
                def weigh(u):
                    act.wait_ge(f_g, u.count(1, 1))
                    for h in range(2):
                        act.wait_ge(f_Y, u.count(2, h + 1))
                        if h == 0 and u.has(2):
                            v = Nth(u.i, u.n - 2, BODY)
                            act.wait_ge(f_add[v.n % B], 16 * CT * (v.block(B) + 1))
                        for t in range(2 * h, 2 * h + 2):
                            ins = act.activation(rows_y[u.n % 2][:, t, :], Y_tok[:, t, :], ACT.Copy,
                                                 scale=g_cur[u.n % 2][:, t, 0:1])
                        ins.then_inc(f_y, 1)

                def step(i, j):
                    u = Nth(i, j, BODY)
                    act.wait_ge(f_T, u.count(1, 1))
                    if u.has(1):
                        act.wait_ge(f_x, u.count(2))
                    for k in range(KD):
                        ins = act.activation(xf[:, k, :], psT[:, k, :], ACT.Identity, bias=sbc[:, j % B, k:k + 1],
                                             scale=cb1[:, j % B, k:k + 1])
                    ins.then_inc(f_xf, 1)
                    if u.has(1):
                        weigh(Nth(i, j - 1, BODY))
                    for m in range(KH):
                        act.wait_ge(f_H, u.count(KH, m + 1))
                        if u.has(1) or m >= HF:
                            act.wait_ge(f_hl, u.count(KH, m + 1 - HF))
                        act.activation(hf[m % HF][:], H_bank[m % 4], ACT.Gelu_apprx_tanh).then_inc(f_hf, 1)
                run_units(act, step)
                weigh(Nth(None, E * B - 1, BODY))

            @block.vector
            def _(dve):
                def split_chunk(e, n, q):
                    raw, parts, at = quarter_of(n, q)
                    dve.wait_ge(f_w1 if q < 2 else f_w2, 16 * e)
                    dve.tensor_copy(parts[0][:, at, :], raw[:, at, :]).then_inc(f_ws, 1)
                    dve.wait_ge(f_ws, 8 * e + (2 * q + 1 - 8))
                    dve.tensor_tensor(parts[1][:, at, :], raw[:, at, :], parts[0][:, at, :].bitcast(F32),
                                      ALU.subtract).then_inc(f_ws, 1)

                def one_hots(v):
                    b, n, e = v.n % B, v.n % 2, bass.ds(v.block(B), 1)
                    if v.has(2):
                        dve.wait_ge(f_lm, v.count(1, -1))
                    dve.sem_inc(held[2], 1)
                    dve.tensor_copy(slot_u[n][:], slot_lo_f[:, b, :, e]).then_inc(f_se, 1)
                    dve.tensor_copy(vals_u[n][:], vals[:, b * ST:(b + 1) * ST, e, :, :]
                                    .rearrange("p t o v c -> p t o (v c)")).then_inc(f_se, 1)
                    dve.wait_ge(f_se, v.count(2, 2))
                    for t in range(ST):
                        ins = dve.tensor_scalar(place[n][:, t, :], row_id[:], slot_u[n][:, t, 0:1], None, ALU.is_equal)
                    ins.then_inc(f_pl, 1)

                def keep_list(v):
                    b, n = v.n % B, v.n % 2
                    dve.wait_ge(f_lm, v.count(1, 1))
                    if v.has(2):
                        dve.wait_ge(f_idx, v.count(1, -1))
                    dve.tensor_copy(lists[n][:], list_psum(v).rearrange("p (v c) -> p v c", v=VALS)).then_inc(f_lc, 1)
                    dve.wait_ge(f_lc, v.count(1, 1))
                    if v.has(2 * B):
                        dve.wait_ge(f_add[b], 16 * CT * (v.block(B) - 1))
                    dve.tensor_tensor(idx_cur[(v.n // B) % 2][:, b, :], lists[n][:, 0, :], lists[n][:, 1, :],
                                      ALU.add).then_inc(f_idx, 1)

                def step(i, j):
                    u = Nth(i, j, BODY)
                    dve.wait_ge(f_xf, u.count(1, 1))
                    if u.has(1):
                        dve.wait_ge(f_H, u.count(KH))
                    dve.tensor_copy(xT[0][:], xf[:]).then_inc(f_x, 1)
                    dve.wait_ge(f_x, u.count(2, 1))
                    dve.tensor_tensor(xT[1][:], xf[:], xT[0][:].bitcast(F32), ALU.subtract).then_inc(f_x, 1)
                    if u.has(2):
                        dve.wait_ge(f_y, u.count(2, -2))
                    dve.sem_inc(held[2], 1)
                    dve.tensor_copy(g_cur[u.n % 2][:], rows_in[u.n % 2][:, :, bass.ds(u.block(B) + D, 1)]).then_inc(f_g, 1)
                    v = listed(i, j)
                    if v:
                        one_hots(v)
                    for m in range(KH):
                        dve.wait_ge(f_hf, u.count(KH, m + 1))
                        if m == 0 and u.has(1):
                            dve.wait_ge(f_Y, u.count(2))
                        dve.tensor_copy(hidT[0][:, m, :], hf[m % HF][:]).then_inc(f_hh, 1)
                        dve.wait_ge(f_hh, u.count(KH, m + 1))
                        dve.tensor_tensor(hidT[1][:, m, :], hf[m % HF][:], hidT[0][:, m, :].bitcast(F32),
                                          ALU.subtract).then_inc(f_hl, 1)
                        if m == 2 and v:
                            keep_list(v)
                        if m == 3 and (i is not None or j // B + 1 < E):
                            split_chunk(u.block(B) + 1, (j // B + 1) % 2, j % B)
                for n in range(LISTED):
                    one_hots(Nth(None, n, BODY))
                    keep_list(Nth(None, n, BODY))
                run_units(dve, step)

            @block.tensor
            def _(pe):
                def turn(u):
                    pe.wait_ge(f_in[u.n % 2], u.turn(2, 16 * CT))
                    if u.has(1):
                        pe.wait_ge(f_xf, u.count(1))
                        if listed(u.i, u.n - 1):
                            pe.wait_ge(f_lc, u.count(1, LISTED))
                    for t in range(CT):
                        for k in range(KD):
                            ins = pe.transpose(psT[:, k, t * P:(t + 1) * P], rows_in[u.n % 2][:, t, k * P:(k + 1) * P],
                                               ident[:])
                    ins.then_inc(f_T, 1)

                def make_list(v):
                    pe.wait_ge(f_pl, v.count(1, 1))
                    for t in range(ST):
                        ins = pe.matmul(list_psum(v), place[v.n % 2][:, t, :], vals_u[v.n % 2][:, t, 0, :],
                                        start=(t == 0), stop=(t == ST - 1))
                    ins.then_inc(f_lm, 1)

                def layer2(u):
                    n = (u.n // B) % 2
                    if u.has(B):
                        pe.wait_ge(f_ws, 8 * u.block(B))
                    for t in range(CT):
                        if t % 2 == 0 and u.has(1):
                            pe.wait_ge(f_y, u.count(2, t // 2 - 1))
                        terms = [(k, q) for k in range(KH) for q in PASSES]
                        for x_, (k, (qs, qm)) in enumerate(terms):
                            if t == 0 and x_ % len(PASSES) == 0:
                                pe.wait_ge(f_hl, u.count(KH, k + 1))
                            ins = pe.matmul(Y_tok[:, t, :], hidT[qs][:, k, t * P:(t + 1) * P], w2_s[n][qm][:, k, :],
                                            start=(x_ == 0), stop=(x_ == len(terms) - 1))
                        if t % 2 == 1:
                            ins.then_inc(f_Y, 1)

                def layer1(u, v):
                    n = (u.n // B) % 2
                    pe.wait_ge(f_x, u.count(2, 2))
                    if u.has(B):
                        pe.wait_ge(f_ws, 8 * u.block(B) - 4)
                    for m in range(KH):
                        if v and m == 2:
                            make_list(v)
                        if u.has(1) or m >= 4:
                            pe.wait_ge(f_hf, u.count(KH, m + 1 - 4))
                        terms = [(k, q) for k in range(KD) for q in PASSES]
                        for x_, (k, (qs, qm)) in enumerate(terms):
                            ins = pe.matmul(H_bank[m % 4], w1_s[n][qs][:, k, m * P:(m + 1) * P], xT[qm][:, k, :],
                                            start=(x_ == 0), stop=(x_ == len(terms) - 1))
                        ins.then_inc(f_H, 1)

                def step(i, j):
                    u = Nth(i, j, BODY)
                    turn(u)
                    if u.has(1):
                        layer2(Nth(i, j - 1, BODY))
                    layer1(u, listed(i, j))
                for n in range(LISTED):
                    make_list(Nth(None, n, BODY))
                run_units(pe, step)
                layer2(Nth(None, E * B - 1, BODY))
        moe.close()

        fin = ExitStack()

        def sbz(name, shape, dt=F32):
            return fin.enter_context(nc.sbuf_tensor(name, shape, dt))

        acc_t = [sbz(f"acc_t{n}", [P, TT, D]) for n in range(4)]
        res_t = [sbz(f"res_t{n}", [P, TT, D]) for n in range(4)]
        acc16 = [sbz(f"acc16_{n}", [P, TT, D], BF16) for n in range(4)]
        prod = [sbz(f"prod{n}", [P, TT, D]) for n in range(4)]
        o_acc = [sem(f"acc_loaded{n}") for n in range(4)]
        o_x1 = [sem(f"x1_loaded{n}") for n in range(4)]
        o_16 = sem("acc16_ready")
        o_p = sem("gated_ready")
        o_r = sem("result_ready")
        o_out = [sem(f"out_stored{n}") for n in range(4)]

        def run_groups(eng, step):
            for s in range(GB):
                step(Nth(None, s, GB))
            with eng.Fori(1, B) as i:
                for s in range(GB):
                    step(Nth(i, s, GB))

        with nc.Block() as block:
            @block.sync
            def _(sp):
                def step(g):
                    n = g.n % 4
                    if g.has(4):
                        sp.wait_ge(o_16, g.count(1, -3))
                        sp.sem_inc(held[3], 1)
                        sp.wait_ge(o_out[n], g.turn(4, 16) - 16)
                    sp.dma_start(acc_t[n][:], rows(acc_dram, g.count(GT))).then_inc(o_acc[n], 16)
                    sp.dma_start(res_t[n][:], rows(x1_dram, g.count(GT))).then_inc(o_x1[n], 16)
                run_groups(sp, step)

            @block.vector
            def _(dve):
                def step(g):
                    n = g.n % 4
                    dve.wait_ge(o_acc[n], g.turn(4))
                    if g.has(4):
                        dve.wait_ge(o_p, g.count(1, -3))
                    dve.tensor_copy(acc16[n][:], acc_t[n][:]).then_inc(o_16, 1)
                    if g.has(1):
                        finish(Nth(g.i, g.n - 1, GB))

                def finish(g):
                    n = g.n % 4
                    dve.wait_ge(o_p, g.count(1, 1))
                    dve.wait_ge(o_x1[n], g.turn(4))
                    dve.tensor_tensor(res_t[n][:], prod[n][:], res_t[n][:], ALU.add).then_inc(o_r, 1)
                run_groups(dve, step)
                finish(Nth(None, NG - 1, GB))

            @block.gpsimd
            def _(pool):
                def step(g):
                    n = g.n % 4
                    pool.wait_ge(o_16, g.count(1, 1))
                    if g.has(4):
                        pool.wait_ge(o_r, g.count(1, -3))
                    pool.sem_inc(held[0], 1)
                    pool.tensor_tensor(prod[n][:], acc16[n][:], gb_bc[:, bass.ds(g.block(GB), 1), :]
                                       .to_broadcast([P, TT, D]), ALU.mult).then_inc(o_p, 1)
                run_groups(pool, step)

            @block.scalar
            def _(act):
                def step(g):
                    act.wait_ge(o_r, g.count(1, 1))
                    act.dma_start(rows(out_rows, g.count(GT)), res_t[g.n % 4][:]).then_inc(o_out[g.n % 4], 16)
                run_groups(act, step)
                for n in range(4):
                    act.wait_ge(o_out[n], 16 * B)
        fin.close()


_INS = ["L0_attn_x", "L0_attn_W_in", "L0_attn_b_in", "L0_attn_W_gx", "L0_attn_b_gx", "L0_attn_W_ga", "L0_attn_b_ga",
        "L0_attn_a_param", "L0_attn_W_out", "L0_attn_b_out", "L0_ffn_gate_w", "L0_ffn_w1", "L0_ffn_w2", "L0_c", "L0_wmod"]


def kernel(**inputs):
    import numpy as _np
    import concourse.bacc as _bacc
    from concourse import mybir as _mybir
    from concourse.bass_utils import run_bass_kernel_spmd as _run

    nc = _bacc.Bacc("TRN2", target_bir_lowering=False, num_devices=1)
    arrays, args = {}, []
    for name in _INS:
        a = _np.ascontiguousarray(inputs[name])
        arrays[f"in_{name}"] = a
        args.append(nc.dram_tensor(f"in_{name}", a.shape, _mybir.dt.from_np(a.dtype), kind="ExternalInput").ap())
    shape = arrays["in_L0_attn_x"].shape
    args.append(nc.dram_tensor("out_x", shape, _mybir.dt.float32, kind="ExternalOutput").ap())
    adaln_kernel(nc, *args)
    r = _run(nc, [arrays], core_ids=[0])
    return r.results[0]["out_x"]
```

```python
from contextlib import ExitStack

import concourse.bass as bass
from concourse import mybir

F32 = mybir.dt.float32
F32R = mybir.dt.float32r
BF16 = mybir.dt.bfloat16
I32 = mybir.dt.int32
ALU = mybir.AluOpType
ACT = mybir.ActivationFunctionType
AX = mybir.AxisListType

P = 128
EPS = 1e-5
GATE_C = 8.0
MOD_MIN = 0.25
CAP = 2
PASSES = ((0, 0), (0, 1), (1, 0))


class Nth:

    def __init__(self, i, n, span):
        self.i, self.n, self.span = i, n, span

    def count(self, per, k=0):
        v = per * self.n + k
        return v if self.i is None else (per * self.span) * self.i + v

    def turn(self, slots, per=16):
        v = per * (self.n // slots + 1)
        return v if self.i is None else (per * self.span // slots) * self.i + v

    def block(self, size):
        v = self.n // size
        return v if self.i is None else (self.span // size) * self.i + v

    def has(self, back):
        return self.i is not None or self.n >= back


def adaln_kernel(nc, x, W_in, b_in, W_gx, b_gx, W_ga, b_ga, a_param, W_out, b_out, gate_w, w1, w2, c, wmod, out):
    B, S, D = x.shape
    E, _, H = w1.shape
    KD = D // P
    KH = H // P
    TOK = B * S
    GT = 512
    TT = GT // P
    NG = TOK // GT
    GB = S // GT
    ST = S // P
    CAPK = CAP * S // E
    CT = CAPK // P
    NMOD = 6
    assert D == 256 and CAPK == GT and ST * E == P and B == 4 and GB == 4

    z_dram = nc.dram_tensor("z_rows", (TOK, D + E), F32, kind="Internal").ap()
    x1_dram = nc.dram_tensor("x1_rows", (TOK, D), F32, kind="Internal").ap()
    acc_dram = nc.dram_tensor("ffn_rows", (TOK, D), F32, kind="Internal").ap()
    x_rows = x.rearrange("b s d -> (b s) d")
    out_rows = out.rearrange("b s d -> (b s) d")

    def rows(dram, first):
        return dram[bass.ds(first, GT), :].rearrange("(t p) d -> p t d", p=P)

    def runs(dram, first):
        return dram[bass.ds(first, GT), :].rearrange("(p t) d -> p t d", p=P)

    keep = ExitStack()
    with keep:
        def sbk(name, shape, dt=F32):
            return keep.enter_context(nc.sbuf_tensor(name, shape, dt))

        def sem(name):
            return keep.enter_context(nc.semaphore(name))

        held = [sem(f"waited_{n}") for n in ("pool", "act", "dve", "sp", "pe")]
        psum = [keep.enter_context(nc.psum_tensor(f"psum{n}", [P, 2, 512], F32)) for n in range(4)]

        ident = sbk("ident", [P, P])
        gb_bc = sbk("gb_bc", [P, B, D])
        cb1 = sbk("cb1", [P, B, KD])
        sbc = sbk("sbc", [P, B, KD])
        scores = sbk("scores", [P, B, ST, E])

        LAG = dict(a=0, b=1, c=2, r=3, d=4, e=5, f=7)
        PEELED = LAG["f"]
        LOOPS = (NG - PEELED) // GB

        recur = ExitStack()

        def sbr(name, shape, dt=F32):
            return recur.enter_context(nc.sbuf_tensor(name, shape, dt))

        W_raw = {n: sbr(f"{n}_raw", [P, KD, D]) for n in ("in", "gx", "ga", "out")}
        G_raw = sbr("G_raw", [P, KD, E])
        Wgx = [sbr(f"Wgx{q}", [P, KD, D], F32R) for q in range(2)]
        Wga = [sbr(f"Wga{q}", [P, KD, D], F32R) for q in range(2)]
        ga_bc = sbr("ga_bc", [P, B, D])
        bias_bc = sbr("bias_bc", [P, B, D])
        ca1 = sbr("ca1", [P, B, KD])
        bias_u = sbr("bias_u", [P, B, KD])
        bias_s = sbr("bias_s", [E, B])
        half_bgx = sbr("half_bgx", [P, KD])
        half_bga = sbr("half_bga", [P, KD])
        decay = sbr("decay", [P, KD])
        decay2 = sbr("decay2", [P, KD])
        mhalf = sbr("mhalf", [P, TT])
        quarter = sbr("quarter", [P, 1])

        x_buf = [sbr(f"x_buf{n}", [P, TT, D]) for n in range(4)]
        ZERO = TOK * D // P // (PEELED + 1)
        zero_row = sbr("zero_row", [P, ZERO])
        r_x = [sem(f"x_loaded{n}") for n in range(4)]

        su = ExitStack()

        def sbs(name, shape, dt=F32):
            return su.enter_context(nc.sbuf_tensor(name, shape, dt))

        wmod_sb = sbs("wmod_sb", [P, KD, NMOD * D])
        cT = sbs("cT", [P, KD, B])
        silu_c = sbs("silu_c", [P, KD, B])
        silu_bc = sbs("silu_bc", [P, KD, B, P])
        sa = sbs("sa", [P, B, KD])
        bcol = {n: sbs(f"{n}_col", [P, KD]) for n in ("in", "gx", "ga", "a")}
        bout_bc = sbs("bout_bc", [P, D])
        ap = {n: sbs(f"sp_{n}", [P, KD]) for n in ("neg", "abs", "exp", "u", "ln", "um", "zero", "num", "den", "rec", "l1", "sp")}
        gtmp = {n: sbs(f"gm_{n}", [P, B, D]) for n in ("sign", "neg", "mag")}

        s_c = sem("c_loaded")
        s_wmod = sem("wmod_loaded")
        s_w = sem("weights_loaded")
        s_b = sem("biases_loaded")
        s_silu = sem("silu_ready")
        s_chain = sem("setup_vector_steps")
        s_exp = sem("setup_exp_ready")
        s_mod = sem("mod_products")
        s_row = sem("mod_rows")
        s_gb = sem("gb_copied")
        s_one = sem("setup_pool")
        s_zero = sem("acc_zeroed")

        SILU_SPREAD, EXP_PLUS_1, MODS_KEPT = 1, 6, 26
        with nc.Block() as block:
            @block.sync
            def _(sp):
                for k in range(KD):
                    sp.dma_start(cT[:, k, :], c[:, k * P:(k + 1) * P].rearrange("b p -> p b"),
                                 allow_slow_non_contiguous=True).then_inc(s_c, 16)
                for k in range(KD):
                    sp.dma_start(wmod_sb[:, k, :], wmod[k * P:(k + 1) * P, :]).then_inc(s_wmod, 16)
                sp.dma_start(x_buf[0][:], rows(x_rows, 0)).then_inc(r_x[0], 16)
                sp.dma_start(bout_bc[:], b_out.rearrange("(o n) -> o n", o=1).to_broadcast([P, D])).then_inc(s_b, 16)
                sp.dma_start(W_raw["out"][:], W_out.rearrange("(k p) n -> p k n", p=P)).then_inc(s_w, 16)
                sp.dma_start(G_raw[:], gate_w.rearrange("(k p) n -> p k n", p=P)).then_inc(s_w, 16)
                sp.wait_ge(s_w, 16 * 5)

            @block.gpsimd
            def _(pool):
                pool.memset(zero_row[:], 0.0).then_inc(s_one, 1)
                pool.memset(mhalf[:], -0.5).then_inc(s_one, 1)
                pool.memset(quarter[:], 0.25).then_inc(s_one, 1)
                pool.memset(ident[:], 0.0).then_inc(s_one, 1)
                pool.wait_ge(s_one, 4)
                pool.affine_select(out=ident[:], in_=ident[:], compare_op=ALU.not_equal, fill=1.0, base=0,
                                   pattern=[[-1, P]], channel_multiplier=1).then_inc(s_one, 1)

            @block.scalar
            def _(act):
                for n, v in (("a", a_param), ("in", b_in), ("gx", b_gx), ("ga", b_ga)):
                    act.dma_start(bcol[n][:], v.rearrange("(k p) -> p k", p=P), allow_slow_non_contiguous=True).then_inc(s_b, 16)
                for n, w in (("gx", W_gx), ("ga", W_ga), ("in", W_in)):
                    act.dma_start(W_raw[n][:], w.rearrange("(k p) n -> p k n", p=P)).then_inc(s_w, 16)
                act.wait_ge(s_c, 16 * KD)
                act.activation(silu_c[:], cT[:], ACT.Silu).then_inc(s_silu, 1)
                act.wait_ge(s_chain, SILU_SPREAD + 2)
                act.activation(ap["exp"][:], ap["abs"][:], ACT.Exp, scale=-1.0).then_inc(s_exp, 1)
                act.wait_ge(s_chain, EXP_PLUS_1)
                act.activation(ap["ln"][:], ap["u"][:], ACT.Ln).then_inc(s_exp, 1)
                act.wait_ge(s_row, 2)
                act.activation(gb_bc[:], psum[2][:].rearrange("p h (q d) -> p (h q) d", d=D), ACT.Copy).then_inc(s_gb, 1)
                act.wait_ge(s_gb, 1)

            @block.tensor
            def _(pe):
                pe.wait_ge(s_wmod, 16 * KD)
                pe.wait_ge(s_silu, 1)
                def on_all_partitions(n, part):
                    for b in range(B):
                        for k in range(KD):
                            last = pe.matmul(psum[n][:, b // 2, (b % 2) * D:(b % 2 + 1) * D], silu_bc[:, k, b, :],
                                             wmod_sb[:, k, part * D:(part + 1) * D], start=(k == 0), stop=(k == KD - 1))
                    last.then_inc(s_row, 1)

                pe.wait_ge(s_chain, SILU_SPREAD)
                on_all_partitions(1, 2)
                cols = psum[0][:, 0, 0:8 * B].rearrange("p (j m b) -> p j m b", j=4, m=KD)
                for j, part in enumerate((0, 1, 3, 4)):
                    for m in range(KD):
                        for k in range(KD):
                            w = wmod_sb[:, k, part * D + m * P:part * D + (m + 1) * P]
                            last = pe.matmul(cols[:, j, m, :], w, silu_c[:, k, :], start=(k == 0), stop=(k == KD - 1))
                last.then_inc(s_mod, 1)
                on_all_partitions(2, 5)
                pe.wait_ge(s_chain, MODS_KEPT)
                pe.wait_ge(s_w, 16 * 5)
                su_cols = psum[0][:, 1, 0:KD * B].rearrange("p (m b) -> p m b", m=KD)
                for m in range(KD):
                    for k in range(KD):
                        pe.matmul(su_cols[:, m, :], W_raw["in"][:, k, m * P:(m + 1) * P], sa[:, :, k],
                                  start=(k == 0), stop=(k == KD - 1))
                for k in range(KD):
                    last = pe.matmul(psum[0][0:E, 1, 64:64 + B], G_raw[:, k, :], sbc[:, :, k], start=(k == 0), stop=(k == KD - 1))
                last.then_inc(s_mod, 1)
            @block.vector
            def _(dve):
                done = [0]

                def step(ins):
                    ins.then_inc(s_chain, 1)
                    done[0] += 1
                    dve.wait_ge(s_chain, done[0])

                dve.wait_ge(s_silu, 1)
                step(dve.tensor_copy(silu_bc[:], silu_c[:].unsqueeze(3).to_broadcast([P, KD, B, P])))
                assert done[0] == SILU_SPREAD
                dve.wait_ge(s_b, 16 * 5)
                step(dve.tensor_scalar(ap["neg"][:], bcol["a"][:], -1.0, None, ALU.mult))
                step(dve.tensor_tensor(ap["abs"][:], bcol["a"][:], ap["neg"][:], ALU.max))
                step(dve.tensor_scalar(half_bgx[:], bcol["gx"][:], 0.5, None, ALU.mult))
                step(dve.tensor_scalar(half_bga[:], bcol["ga"][:], 0.5, None, ALU.mult))
                dve.wait_ge(s_exp, 1)
                step(dve.tensor_scalar(ap["u"][:], ap["exp"][:], 1.0, None, ALU.add))
                assert done[0] == EXP_PLUS_1
                step(dve.tensor_scalar(ap["um"][:], ap["u"][:], -1.0, None, ALU.add))
                step(dve.tensor_scalar(ap["zero"][:], ap["um"][:], 0.0, None, ALU.is_equal))
                step(dve.tensor_tensor(ap["den"][:], ap["um"][:], ap["zero"][:], ALU.add))
                step(dve.reciprocal(ap["rec"][:], ap["den"][:]))
                dve.wait_ge(s_exp, 2)
                step(dve.tensor_tensor(ap["num"][:], ap["ln"][:], ap["zero"][:], ALU.add))
                step(dve.tensor_tensor(ap["l1"][:], ap["num"][:], ap["rec"][:], ALU.mult))
                step(dve.tensor_tensor(ap["l1"][:], ap["l1"][:], ap["exp"][:], ALU.mult))
                step(dve.scalar_tensor_tensor(out=ap["sp"][:], in0=bcol["a"][:], scalar=0.0, in1=ap["l1"][:],
                                              op0=ALU.max, op1=ALU.add))
                step(dve.tensor_scalar(decay[:], ap["sp"][:], -GATE_C / 2, None, ALU.mult))
                step(dve.tensor_scalar(decay2[:], ap["sp"][:], -GATE_C, None, ALU.mult))
                dve.wait_ge(s_w, 16 * 5)
                for w, parts in ((W_raw["gx"], Wgx), (W_raw["ga"], Wga)):
                    step(dve.tensor_copy(parts[0][:], w[:]))
                    step(dve.tensor_tensor(parts[1][:], w[:], parts[0][:].bitcast(F32), ALU.subtract))
                dve.wait_ge(s_row, 1)
                g = psum[1][:].rearrange("p h (q d) -> p (h q) d", d=D)
                step(dve.tensor_scalar(gtmp["sign"][:], g, 0.0, 2.0, ALU.is_ge, ALU.mult))
                step(dve.tensor_scalar(gtmp["neg"][:], g, -1.0, MOD_MIN, ALU.mult, ALU.max))
                dve.wait_ge(s_mod, 1)
                cols = psum[0][:, 0, 0:8 * B].rearrange("p (j m b) -> p j b m", j=4, m=KD)
                step(dve.tensor_copy(sa[:], cols[:, 0]))
                step(dve.tensor_scalar(ca1[:], cols[:, 1], 1.0, None, ALU.add))
                step(dve.tensor_copy(sbc[:], cols[:, 2]))
                step(dve.tensor_scalar(cb1[:], cols[:, 3], 1.0, None, ALU.add))
                assert done[0] == MODS_KEPT
                step(dve.tensor_tensor(gtmp["mag"][:], g, gtmp["neg"][:], ALU.max))
                step(dve.scalar_tensor_tensor(out=ga_bc[:], in0=gtmp["sign"][:], scalar=-1.0, in1=gtmp["mag"][:],
                                              op0=ALU.add, op1=ALU.mult))
                step(dve.tensor_tensor(bias_bc[:], ga_bc[:], bout_bc[:].unsqueeze(1).to_broadcast([P, B, D]), ALU.mult))
                dve.wait_ge(s_mod, 2)
                step(dve.tensor_tensor(bias_u[:], psum[0][:, 1, 0:KD * B].rearrange("p (m b) -> p b m", m=KD),
                                       bcol["in"][:].unsqueeze(1).to_broadcast([P, B, KD]), ALU.add))
                step(dve.tensor_copy(bias_s[:], psum[0][0:E, 1, 64:64 + B]))
        su.close()

        xb_buf = [sbr(f"xb_buf{n}", [P, TT, D]) for n in range(4)]
        st1 = sbr("st1", [P, TT, 6])
        mv1 = [sbr(f"mv1_{n}", [P, TT, 2]) for n in range(2)]
        ve1 = sbr("ve1", [P, TT])
        rs1 = sbr("rs1", [P, TT])
        z1 = [sbr(f"z1_{n}", [P, TT, D]) for n in range(2)]
        zT = sbr("zT", [P, KD, GT])
        u_f = [sbr(f"u_f{n}", [P, KD, GT]) for n in range(2)]
        uT = [sbr(f"uT{q}", [P, KD, GT], F32R) for q in range(2)]
        tx = sbr("tx", [P, KD, GT])
        ta = sbr("ta", [P, KD, GT])
        a_t = [sbr(f"a_t{n}", [P, KD, GT]) for n in range(2)]
        a2_t = [sbr(f"a2_t{n}", [P, KD, GT]) for n in range(2)]
        sc_t = sbr("sc_t", [P, KD, GT])
        xg = [sbr(f"xg{n}", [P, KD, GT]) for n in range(2)]
        b_t = sbr("b_t", [P, KD, GT])
        hs = [sbr(f"hs{n}", [P, KD, GT]) for n in range(2)]
        hT = [sbr(f"hT{q}", [P, KD, GT], F32R) for q in range(2)]
        x1 = sbr("x1", [P, TT, D])
        st2 = sbr("st2", [P, TT, 6])
        mv2 = sbr("mv2", [P, TT, 2])
        ve2 = sbr("ve2", [P, TT])
        rs2 = sbr("rs2", [P, TT])
        z2 = [sbr(f"z2_{n}", [P, TT, D]) for n in range(2)]
        z2T = [sbr(f"z2T{n}", [P, KD, GT]) for n in range(2)]
        Win = sbr("Win", [P, KD, D])
        Wout_f = sbr("Wout_f", [P, KD, D])
        Wout = [sbr(f"Wout{q}", [P, KD, D], F32R) for q in range(2)]
        G = sbr("G", [P, KD, E])
        scoresT = sbr("scoresT", [E, GT])

        psT, psU, psG, psO = psum
        O_tok = psO[:].rearrange("p h (q d) -> p (h q) d", d=D)

        r_st = sem("stats1_written")
        r_rs = sem("rstd1_steps")
        r_z1 = sem("z1_ready")
        r_xb = sem("xb_ready")
        r_zps = sem("z1T_in_psum")
        r_zT = sem("zT_ready")
        r_U = sem("u_in_psum")
        r_uf = sem("u_ready")
        r_uh = sem("uT_split")
        r_X = sem("gate_x_in_psum")
        r_A = sem("gate_a_in_psum")
        r_tx = sem("tx_ready")
        r_ta = sem("ta_ready")
        r_a = sem("a_ready")
        r_m = sem("min_a2_ready")
        r_sc = sem("scale_ready")
        r_xg = sem("xg_ready")
        r_b = sem("b_ready")
        r_hs = sem("h_ready")
        r_hh = sem("hT_hi_ready")
        r_hl = sem("hT_lo_ready")
        r_O = sem("out_in_psum")
        r_x1 = sem("x1_ready")
        r_st2 = sem("stats2_written")
        r_rs2 = sem("rstd2_steps")
        r_z2 = sem("z2_ready")
        r_x1s = sem("x1_stored")
        r_z2s = sem("z2_stored")
        r_z2ps = sem("z2T_in_psum")
        r_z2T = sem("z2T_ready")
        r_S = sem("scores_in_psum")
        r_sT = sem("scoresT_ready")
        r_sps = sem("scores_turned")
        r_se = sem("scores_kept")
        r_win = sem("W_in_ready")
        r_wout = sem("W_out_steps")
        r_g = sem("gate_w_ready")

        AHEAD = 1
        LAST = NG - 1 + LAG["f"]

        def run_steps(eng, step):
            for s in range(PEELED):
                step(None, s)
            with eng.Fori(0, LOOPS) as i:
                for s in range(PEELED, PEELED + GB):
                    step(i, s)
            for s in range(PEELED + LOOPS * GB, LAST + 1):
                step(None, s)

        def stage(i, s, name):
            n = s - LAG[name]
            return Nth(i, n, GB) if i is not None or 0 <= n < NG else None

        def draining(i, s):
            return i is None and s > NG + LAG["b"]

        def score_psum(i, s):
            return (psG if draining(i, s) else psO)[0:E, 0, :]

        def through(i, s, name):
            n = s - LAG[name]
            return GB * i + n if i is not None else max(0, min(n, NG))

        with nc.Block() as block:
            @block.sync
            def _(sp):
                def load_x(g):
                    if g.has(4):
                        sp.wait_ge(r_z1, g.count(1, -3))
                        sp.wait_ge(r_xb, g.count(1, -3))
                    sp.sem_inc(held[3], 1)
                    sp.dma_start(x_buf[g.n % 4][:], rows(x_rows, g.count(GT))).then_inc(r_x[g.n % 4], 16)

                def step(i, s):
                    if i is None and s == 0:
                        for n in range(1, AHEAD):
                            load_x(Nth(None, n, GB))
                    if i is not None or s + AHEAD < NG:
                        load_x(Nth(i, s + AHEAD, GB))
                    if i is None and s < PEELED or s == LAST:
                        part = slice(min(s, PEELED) * ZERO, (min(s, PEELED) + 1) * ZERO)
                        sp.dma_start(acc_flat[:, part], zero_row[:]).then_inc(s_zero, 16)
                    d = stage(i, s, "d")
                    if d:
                        sp.wait_ge(r_x1, d.count(1, 1))
                        sp.sem_inc(held[3], 1)
                        sp.dma_start(rows(x1_dram, d.count(GT)), x1[:]).then_inc(r_x1s, 16)
                        sp.wait_ge(r_z2, d.count(1, 1))
                        sp.sem_inc(held[3], 1)
                        if d.has(1):
                            sp.wait_ge(r_z2s, d.count(16))
                        sp.sem_inc(held[3], 1)
                        sp.dma_start(rows(z_dram, d.count(GT))[:, :, 0:D], z2[d.n % 2][:]).then_inc(r_z2s, 16)

                acc_flat = acc_dram.rearrange("(p r) d -> p (r d)", p=P)
                run_steps(sp, step)
                sp.wait_ge(s_zero, 16 * (PEELED + 1))
                sp.wait_ge(r_x1s, 16 * NG)
                sp.wait_ge(r_z2s, 16 * NG)

            @block.gpsimd
            def _(pool):
                def step(i, s):
                    a, r_, d = (stage(i, s, k) for k in "ard")
                    if a:
                        pool.wait_ge(r_st, a.count(2, 2))
                        if a.has(1):
                            pool.wait_ge(r_z1, a.count(1))
                        pool.sem_inc(held[0], 1)
                        pool.tensor_scalar(ve1[:], mv1[a.n % 2][:, :, 1], EPS, None, ALU.add).then_inc(r_rs, 1)
                        pool.wait_ge(r_rs, a.count(2, 1))
                        pool.tensor_tensor(rs1[:], ve1[:], mhalf[:], ALU.pow).then_inc(r_rs, 1)
                    if r_:
                        pool.wait_ge(r_xg, r_.count(1, 1))
                        pool.wait_ge(r_sc, r_.count(1, 1))
                        if r_.has(1):
                            pool.wait_ge(r_hs, r_.count(1))
                        pool.tensor_tensor(b_t[:], xg[r_.n % 2][:], sc_t[:], ALU.mult).then_inc(r_b, 1)
                    def rstd2():
                        if d:
                            pool.wait_ge(r_st2, d.count(2, 2))
                            if d.has(1):
                                pool.wait_ge(r_z2, d.count(1))
                            pool.sem_inc(held[0], 1)
                            pool.tensor_scalar(ve2[:], mv2[:, :, 1], EPS, None, ALU.add).then_inc(r_rs2, 1)
                            pool.wait_ge(r_rs2, d.count(2, 1))
                            pool.tensor_tensor(rs2[:], ve2[:], mhalf[:], ALU.pow).then_inc(r_rs2, 1)

                    def h_lo():
                        if r_:
                            pool.wait_ge(r_hh, r_.count(1, 1))
                            pool.tensor_tensor(hT[1][:], hs[r_.n % 2][:], hT[0][:].bitcast(F32),
                                               ALU.subtract).then_inc(r_hl, 1)

                    for part in (h_lo, rstd2) if draining(i, s) else (rstd2, h_lo):
                        part()
                    if a:
                        pool.wait_ge(r_x[a.n % 4], a.turn(4))
                        if a.has(4):
                            pool.wait_ge(r_x1, a.count(1, -3))
                        pool.sem_inc(held[0], 1)
                        pool.tensor_tensor(xb_buf[a.n % 4][:], x_buf[a.n % 4][:],
                                           bias_bc[:, bass.ds(a.block(GB), 1), :].to_broadcast([P, TT, D]),
                                           ALU.add).then_inc(r_xb, 1)

                run_steps(pool, step)

            @block.scalar
            def _(act):
                def step(i, s):
                    b_, c_, r_, e_, f_ = (stage(i, s, k) for k in "bcref")
                    def scores_out():
                        if f_:
                            act.wait_ge(r_S, f_.count(1, 1))
                            if f_.has(1):
                                act.wait_ge(r_sps, f_.count(1, 1))
                            act.sem_inc(held[1], 1)
                            act.activation(scoresT[:], score_psum(i, s), ACT.Identity,
                                           bias=bias_s[:, bass.ds(f_.block(GB), 1)]).then_inc(r_sT, 1)

                    def scale():
                        if r_:
                            act.wait_ge(r_m, r_.count(1, 1))
                            if r_.has(1):
                                act.wait_ge(r_b, r_.count(1))
                            act.activation(sc_t[:], a2_t[r_.n % 2][:], ACT.Sqrt, bias=quarter[:, 0:1],
                                           scale=0.25).then_inc(r_sc, 1)

                    if draining(i, s):
                        scale()
                    scores_out()
                    if b_:
                        act.wait_ge(r_zps, b_.count(1, 1))
                        if b_.has(1):
                            act.wait_ge(r_U, b_.count(2))
                        act.activation(zT[:], psT[:], ACT.Copy).then_inc(r_zT, 1)
                    if not draining(i, s):
                        scale()
                    if c_:
                        act.wait_ge(r_X, c_.count(1, 1))
                        if c_.has(1):
                            act.wait_ge(r_xg, c_.count(1))
                        for m in range(KD):
                            ins = act.activation(tx[:, m, :], psG[:, m, :], ACT.Tanh, bias=half_bgx[:, m:m + 1], scale=0.5)
                        ins.then_inc(r_tx, 1)
                    if c_:
                        act.wait_ge(r_A, c_.count(1, 1))
                        if c_.has(1):
                            act.wait_ge(r_a, c_.count(2))
                        for m in range(KD):
                            ins = act.activation(ta[:, m, :], psU[:, m, :], ACT.Tanh, bias=half_bga[:, m:m + 1], scale=0.5)
                        ins.then_inc(r_ta, 1)
                        act.wait_ge(r_ta, c_.count(1, 1))
                        if c_.has(2):
                            act.wait_ge(r_sc, c_.count(1, -1))
                        for m in range(KD):
                            ins = act.activation(a2_t[c_.n % 2][:, m, :], ta[:, m, :], ACT.Exp, bias=decay2[:, m:m + 1],
                                                 scale=decay2[:, m:m + 1])
                        ins.then_inc(r_a, 1)
                        if c_.has(2):
                            act.wait_ge(r_hs, c_.count(1, -1))
                        for m in range(KD):
                            ins = act.activation(a_t[c_.n % 2][:, m, :], ta[:, m, :], ACT.Exp, bias=decay[:, m:m + 1],
                                                 scale=decay[:, m:m + 1])
                        ins.then_inc(r_a, 1)
                    if r_:
                        act.wait_ge(r_hs, r_.count(1, 1))
                        if r_.has(1):
                            act.wait_ge(r_O, r_.count(1))
                        act.activation(hT[0][:], hs[r_.n % 2][:], ACT.Copy).then_inc(r_hh, 1)
                    if b_:
                        if b_.has(2):
                            act.wait_ge(r_xg, b_.count(1, -1))
                        for m in range(KD):
                            act.wait_ge(r_U, b_.count(2, m + 1))
                            act.sem_inc(held[1], 1)
                            act.activation(u_f[b_.n % 2][:, m, :], psU[:, m, :], ACT.Identity,
                                           bias=bias_u[:, bass.ds(b_.block(GB), 1), m]).then_inc(r_uf, 1)
                    if e_:
                        act.wait_ge(r_z2ps, e_.count(1, 1))
                        if e_.has(2):
                            act.wait_ge(r_S, e_.count(1, -1))
                        act.activation(z2T[e_.n % 2][:], psT[:], ACT.Copy).then_inc(r_z2T, 1)

                run_steps(act, step)

            @block.vector
            def _(dve):
                def split(parts, full, done, count):
                    dve.tensor_copy(parts[0][:], full[:]).then_inc(done, 1)
                    dve.wait_ge(done, count + 1)
                    dve.tensor_tensor(parts[1][:], full[:], parts[0][:].bitcast(F32), ALU.subtract).then_inc(done, 1)

                def scale_w_in(i, s):
                    b_ = stage(i, s, "b")
                    if b_ and b_.n % GB == 0:
                        if b_.has(1):
                            dve.wait_ge(r_U, b_.count(2))
                        for k in range(KD):
                            ins = dve.tensor_scalar(Win[:, k, :], W_raw["in"][:, k, :],
                                                    ca1[:, bass.ds(b_.block(GB), 1), k], None, ALU.mult)
                        ins.then_inc(r_win, 1)

                def scale_w_out(i, s):
                    d = stage(i, s, "d")
                    if d and d.n % GB == 0:
                        if d.has(1):
                            dve.wait_ge(r_O, d.count(1))
                        dve.tensor_tensor(Wout_f[:], W_raw["out"][:],
                                          ga_bc[:, bass.ds(d.block(GB), 1), :].to_broadcast([P, KD, D]),
                                          ALU.mult).then_inc(r_wout, 1)
                        dve.wait_ge(r_wout, 3 * d.block(GB) + 1)
                        split(Wout, Wout_f, r_wout, 3 * d.block(GB) + 1)

                def scale_gate_w(i, s):
                    f_ = stage(i, s, "f")
                    if f_ and f_.n % GB == 0:
                        if f_.has(1):
                            dve.wait_ge(r_S, f_.count(1))
                        for k in range(KD):
                            ins = dve.tensor_scalar(G[:, k, :], G_raw[:, k, :], cb1[:, bass.ds(f_.block(GB), 1), k],
                                                    None, ALU.mult)
                        ins.then_inc(r_g, 1)

                def step(i, s):
                    a, b_, c_, r_, d, e_, f_ = (stage(i, s, k) for k in "abcrdef")
                    if a:
                        dve.wait_ge(r_x[a.n % 4], a.turn(4))
                        if a.has(1):
                            dve.wait_ge(r_st, a.count(2))
                        for t in range(TT):
                            ins = dve.bn_stats(st1[:, t, :], x_buf[a.n % 4][:, t, :])
                        ins.then_inc(r_st, 1)
                        dve.wait_ge(r_st, a.count(2, 1))
                        if a.has(2):
                            dve.wait_ge(r_z1, a.count(1, -1))
                        dve.sem_inc(held[2], 1)
                        for t in range(TT):
                            ins = dve.bn_aggr(mv1[a.n % 2][:, t, :], st1[:, t, :])
                        ins.then_inc(r_st, 1)
                    if a:
                        dve.wait_ge(r_rs, a.count(2, 2))
                        if a.has(2):
                            dve.wait_ge(r_zps, a.count(1, -1))
                        dve.sem_inc(held[2], 1)
                        for t in range(TT):
                            ins = dve.tensor_scalar(z1[a.n % 2][:, t, :], x_buf[a.n % 4][:, t, :],
                                                    mv1[a.n % 2][:, t, 0:1], rs1[:, t:t + 1], ALU.subtract, ALU.mult)
                        ins.then_inc(r_z1, 1)
                    if c_:
                        dve.wait_ge(r_tx, c_.count(1, 1))
                        dve.wait_ge(r_uf, c_.count(2, 2))
                        if c_.has(2):
                            dve.wait_ge(r_b, c_.count(1, -1))
                        dve.scalar_tensor_tensor(out=xg[c_.n % 2][:], in0=tx[:], scalar=1.0, in1=u_f[c_.n % 2][:],
                                                 op0=ALU.add, op1=ALU.mult).then_inc(r_xg, 1)
                    if r_:
                        dve.wait_ge(r_b, r_.count(1, 1))
                        dve.wait_ge(r_a, r_.count(2, 2))
                        if r_.has(1):
                            dve.wait_ge(r_hs, r_.count(1))
                        if r_.has(2):
                            dve.wait_ge(r_hl, r_.count(1, -1))
                        for m in range(KD):
                            before = 0.0 if r_.n % GB == 0 else hs[(r_.n - 1) % 2][:, m, GT - 1:GT]
                            ins = dve.tensor_tensor_scan(hs[r_.n % 2][:, m, :], a_t[r_.n % 2][:, m, :], b_t[:, m, :],
                                                         before, ALU.mult, ALU.add)
                        ins.then_inc(r_hs, 1)
                    scale_gate_w(i, s + 1)
                    if d:
                        dve.wait_ge(r_O, d.count(1, 1))
                        dve.wait_ge(r_xb, d.count(1, 1))
                        if d.has(1):
                            dve.wait_ge(r_x1s, d.count(16))
                            dve.wait_ge(r_z2, d.count(1))
                        dve.tensor_tensor(x1[:], O_tok, xb_buf[d.n % 4][:], ALU.add).then_inc(r_x1, 1)
                        dve.wait_ge(r_x1, d.count(1, 1))
                        for t in range(TT):
                            ins = dve.bn_stats(st2[:, t, :], x1[:, t, :])
                        ins.then_inc(r_st2, 1)
                        dve.wait_ge(r_st2, d.count(2, 1))
                        dve.sem_inc(held[2], 1)
                        for t in range(TT):
                            ins = dve.bn_aggr(mv2[:, t, :], st2[:, t, :])
                        ins.then_inc(r_st2, 1)
                    scale_w_out(i, s + 1)
                    if c_:
                        dve.wait_ge(r_a, c_.count(2, 1))
                        dve.tensor_scalar(a2_t[c_.n % 2][:], a2_t[c_.n % 2][:], 1.0, -1.0, ALU.min,
                                          ALU.mult).then_inc(r_m, 1)
                    if f_:
                        dve.wait_ge(r_sps, f_.count(1, 2))
                        q = f_.n % GB
                        dve.tensor_copy(scores[:, bass.ds(f_.block(GB), 1), TT * q:TT * (q + 1), :],
                                        psG[:, 0, 0:TT * E].rearrange("p (o t e) -> p o t e", o=1, e=E)).then_inc(r_se, 1)
                    if b_:
                        if b_.has(1):
                            dve.wait_ge(r_A, b_.count(1))
                        for m in range(KD):
                            half, u = [p[:, m, :] for p in uT], u_f[b_.n % 2][:, m, :]
                            dve.wait_ge(r_uf, b_.count(2, m + 1))
                            dve.tensor_copy(half[0], u).then_inc(r_uh, 1)
                            dve.wait_ge(r_uh, b_.count(4, 2 * m + 1))
                            dve.tensor_tensor(half[1], u, half[0].bitcast(F32), ALU.subtract).then_inc(r_uh, 1)
                    if d:
                        dve.wait_ge(r_rs2, d.count(2, 2))
                        if d.has(2):
                            dve.wait_ge(r_z2ps, d.count(1, -1))
                            dve.wait_ge(r_z2s, d.count(16, -16))
                        dve.sem_inc(held[2], 1)
                        for t in range(TT):
                            ins = dve.tensor_scalar(z2[d.n % 2][:, t, :], x1[:, t, :], mv2[:, t, 0:1], rs2[:, t:t + 1],
                                                    ALU.subtract, ALU.mult)
                        ins.then_inc(r_z2, 1)
                    scale_w_in(i, s + 1)

                dve.sem_inc(r_se, 1)
                run_steps(dve, step)

            @block.tensor
            def _(pe):
                def product(out_, stationary, moving):
                    terms = [(k, q) for k in range(KD) for q in PASSES]
                    for j, (k, (qs, qm)) in enumerate(terms):
                        ins = pe.matmul(out_, stationary(qs, k), moving(qm, k), start=(j == 0), stop=(j == len(terms) - 1))
                    return ins

                def cols(w, m):
                    return lambda q, k: w[q][:, k, m * P:(m + 1) * P]

                def whole(t):
                    return lambda q, k: t[q][:, k, :]

                def to_channels(z):
                    for t in range(TT):
                        for k in range(KD):
                            ins = pe.transpose(psT[:, k, t * P:(t + 1) * P], z[:, t, k * P:(k + 1) * P], ident[:])
                    return ins

                def step(i, s):
                    b_, c_, d, e_, f_ = (stage(i, s, k) for k in "bcdef")
                    def score_product():
                        if f_:
                            pe.wait_ge(r_z2T, f_.count(1, 1))
                            pe.wait_ge(r_g, f_.block(GB) + 1)
                            if draining(i, s):
                                pe.wait_ge(r_tx, through(i, s, "c"))
                                pe.wait_ge(r_se, f_.count(1, 1))
                            else:
                                pe.wait_ge(r_x1, through(i, s, "d"))
                            for k in range(KD):
                                ins = pe.matmul(score_psum(i, s), G[:, k, :], z2T[f_.n % 2][:, k, :],
                                                start=(k == 0), stop=(k == KD - 1))
                            ins.then_inc(r_S, 1)

                    def out_product():
                        if d:
                            pe.wait_ge(r_hl, d.count(1, 1))
                            pe.wait_ge(r_wout, 3 * d.block(GB) + 3)
                            if d.has(1):
                                pe.wait_ge(r_x1, d.count(1))
                            if f_ and not draining(i, s):
                                pe.wait_ge(r_sT, f_.count(1, 1))
                            elif f_ and f_.has(1):
                                pe.wait_ge(r_sT, f_.count(1))
                            for t in range(TT):
                                ins = product(O_tok[:, t, :], cols(hT, t), whole(Wout))
                            ins.then_inc(r_O, 1)

                    if draining(i, s):
                        out_product()
                    score_product()
                    if b_:
                        pe.wait_ge(r_z1, b_.count(1, 1))
                        if i is not None or s > LAG["e"]:
                            pe.wait_ge(r_z2T, through(i, s, "e"))
                        elif b_.has(1):
                            pe.wait_ge(r_zT, b_.count(1))
                        to_channels(z1[b_.n % 2]).then_inc(r_zps, 1)
                    if c_:
                        if c_.has(1):
                            pe.wait_ge(r_tx, c_.count(1))
                        if f_:
                            pe.wait_ge(r_se, f_.count(1, 1))
                        for m in range(KD):
                            for k in range(KD):
                                if m == 0:
                                    pe.wait_ge(r_uh, c_.count(4, 2 * k + 2))
                                for x_, (qs, qm) in enumerate(PASSES):
                                    ins = pe.matmul(psG[:, m, :], Wgx[qs][:, k, m * P:(m + 1) * P], uT[qm][:, k, :],
                                                    start=(k == 0 and x_ == 0),
                                                    stop=(k == KD - 1 and x_ == len(PASSES) - 1))
                        ins.then_inc(r_X, 1)
                        for m in range(KD):
                            ins = product(psU[:, m, :], cols(Wga, m), whole(uT))
                        ins.then_inc(r_A, 1)
                    if not draining(i, s):
                        out_product()
                    if b_:
                        pe.wait_ge(r_zT, b_.count(1, 1))
                        pe.wait_ge(r_win, b_.block(GB) + 1)
                        if c_:
                            pe.wait_ge(r_ta, c_.count(1, 1))
                        for m in range(KD):
                            for k in range(KD):
                                ins = pe.matmul(psU[:, m, :], Win[:, k, m * P:(m + 1) * P], zT[:, k, :],
                                                start=(k == 0), stop=(k == KD - 1))
                            ins.then_inc(r_U, 1)
                    if f_:
                        pe.wait_ge(r_sT, f_.count(1, 1))
                        pe.wait_ge(r_tx, through(i, s + 1, "c"))
                        pe.sem_inc(held[4], 1)
                        for t in range(TT):
                            ins = pe.transpose(psG[:, 0, t * E:(t + 1) * E], scoresT[:, t * P:(t + 1) * P], ident[0:E, 0:E])
                        ins.then_inc(r_sps, 1)
                    if e_:
                        pe.wait_ge(r_z2, e_.count(1, 1))
                        pe.wait_ge(r_zT, through(i, s + 1, "b"))
                        if not b_:
                            pe.wait_ge(r_z2T, e_.count(1))
                        to_channels(z2[e_.n % 2]).then_inc(r_z2ps, 1)

                pe.sem_inc(r_sps, 1)
                run_steps(pe, step)
        recur.close()

        NC = B * ST * E
        BITS = 30
        ROUNDS = 5
        VALS = 2
        moe = ExitStack()

        def sbf(name, shape, dt=F32):
            return moe.enter_context(nc.sbuf_tensor(name, shape, dt))

        w1_raw = sbf("w1_raw", [P, KD, H])
        w2_raw = sbf("w2_raw", [P, KH, D])
        w1_s = [[sbf(f"w1_{n}{q}", [P, KD, H], F32R) for q in range(2)] for n in range(2)]
        w2_s = [[sbf(f"w2_{n}{q}", [P, KH, D], F32R) for q in range(2)] for n in range(2)]
        w1_v = w1.rearrange("e (k p) h -> e p k h", p=P)
        w2_v = w2.rearrange("e (k p) d -> e p k d", p=P)
        row_id = sbf("row_id", [P, P], BF16)
        slot_lo_f = sbf("slot_lo_f", [P, B, ST, E])
        vals = sbf("vals", [P, B * ST, E, VALS, CT], BF16)

        def quarter_of(w_s, q):
            raw, parts, half = (w1_raw, w1_s[w_s], q) if q < 2 else (w2_raw, w2_s[w_s], q - 2)
            return raw, parts, slice(half, half + 1) if q < 2 else slice(half * KH // 2, (half + 1) * KH // 2)

        route = ExitStack()

        def sbt(name, shape, dt=F32):
            return route.enter_context(nc.sbuf_tensor(name, shape, dt))

        top = sbt("top", [P, B * ST])
        shifted = sbt("shifted", [P, NC])
        expd = sbt("expd", [P, NC])
        total = sbt("total", [P, B * ST])
        inv = sbt("inv", [P, B * ST])
        probs = sbt("probs", [P, NC])
        probsT = sbt("probsT", [P, B, P])
        rel = sbt("rel", [P, P], I32)
        rel7 = sbt("rel7", [P, P], I32)
        same_e = sbt("same_e", [P, P], BF16)
        before_e = sbt("before_e", [P, P], BF16)
        tok_id = sbt("tok_id", [P, 1])
        tile_id = sbt("tile_id", [P, NC])
        ones = sbt("ones", [P, P])
        cand = sbt("cand", [P, B], I32)
        bit_f = sbt("bit_f", [P, 1])
        bit_i = sbt("bit_i", [P, 1], I32)
        kept = sbt("kept", [P, B], I32)
        flip = sbt("flip", [P, B], I32)
        hit = sbt("hit", [P, B, P], BF16)
        n_hit = sbt("n_hit", [P, B], BF16)
        gt = sbt("gt", [P, B, P])
        eq = sbt("eq", [P, B, P])
        ceq = sbt("ceq", [P, B, P])
        n_eq = sbt("n_eq", [P, B], BF16)
        need = sbt("need", [P, B])
        room = sbt("room", [P, B])
        sel = sbt("sel", [P, B, P])
        csel = sbt("csel", [P, B, P])
        n_sel = sbt("n_sel", [P, B], BF16)
        first_slot = sbt("first_slot", [P, B])
        slot1 = sbt("slot1", [P, B, P])
        slot_i = sbt("slot_i", [P, NC], I32)
        slot_lo = sbt("slot_lo", [P, NC], I32)
        slot_hi = sbt("slot_hi", [P, NC], I32)
        t_pool = sem("route_pool")
        t_step = sem("route_vector_steps")
        t_exp = sem("route_exp")
        t_pT = sem("probsT_in_psum")
        t_cnt = sem("hits_counted")
        t_num = sem("hits_summed")
        t_bit = sem("candidate_steps")
        t_off = sem("offsets_in_psum")
        t_slot = sem("slots_turned")
        t_gb = sem("gb_steps")
        g_sign = sbt("g_sign", [P, B, D])
        g_mag = sbt("g_mag", [P, B, D])
        t_w = sem("first_weights_loaded")
        t_wh = sem("first_weights_hi")
        t_wl = sem("first_weights_lo")
        t_pz = sem("probs_stored")
        PROBS_KNOWN, COUNTS_DONE, SELECTED, SLOT_KNOWN = 5, 15, 21, 23
        with nc.Block() as block:
            @block.sync
            def _(sp):
                sp.dma_start(w1_raw[:], w1_v[0]).then_inc(t_w, 16)
                sp.dma_start(w2_raw[:], w2_v[0]).then_inc(t_w, 16)
                sp.wait_ge(t_step, PROBS_KNOWN)
                sp.dma_start(z_dram[:, D:].rearrange("(t p) e -> p t e", p=P), probs[:].rearrange("p (t e) -> p t e", e=E),
                             allow_slow_non_contiguous=True).then_inc(t_pz, 16)
                sp.wait_ge(t_pz, 16)

            @block.gpsimd
            def _(pool):
                pool.iota(rel[:], [[1, P]], base=P, channel_multiplier=-1).then_inc(t_pool, 1)
                pool.iota(row_id[:], [[1, P]], base=0, channel_multiplier=0,
                          allow_small_or_imprecise_dtypes=True).then_inc(t_pool, 1)
                pool.iota(tok_id[:], [[1, 1]], base=0, channel_multiplier=1,
                          allow_small_or_imprecise_dtypes=True).then_inc(t_pool, 1)
                pool.iota(tile_id[:], [[P, B * ST], [0, E]], base=0, channel_multiplier=0,
                          allow_small_or_imprecise_dtypes=True).then_inc(t_pool, 1)
                pool.memset(ones[:], 1.0).then_inc(t_pool, 1)
                for q in range(4):
                    raw, parts, at = quarter_of(0, q)
                    pool.wait_ge(t_wh, q + 1)
                    pool.tensor_tensor(parts[1][:, at, :], raw[:, at, :], parts[0][:, at, :].bitcast(F32),
                                       ALU.subtract).then_inc(t_wl, 1)
                pool.tensor_scalar(g_sign[:], gb_bc[:], 0.0, 2.0, ALU.is_ge, ALU.mult).then_inc(t_gb, 1)
                pool.wait_ge(t_gb, 1)
                pool.tensor_scalar(g_sign[:], g_sign[:], -1.0, None, ALU.add).then_inc(t_gb, 1)
                pool.wait_ge(t_gb, 2)
                pool.tensor_tensor(g_mag[:], gb_bc[:], g_sign[:], ALU.mult).then_inc(t_gb, 1)
                pool.wait_ge(t_gb, 3)
                pool.tensor_scalar(g_mag[:], g_mag[:], MOD_MIN, None, ALU.max).then_inc(t_gb, 1)
                pool.wait_ge(t_gb, 4)
                pool.tensor_tensor(gb_bc[:], g_mag[:], g_sign[:], ALU.mult).then_inc(t_gb, 1)

            @block.scalar
            def _(act):
                act.wait_ge(t_step, 2)
                act.activation(expd[:], shifted[:], ACT.Exp).then_inc(t_exp, 1)
                act.wait_ge(t_w, 32)
                for q in range(4):
                    raw, parts, at = quarter_of(0, q)
                    act.activation(parts[0][:, at, :], raw[:, at, :], ACT.Copy).then_inc(t_wh, 1)

            @block.tensor
            def _(pe):
                pe.wait_ge(t_step, PROBS_KNOWN)
                for b in range(B):
                    ins = pe.transpose(psum[0][:, 0, b * P:(b + 1) * P], probs[:, b * P:(b + 1) * P], ident[:])
                ins.then_inc(t_pT, 1)
                def count_hits(j, n):
                    r = Nth(j, n, ROUNDS)
                    pe.wait_ge(t_cnt, r.count(1, 1))
                    pe.matmul(psum[1][:, 0, 0:B], same_e[:], n_hit[:], start=True, stop=True).then_inc(t_num, 1)

                with pe.Fori(0, BITS // ROUNDS) as j:
                    for n in range(ROUNDS):
                        count_hits(j, n)
                pe.wait_ge(t_step, COUNTS_DONE)
                pe.matmul(psum[1][:, 1, 0:B], same_e[:], n_hit[:], start=True, stop=True)
                pe.matmul(psum[1][:, 1, B:2 * B], before_e[:], n_eq[:], start=True, stop=True).then_inc(t_off, 1)
                pe.wait_ge(t_step, SELECTED)
                pe.matmul(psum[1][:, 1, 2 * B:3 * B], before_e[:], n_sel[:], start=True, stop=True).then_inc(t_off, 1)
                pe.wait_ge(t_step, SLOT_KNOWN)
                for b in range(B):
                    ins = pe.transpose(psum[0][:, 1, b * P:(b + 1) * P], slot1[:, b, :], ident[:])
                ins.then_inc(t_slot, 1)

            @block.vector
            def _(dve):
                n_step = [0]

                def step(ins):
                    ins.then_inc(t_step, 1)
                    n_step[0] += 1
                    dve.wait_ge(t_step, n_step[0])

                sc = scores[:].rearrange("p b t e -> p (b t) e")
                sh = shifted[:].rearrange("p (t e) -> p t e", e=E)
                ex = expd[:].rearrange("p (t e) -> p t e", e=E)
                step(dve.tensor_reduce(top[:], sc, AX.X, ALU.max))
                step(dve.tensor_tensor(sh, sc, top[:].unsqueeze(2).to_broadcast([P, B * ST, E]), ALU.subtract))
                dve.wait_ge(t_exp, 1)
                step(dve.tensor_reduce(total[:], ex, AX.X, ALU.add))
                step(dve.reciprocal(inv[:], total[:]))
                step(dve.tensor_tensor(probs[:].rearrange("p (t e) -> p t e", e=E), ex,
                                       inv[:].unsqueeze(2).to_broadcast([P, B * ST, E]), ALU.mult))
                dve.wait_ge(t_pool, 5)
                step(dve.tensor_scalar(rel7[:], rel[:], E - 1, None, ALU.bitwise_and))
                step(dve.tensor_scalar(same_e[:], rel7[:], 0, None, ALU.is_equal))
                step(dve.scalar_tensor_tensor(out=before_e[:], in0=rel[:], scalar=float(P), in1=same_e[:],
                                              op0=ALU.is_gt, op1=ALU.mult))
                step(dve.memset(cand[:], 1 << (BITS - 1)))
                step(dve.memset(bit_f[:], float(1 << BITS)))
                step(dve.memset(bit_i[:], 1 << (BITS - 1)))
                dve.wait_ge(t_pT, 1)
                step(dve.tensor_copy(probsT[:], psum[0][:, 0, :].rearrange("p (b t) -> p b t", b=B)))
                cand_f = cand[:].bitcast(F32)

                def search(j, n):
                    r = Nth(j, n, ROUNDS)
                    for b in range(B):
                        ins = dve.tensor_scalar(hit[:, b, :], probsT[:, b, :], cand_f[:, b:b + 1], None, ALU.is_ge,
                                                ALU.add, accum_out=n_hit[:, b:b + 1])
                    ins.then_inc(t_cnt, 1)
                    dve.tensor_scalar(bit_i[:], bit_i[:], 1, None, ALU.arith_shift_right).then_inc(t_bit, 1)
                    dve.tensor_scalar(bit_f[:], bit_f[:], 0.5, None, ALU.mult).then_inc(t_bit, 1)
                    dve.wait_ge(t_bit, r.count(5, 2))
                    dve.tensor_tensor(kept[:], cand[:], bit_i[:].to_broadcast([P, B]), ALU.bitwise_or).then_inc(t_bit, 1)
                    dve.wait_ge(t_num, r.count(1, 1))
                    dve.tensor_scalar(flip[:], psum[1][:, 0, 0:B], float(CAPK), bit_f[:, 0:1], ALU.is_lt,
                                      ALU.mult).then_inc(t_bit, 1)
                    dve.wait_ge(t_bit, r.count(5, 4))
                    dve.tensor_tensor(cand[:], kept[:], flip[:], ALU.bitwise_xor).then_inc(t_bit, 1)
                    dve.wait_ge(t_bit, r.count(5, 5))

                with dve.Fori(0, BITS // ROUNDS) as j:
                    for n in range(ROUNDS):
                        search(j, n)
                for b in range(B):
                    dve.tensor_scalar(gt[:, b, :], probsT[:, b, :], cand_f[:, b:b + 1], None, ALU.is_gt, ALU.add,
                                            accum_out=n_hit[:, b:b + 1])
                    eq_last = dve.tensor_scalar(eq[:, b, :], probsT[:, b, :], cand_f[:, b:b + 1], None, ALU.is_equal)
                step(eq_last)
                for b in range(B):
                    ins = dve.tensor_tensor_scan(ceq[:, b, :], ones[:], eq[:, b, :], 0.0, ALU.mult, ALU.add)
                step(ins)
                step(dve.tensor_copy(n_eq[:], ceq[:, :, P - 1]))
                assert n_step[0] == COUNTS_DONE
                dve.wait_ge(t_off, 1)
                step(dve.tensor_scalar(need[:], psum[1][:, 1, 0:B], -1.0, float(CAPK), ALU.mult, ALU.add))
                step(dve.tensor_tensor(room[:], need[:], psum[1][:, 1, B:2 * B], ALU.subtract))
                for b in range(B):
                    ins = dve.scalar_tensor_tensor(out=sel[:, b, :], in0=ceq[:, b, :], scalar=room[:, b:b + 1],
                                                   in1=eq[:, b, :], op0=ALU.is_le, op1=ALU.mult)
                step(ins)
                step(dve.tensor_tensor(sel[:], sel[:], gt[:], ALU.add))
                for b in range(B):
                    ins = dve.tensor_tensor_scan(csel[:, b, :], ones[:], sel[:, b, :], 0.0, ALU.mult, ALU.add)
                step(ins)
                step(dve.tensor_copy(n_sel[:], csel[:, :, P - 1]))
                assert n_step[0] == SELECTED
                dve.wait_ge(t_off, 2)
                step(dve.tensor_copy(first_slot[:], psum[1][:, 1, 2 * B:3 * B]))
                for b in range(B):
                    ins = dve.scalar_tensor_tensor(out=slot1[:, b, :], in0=csel[:, b, :], scalar=first_slot[:, b:b + 1],
                                                   in1=sel[:, b, :], op0=ALU.add, op1=ALU.mult)
                step(ins)
                assert n_step[0] == SLOT_KNOWN
                dve.wait_ge(t_slot, 1)
                step(dve.tensor_scalar(slot_i[:], psum[0][:, 1, :], -1.0, None, ALU.add))
                step(dve.tensor_scalar(slot_lo[:], slot_i[:], P - 1, None, ALU.bitwise_and))
                step(dve.tensor_copy(slot_lo_f[:].rearrange("p b t e -> p (b t e)"), slot_lo[:]))
                step(dve.tensor_scalar(slot_hi[:], slot_i[:], P.bit_length() - 1, None, ALU.arith_shift_right))
                ids = vals[:].rearrange("p t e v c -> p (t e) v c")
                for t in range(CT):
                    dve.tensor_scalar(ids[:, :, 0, t], slot_hi[:], t, tok_id[:, 0:1], ALU.is_equal, ALU.mult)
                    last = dve.scalar_tensor_tensor(out=ids[:, :, 1, t], in0=slot_hi[:], scalar=float(t), in1=tile_id[:],
                                                    op0=ALU.is_equal, op1=ALU.mult)
                step(last)
        route.close()
        BODY = 2 * B
        PASSES_F = E // 2
        LAST_PASS = [(e, b) for half in ((0, 1), (2,), (3,)) for e in range(2) for b in half]
        DONE_IN = [next(j for j in range(BODY) if LAST_PASS[j] == (1, b)) for b in range(B)]

        class Unit(Nth):

            def __init__(self, i, n, span):
                super().__init__(i, n, span)
                first = (PASSES_F - 1) * BODY
                permuted = i is None and n >= first
                self.slot, self.b = LAST_PASS[n - first] if permuted else (n // B % 2, n % B)
                self.e = 2 * (PASSES_F - 1) + self.slot if permuted else self.block(B)

        idx_cur = [sbf(f"idx_cur{n}", [P, B, CT], I32) for n in range(2)]
        g_cur = [sbf(f"g_cur{n}", [P, CT, 1]) for n in range(2)]
        slot_u = [sbf(f"slot_u{n}", [P, ST, 1]) for n in range(2)]
        vals_u = [sbf(f"vals_u{n}", [P, ST, 1, VALS * CT], BF16) for n in range(2)]
        place = [sbf(f"place{n}", [P, ST, P], BF16) for n in range(2)]
        lists = [sbf(f"lists{n}", [P, VALS, CT]) for n in range(2)]
        rows_in = [sbf(f"rows_in{n}", [P, CT, D + E]) for n in range(2)]
        xf = sbf("xf", [P, KD, CAPK])
        xT = [sbf(f"xT{q}", [P, KD, CAPK], F32R) for q in range(2)]
        HF = 4
        hf = [sbf(f"hf{n}", [P, CAPK]) for n in range(HF)]
        hidT = [sbf(f"hidT{q}", [P, KH, CAPK], F32R) for q in range(2)]
        rows_y = [sbf(f"rows_y{n}", [P, CT, D]) for n in range(2)]

        f_w1 = sem("w1_loaded")
        f_w2 = sem("w2_loaded")
        f_ws = sem("weights_split")
        f_se = sem("unit_slots_ready")
        f_pl = sem("place_ready")
        f_lm = sem("list_in_psum")
        f_lc = sem("list_copied")
        f_idx = sem("idx_cur_ready")
        f_g = sem("g_cur_ready")
        f_in = [sem(f"rows_gathered{n}") for n in range(2)]
        f_T = sem("rows_turned")
        f_xf = sem("xf_ready")
        f_x = sem("xT_split")
        f_H = sem("hidden_in_psum")
        f_hf = sem("hidden_ready")
        f_hh = sem("hidT_hi_ready")
        f_hl = sem("hidT_lo_ready")
        f_Y = sem("y_in_psum")
        f_y = sem("rows_y_ready")
        f_add = [sem(f"rows_added{b}") for b in range(B)]

        acc_t = [t[:].rearrange("p k n -> p (k n)")[:, h * TT * D:(h + 1) * TT * D].rearrange("p (t d) -> p t d", d=D)
                 for t in (w1_raw, w2_raw) for h in range(2)]
        res_t = [sbf(f"res_t{n}", [P, TT, D])[:] for n in range(6)]
        SA, SR = len(acc_t), len(res_t)
        acc16 = [sbf(f"acc16_{n}", [P, TT, D], BF16) for n in range(GB)]
        AHEAD_A, AHEAD_R = SA, SR - 1
        o_acc = [sem(f"acc_loaded{n}") for n in range(SA)]
        o_x1 = [sem(f"x1_loaded{n}") for n in range(SR)]
        o_16 = sem("acc16_ready")
        o_pp = sem("gated_by_pool")
        o_pd = sem("gated_by_dve")
        o_r = sem("result_ready")
        o_out = [sem(f"out_stored{n}") for n in range(SR)]
        POOL_GATES = [k < NG - GB or k % 2 == 1 for k in range(NG)]

        def wait_gated(eng, k):
            if POOL_GATES[k]:
                eng.wait_ge(o_pp, sum(POOL_GATES[:k + 1]))
            else:
                eng.wait_ge(o_pd, k + 1 - sum(POOL_GATES[:k + 1]))

        def gate(eng, k):
            eng.wait_ge(o_16, k + 1)
            return eng.tensor_tensor(acc_t[k % SA], acc16[k % GB][:], gb_bc[:, k // GB:k // GB + 1, :].to_broadcast([P, TT, D]),
                                     ALU.mult)

        def along(i, j, m):
            for b in range(B - 1):
                if i is None and j == (PASSES_F - 1) * BODY + DONE_IN[b] + 2 and m % 2 == 1:
                    return b * GB + m // 2
            return None

        psT, psH0, psH1, psY = psum
        H_bank = [psH0[:, 0, :], psH0[:, 1, :], psH1[:, 0, :], psH1[:, 1, :]]
        Y_tok = psY[:].rearrange("p h (q d) -> p (h q) d", d=D)

        LISTED = 2

        def list_psum(v):
            in_prologue = v.i is None and v.n < LISTED
            return psY[:, 0, 8 * v.n:8 * v.n + VALS * CT] if in_prologue else psT[:, 0, 0:VALS * CT]

        def listed(i, j):
            return Unit(i, j + LISTED, BODY) if i is not None or j + LISTED < E * B else None

        def run_units(eng, step):
            for j in range(BODY):
                step(None, j)
            with eng.Fori(1, PASSES_F - 1) as i:
                for j in range(BODY):
                    step(i, j)
            for j in range((PASSES_F - 1) * BODY, PASSES_F * BODY):
                step(None, j)

        with nc.Block() as block:
            @block.sync
            def _(sp):
                def load(e):
                    if e.has(2):
                        sp.wait_ge(f_ws, e.count(8, -12))
                    sp.dma_start(w1_raw[:], w1_v[bass.ds(e.count(1), 1)].rearrange("o p k h -> p (o k) h")).then_inc(f_w1, 16)
                    if e.has(2):
                        sp.wait_ge(f_ws, e.count(8, -8))
                    sp.dma_start(w2_raw[:], w2_v[bass.ds(e.count(1), 1)].rearrange("o p k d -> p (o k) d")).then_inc(f_w2, 16)
                load(Nth(None, 1, 1))
                with sp.Fori(2, E) as i:
                    load(Nth(i, 0, 1))

                def load_acc(k):
                    if k % GB == 0:
                        sp.wait_ge(f_add[k // GB], 16 * CT * E)
                    if k >= SA:
                        sp.wait_ge(o_r, k - SA + 1)
                    sp.dma_start(acc_t[k % SA], runs(acc_dram, k * GT)).then_inc(o_acc[k % SA], 16)

                def load_x1(k):
                    if k >= SR:
                        sp.wait_ge(o_out[k % SR], 16 * (k // SR))
                    sp.dma_start(res_t[k % SR], runs(x1_dram, k * GT)).then_inc(o_x1[k % SR], 16)

                sp.wait_ge(f_ws, 8 * (E - 1))
                for k in range(AHEAD_R):
                    load_x1(k)
                for k in range(AHEAD_A):
                    load_acc(k)
                for k in range(NG):
                    sp.wait_ge(o_r, k + 1)
                    sp.dma_start(runs(out_rows, k * GT), res_t[k % SR]).then_inc(o_out[k % SR], 16)
                    if k + AHEAD_R < NG:
                        load_x1(k + AHEAD_R)
                    if k + AHEAD_A < NG - GB:
                        load_acc(k + AHEAD_A)
                    if k == NG - GB - 1:
                        for last in range(NG - GB, NG):
                            load_acc(last)
                for n in range(SR):
                    sp.wait_ge(o_out[n], 16 * len(range(n, NG, SR)))

            @block.gpsimd
            def _(pool):
                def fetch(u):
                    n = u.slot
                    pool.wait_ge(f_idx, u.count(1, 1))
                    if u.has(2):
                        pool.wait_ge(f_T, u.count(1, -1))
                        pool.wait_ge(f_g, u.count(1, -1))
                    pool.sem_inc(held[0], 1)
                    for t in range(CT):
                        pool.indirect_dma_start(rows_in[u.n % 2][:, t, :], None, z_dram,
                                                bass.IndirectOffsetOnAxis(ap=idx_cur[n][:, u.b, t:t + 1], axis=0))\
                            .then_inc(f_in[u.n % 2], 16)

                def add(u):
                    n, b = u.slot, u.b
                    pool.wait_ge(f_y, u.count(2, 2))
                    if u.has(B):
                        pool.wait_ge(f_add[b], 16 * CT * u.e)
                    pool.sem_inc(held[0], 1)
                    for t in range(CT):
                        pool.indirect_dma_start(acc_dram, bass.IndirectOffsetOnAxis(ap=idx_cur[n][:, b, t:t + 1], axis=0),
                                                rows_y[u.n % 2][:, t, :], None, compute_op=ALU.add).then_inc(f_add[b], 16)

                def step(i, j):
                    if i is not None or j + 1 < E * B:
                        fetch(Unit(i, j + 1, BODY))
                    if i is not None or j >= 1:
                        add(Unit(i, j - 1, BODY))
                    for m in range(KH):
                        k = along(i, j, m)
                        if k is not None:
                            gate(pool, k).then_inc(o_pp, 1)
                fetch(Unit(None, 0, BODY))
                run_units(pool, step)
                add(Unit(None, E * B - 1, BODY))
                for k in range(NG - GB, NG):
                    if POOL_GATES[k]:
                        gate(pool, k).then_inc(o_pp, 1)

            @block.scalar
            def _(act):
                def weigh(u):
                    act.wait_ge(f_g, u.count(1, 1))
                    for h in range(2):
                        act.wait_ge(f_Y, u.count(2, h + 1))
                        if h == 0 and u.has(2):
                            v = Unit(u.i, u.n - 2, BODY)
                            act.wait_ge(f_add[v.b], 16 * CT * (v.e + 1))
                        for t in range(2 * h, 2 * h + 2):
                            ins = act.activation(rows_y[u.n % 2][:, t, :], Y_tok[:, t, :], ACT.Copy,
                                                 scale=g_cur[u.n % 2][:, t, 0:1])
                        ins.then_inc(f_y, 1)

                def round_sum(k):
                    act.wait_ge(o_acc[k % SA], 16 * (k // SA + 1))
                    if k >= GB:
                        wait_gated(act, k - GB)
                    act.activation(acc16[k % GB][:], acc_t[k % SA], ACT.Copy).then_inc(o_16, 1)

                def step(i, j):
                    u = Unit(i, j, BODY)
                    act.wait_ge(f_T, u.count(1, 1))
                    if u.has(1):
                        act.wait_ge(f_x, u.count(2))
                    for k in range(KD):
                        ins = act.activation(xf[:, k, :], psT[:, k, :], ACT.Identity, bias=sbc[:, u.b, k:k + 1],
                                             scale=cb1[:, u.b, k:k + 1])
                    ins.then_inc(f_xf, 1)
                    if u.has(1):
                        weigh(Unit(i, j - 1, BODY))
                    for m in range(KH):
                        act.wait_ge(f_H, u.count(KH, m + 1))
                        if u.has(1) or m >= HF:
                            act.wait_ge(f_hl, u.count(KH, m + 1 - HF))
                        act.activation(hf[m % HF][:], H_bank[m % 4], ACT.Gelu_apprx_tanh).then_inc(f_hf, 1)
                        k = along(i, j, m)
                        if k is not None:
                            round_sum(k)
                run_units(act, step)
                weigh(Unit(None, E * B - 1, BODY))
                for k in range(NG - GB, NG):
                    round_sum(k)

            @block.vector
            def _(dve):
                def split_chunk(e, n, q):
                    raw, parts, at = quarter_of(n, q)
                    dve.wait_ge(f_w1 if q < 2 else f_w2, 16 * e)
                    dve.tensor_copy(parts[0][:, at, :], raw[:, at, :]).then_inc(f_ws, 1)
                    dve.wait_ge(f_ws, 8 * e + (2 * q + 1 - 8))
                    dve.tensor_tensor(parts[1][:, at, :], raw[:, at, :], parts[0][:, at, :].bitcast(F32),
                                      ALU.subtract).then_inc(f_ws, 1)

                def one_hots(v):
                    b, n, e = v.b, v.n % 2, bass.ds(v.e, 1)
                    if v.has(2):
                        dve.wait_ge(f_lm, v.count(1, -1))
                    dve.sem_inc(held[2], 1)
                    dve.tensor_copy(slot_u[n][:], slot_lo_f[:, b, :, e]).then_inc(f_se, 1)
                    dve.tensor_copy(vals_u[n][:], vals[:, b * ST:(b + 1) * ST, e, :, :]
                                    .rearrange("p t o v c -> p t o (v c)")).then_inc(f_se, 1)
                    dve.wait_ge(f_se, v.count(2, 2))
                    for t in range(ST):
                        ins = dve.tensor_scalar(place[n][:, t, :], row_id[:], slot_u[n][:, t, 0:1], None, ALU.is_equal)
                    ins.then_inc(f_pl, 1)

                def keep_list(v):
                    b, n = v.b, v.n % 2
                    dve.wait_ge(f_lm, v.count(1, 1))
                    if v.has(2):
                        dve.wait_ge(f_idx, v.count(1, -1))
                    dve.tensor_copy(lists[n][:], list_psum(v).rearrange("p (v c) -> p v c", v=VALS)).then_inc(f_lc, 1)
                    dve.wait_ge(f_lc, v.count(1, 1))
                    if v.has(2 * B):
                        dve.wait_ge(f_add[b], 16 * CT * (v.e - 1))
                    dve.tensor_tensor(idx_cur[v.slot][:, b, :], lists[n][:, 0, :], lists[n][:, 1, :],
                                      ALU.add).then_inc(f_idx, 1)

                def finish_sum(k):
                    if not POOL_GATES[k]:
                        gate(dve, k).then_inc(o_pd, 1)
                    wait_gated(dve, k)
                    dve.wait_ge(o_x1[k % SR], 16 * (k // SR + 1))
                    dve.tensor_tensor(res_t[k % SR], acc_t[k % SA], res_t[k % SR], ALU.add).then_inc(o_r, 1)

                def step(i, j):
                    u = Unit(i, j, BODY)
                    dve.wait_ge(f_xf, u.count(1, 1))
                    if u.has(1):
                        dve.wait_ge(f_H, u.count(KH))
                    dve.tensor_copy(xT[0][:], xf[:]).then_inc(f_x, 1)
                    dve.wait_ge(f_x, u.count(2, 1))
                    dve.tensor_tensor(xT[1][:], xf[:], xT[0][:].bitcast(F32), ALU.subtract).then_inc(f_x, 1)
                    if u.has(2):
                        dve.wait_ge(f_y, u.count(2, -2))
                    dve.sem_inc(held[2], 1)
                    dve.tensor_copy(g_cur[u.n % 2][:], rows_in[u.n % 2][:, :, bass.ds(u.e + D, 1)]).then_inc(f_g, 1)
                    v = listed(i, j)
                    if v:
                        one_hots(v)
                    in_last_pass = max(0, j + 1 - (PASSES_F - 1) * BODY) if i is None else 0
                    if 1 <= in_last_pass <= 2:
                        split_chunk(E - 1, 1, 2 * in_last_pass - 2)
                    for m in range(KH):
                        dve.wait_ge(f_hf, u.count(KH, m + 1))
                        if m == 0 and u.has(1):
                            dve.wait_ge(f_Y, u.count(2))
                        dve.tensor_copy(hidT[0][:, m, :], hf[m % HF][:]).then_inc(f_hh, 1)
                        dve.wait_ge(f_hh, u.count(KH, m + 1))
                        dve.tensor_tensor(hidT[1][:, m, :], hf[m % HF][:], hidT[0][:, m, :].bitcast(F32),
                                          ALU.subtract).then_inc(f_hl, 1)
                        if m == 2 and v:
                            keep_list(v)
                        if in_last_pass:
                            if in_last_pass <= 2 and m == 3:
                                split_chunk(E - 1, 1, 2 * in_last_pass - 1)
                        elif m == 3:
                            split_chunk(u.e + 1, 1 - u.slot, u.b)
                        k = along(i, j, m)
                        if m == KH - 1 and k is not None:
                            for done in range(k - GB + 1, k + 1):
                                finish_sum(done)
                for n in range(LISTED):
                    one_hots(Unit(None, n, BODY))
                    keep_list(Unit(None, n, BODY))
                run_units(dve, step)
                for k in range(NG - GB, NG):
                    finish_sum(k)

            @block.tensor
            def _(pe):
                def turn(u):
                    pe.wait_ge(f_in[u.n % 2], u.turn(2, 16 * CT))
                    if u.has(1):
                        pe.wait_ge(f_xf, u.count(1))
                        if listed(u.i, u.n - 1):
                            pe.wait_ge(f_lc, u.count(1, LISTED))
                    for t in range(CT):
                        for k in range(KD):
                            ins = pe.transpose(psT[:, k, t * P:(t + 1) * P], rows_in[u.n % 2][:, t, k * P:(k + 1) * P],
                                               ident[:])
                    ins.then_inc(f_T, 1)

                def make_list(v):
                    pe.wait_ge(f_pl, v.count(1, 1))
                    for t in range(ST):
                        ins = pe.matmul(list_psum(v), place[v.n % 2][:, t, :], vals_u[v.n % 2][:, t, 0, :],
                                        start=(t == 0), stop=(t == ST - 1))
                    ins.then_inc(f_lm, 1)

                def layer2(u):
                    n = u.slot
                    if u.has(B):
                        pe.wait_ge(f_ws, 8 * u.e)
                    for t in range(CT):
                        if t % 2 == 0 and u.has(1):
                            pe.wait_ge(f_y, u.count(2, t // 2 - 1))
                        terms = [(k, q) for k in range(KH) for q in PASSES]
                        for x_, (k, (qs, qm)) in enumerate(terms):
                            if t == 0 and x_ % len(PASSES) == 0:
                                pe.wait_ge(f_hl, u.count(KH, k + 1))
                            ins = pe.matmul(Y_tok[:, t, :], hidT[qs][:, k, t * P:(t + 1) * P], w2_s[n][qm][:, k, :],
                                            start=(x_ == 0), stop=(x_ == len(terms) - 1))
                        if t % 2 == 1:
                            ins.then_inc(f_Y, 1)

                def layer1(u, v):
                    n = u.slot
                    pe.wait_ge(f_x, u.count(2, 2))
                    if u.has(B):
                        pe.wait_ge(f_ws, 8 * u.e - 4)
                    for m in range(KH):
                        if v and m == 2:
                            make_list(v)
                        if u.has(1) or m >= 4:
                            pe.wait_ge(f_hf, u.count(KH, m + 1 - 4))
                        terms = [(k, q) for k in range(KD) for q in PASSES]
                        for x_, (k, (qs, qm)) in enumerate(terms):
                            ins = pe.matmul(H_bank[m % 4], w1_s[n][qs][:, k, m * P:(m + 1) * P], xT[qm][:, k, :],
                                            start=(x_ == 0), stop=(x_ == len(terms) - 1))
                        ins.then_inc(f_H, 1)

                def step(i, j):
                    u = Unit(i, j, BODY)
                    turn(u)
                    if u.has(1):
                        layer2(Unit(i, j - 1, BODY))
                    layer1(u, listed(i, j))
                for n in range(LISTED):
                    make_list(Unit(None, n, BODY))
                run_units(pe, step)
                layer2(Unit(None, E * B - 1, BODY))
        moe.close()


_INS = ["L0_attn_x", "L0_attn_W_in", "L0_attn_b_in", "L0_attn_W_gx", "L0_attn_b_gx", "L0_attn_W_ga", "L0_attn_b_ga",
        "L0_attn_a_param", "L0_attn_W_out", "L0_attn_b_out", "L0_ffn_gate_w", "L0_ffn_w1", "L0_ffn_w2", "L0_c", "L0_wmod"]


def kernel(**inputs):
    import numpy as _np
    import concourse.bacc as _bacc
    from concourse import mybir as _mybir
    from concourse.bass_utils import run_bass_kernel_spmd as _run

    nc = _bacc.Bacc("TRN2", target_bir_lowering=False, num_devices=1)
    arrays, args = {}, []
    for name in _INS:
        a = _np.ascontiguousarray(inputs[name])
        arrays[f"in_{name}"] = a
        args.append(nc.dram_tensor(f"in_{name}", a.shape, _mybir.dt.from_np(a.dtype), kind="ExternalInput").ap())
    shape = arrays["in_L0_attn_x"].shape
    args.append(nc.dram_tensor("out_x", shape, _mybir.dt.float32, kind="ExternalOutput").ap())
    adaln_kernel(nc, *args)
    r = _run(nc, [arrays], core_ids=[0])
    return r.results[0]["out_x"]
```
